# Optimizing a Trainium2 kernel written in Bass

```python
import numpy as np
import jax
import jax.numpy as jnp

def _softmax(x, axis=-1):
    return jax.nn.softmax(x, axis=axis)

def _gelu(x):
    return jax.nn.gelu(x, approximate=True)

def _silu(x):
    return jax.nn.silu(x)

def _sigmoid(x):
    return jax.nn.sigmoid(x)

def _layernorm(x, axis=-1, eps=1e-05):
    m = jnp.mean(x, axis=axis, keepdims=True)
    v = jnp.var(x, axis=axis, keepdims=True)
    return (x - m) / jnp.sqrt(v + eps)

def _scatter_add(tgt, idx, src, axis=0):
    return tgt.at[idx].add(src)

def _segment_sum(src, seg, n):
    return jax.ops.segment_sum(src, seg, n)
kernel_name = 'mk_decoder_postln_d2_seqx_r4_adc715'

def setup_inputs(seed: int=0):
    np.random.seed(seed)
    _w = jnp.asarray

    def _rec_inputs():
        import jax
        import jax.numpy as jnp
        _rk = jax.random.key(seed)
        x = 7.22e-05 + 1 * jax.random.normal(jax.random.fold_in(_rk, 1), (16, 128, 256), jnp.float32)
        _lenS = 128 - jax.random.randint(jax.random.fold_in(_rk, 7), (16,), 0, max(1, 128 // 4) + 1, jnp.int32)
        _lenS2 = 128 - jax.random.randint(jax.random.fold_in(_rk, 8), (16,), 0, max(1, 128 // 4) + 1, jnp.int32)
        _ctx_1024P = jax.random.normal(jax.random.fold_in(_rk, 11), (16, 16, 256), jnp.float32)
        _ctx_1024c = jax.random.dirichlet(jax.random.fold_in(_rk, 511), 0.3 * jnp.ones((16,), jnp.float32), (16, 128))
        _ctx_1024t = jnp.einsum('bsk,bkd->bsd', _ctx_1024c, _ctx_1024P)
        _ctx_1024t = _ctx_1024t * jax.lax.rsqrt(jnp.mean(jnp.square(_ctx_1024t)) + 1e-12) * 0.953939
        ctx_1024 = 4.13588e-05 + 0.999923 * (_ctx_1024t + 0.3 * jax.random.normal(jax.random.fold_in(_rk, 611), (16, 128, 256), jnp.float32))
        return (x, ctx_1024)
    x, ctx_1024 = _rec_inputs()

    def _L0_attn_setup():
        import jax, jax.numpy as jnp
        import numpy as np
        DIM = 256
        NUM_HEAD = 16
        DIM_HEAD = DIM // NUM_HEAD
        RMS_EPS = 1.1920929e-07
        EPS_LIN = 1e-06
        THETA = 10000.0

        def rmsnorm(x, g, eps=RMS_EPS):
            return x * jax.lax.rsqrt(jnp.mean(x * x, axis=-1, keepdims=True) + eps) * g

        def rope_cos_sin(seq_len, dim_head, dtype=jnp.float32):
            inv_freq = 1.0 / THETA ** (jnp.arange(0, dim_head, 2, dtype=dtype) / dim_head)
            t = jnp.arange(seq_len, dtype=dtype)
            freqs = jnp.outer(t, inv_freq)
            return (jnp.cos(freqs), jnp.sin(freqs))

        def apply_rope(t, cos, sin):
            tr = t[..., 0::2]
            ti = t[..., 1::2]
            out_r = tr * cos - ti * sin
            out_i = tr * sin + ti * cos
            return jnp.stack([out_r, out_i], axis=-1).reshape(t.shape)
        key = jax.random.key(seed)
        ks = jax.random.split(key, 5)
        B, L = (4, 1024)
        x = jax.random.normal(ks[0], (B, L, DIM), dtype=jnp.float32)
        Wqkv = jax.random.normal(ks[1], (3 * DIM, DIM), dtype=jnp.float32) * 0.02
        bqkv = jax.random.normal(ks[2], (3 * DIM,), dtype=jnp.float32) * 0.02
        gq = jnp.ones((DIM,), dtype=jnp.float32)
        gk = jnp.ones((DIM,), dtype=jnp.float32)
        Wout = jax.random.normal(ks[3], (DIM, DIM), dtype=jnp.float32) * 0.02
        bout = jax.random.normal(ks[4], (DIM,), dtype=jnp.float32) * 0.02
        gout = jnp.ones((DIM,), dtype=jnp.float32)
        return {'x': x, 'Wqkv': Wqkv, 'bqkv': bqkv, 'gq': gq, 'gk': gk, 'Wout': Wout, 'bout': bout, 'gout': gout}
    _L0_attn_all = _L0_attn_setup()
    _L0_attn_in = {k: v for k, v in _L0_attn_all.items() if k in ('Wqkv', 'bqkv', 'gq', 'gk', 'Wout', 'bout', 'gout')}
    del _L0_attn_all

    def _L0_xattn_setup():
        import jax, jax.numpy as jnp
        import numpy as np
        D_MODEL = 256
        NUM_HEADS = 16
        HEAD_SIZE = D_MODEL // NUM_HEADS
        key = jax.random.key(seed)
        ks = jax.random.split(key, 7)
        B, L, D = (4, 512, D_MODEL)
        q = jax.random.normal(ks[0], (B, L, D), dtype=jnp.float32)
        k = jax.random.normal(ks[1], (B, L, D), dtype=jnp.float32)
        v = jax.random.normal(ks[2], (B, L, D), dtype=jnp.float32)
        s = 1.0 / np.sqrt(D)
        Wq = jax.random.uniform(ks[3], (D, D), jnp.float32, -s, s)
        Wk = jax.random.uniform(ks[4], (D, D), jnp.float32, -s, s)
        Wv = jax.random.uniform(ks[5], (D, D), jnp.float32, -s, s)
        Wproj = jax.random.uniform(ks[6], (D, D), jnp.float32, -s, s)
        return {'q': q, 'k': k, 'v': v, 'Wq': Wq, 'Wk': Wk, 'Wv': Wv, 'Wproj': Wproj}
    _L0_xattn_all = _L0_xattn_setup()
    _L0_xattn_in = {k: v for k, v in _L0_xattn_all.items() if k in ('Wq', 'Wk', 'Wv', 'Wproj')}
    del _L0_xattn_all

    def _L0_ffn_setup():
        import jax, jax.numpy as jnp
        import numpy as np
        B, S, D, H, F = (4, 1024, 256, 16, 1024)
        CAP = 0.125
        ROPE_BASE = 10000.0

        def rmsnorm(x, g):
            return x * jax.lax.rsqrt(jnp.mean(x * x, -1, keepdims=True) + 1e-06) * g

        def rope(t, pos):
            hd = t.shape[-1]
            inv = 1.0 / ROPE_BASE ** (jnp.arange(0, hd, 2, dtype=jnp.float32) / hd)
            f = pos[:, None, :, None].astype(jnp.float32) * inv
            emb = jnp.concatenate([f, f], axis=-1)
            cos, sin = (jnp.cos(emb), jnp.sin(emb))
            rot = jnp.concatenate([-t[..., hd // 2:], t[..., :hd // 2]], axis=-1)
            return t * cos + rot * sin
        key = jax.random.key(seed)
        ks = jax.random.split(key, 9)
        scale = 0.02
        x = jax.random.normal(ks[0], (B, S, D), jnp.float32)
        causal = jnp.where(jnp.tril(jnp.ones((S, S), bool)), 0.0, -1000000000.0).astype(jnp.float32)
        attention_mask = jnp.broadcast_to(causal[None, None], (B, 1, S, S))
        position_ids = jnp.broadcast_to(jnp.arange(S, dtype=jnp.int32), (B, S))
        return {'x': x, 'attention_mask': attention_mask, 'position_ids': position_ids, 'router_w': jax.random.normal(ks[1], (D, 1), jnp.float32) * scale, 'router_b': jnp.zeros((1,), jnp.float32), 'wq': jax.random.normal(ks[2], (D, D), jnp.float32) * scale, 'wk': jax.random.normal(ks[3], (D, D), jnp.float32) * scale, 'wv': jax.random.normal(ks[4], (D, D), jnp.float32) * scale, 'wo': jax.random.normal(ks[5], (D, D), jnp.float32) * scale, 'w1': jax.random.normal(ks[6], (D, F), jnp.float32) * scale, 'w2': jax.random.normal(ks[7], (F, D), jnp.float32) * scale, 'ln1': jnp.ones((D,), jnp.float32), 'ln2': jnp.ones((D,), jnp.float32)}
    _L0_ffn_all = _L0_ffn_setup()
    _L0_ffn_in = {k: v for k, v in _L0_ffn_all.items() if k in ('attention_mask', 'position_ids', 'router_w', 'router_b', 'wq', 'wk', 'wv', 'wo', 'w1', 'w2', 'ln1', 'ln2')}
    del _L0_ffn_all

    def _L1_attn_setup():
        import jax, jax.numpy as jnp
        import numpy as np
        NUM_HEADS = 16
        key = jax.random.key(seed)
        ks = jax.random.split(key, 5)
        B, N, C = (4, 512, 256)
        s = 0.02
        return {'x': jax.random.normal(ks[0], (B, N, C), jnp.float32), 'w_qkv': jax.random.normal(ks[1], (C, 3 * C), jnp.float32) * s, 'b_qkv': jnp.zeros((3 * C,), jnp.float32), 'w_proj': jax.random.normal(ks[2], (C, C), jnp.float32) * s, 'b_proj': jnp.zeros((C,), jnp.float32)}
    _L1_attn_all = _L1_attn_setup()
    _L1_attn_in = {k: v for k, v in _L1_attn_all.items() if k in ('w_qkv', 'b_qkv', 'w_proj', 'b_proj')}
    del _L1_attn_all

    def _L1_xattn_setup():
        import jax, jax.numpy as jnp
        import numpy as np
        HIDDEN = 256
        HEADS = 16
        HEAD_DIM = HIDDEN // HEADS
        SCALE = 1.0 / np.sqrt(HEAD_DIM).astype(np.float32)
        key = jax.random.key(seed)
        ks = jax.random.split(key, 8)
        b, t = (2, 512)
        x = jax.random.normal(ks[0], (b, t, HIDDEN), dtype=jnp.float32)
        context = x
        s = 0.02
        Wq = jax.random.normal(ks[1], (HIDDEN, HIDDEN), dtype=jnp.float32) * s
        Wk = jax.random.normal(ks[2], (HIDDEN, HIDDEN), dtype=jnp.float32) * s
        Wv = jax.random.normal(ks[3], (HIDDEN, HIDDEN), dtype=jnp.float32) * s
        Wo = jax.random.normal(ks[4], (HIDDEN, HIDDEN), dtype=jnp.float32) * s
        bo = jnp.zeros((HIDDEN,), dtype=jnp.float32)
        return {'x': x, 'context': context, 'Wq': Wq, 'Wk': Wk, 'Wv': Wv, 'Wo': Wo, 'bo': bo}
    _L1_xattn_all = _L1_xattn_setup()
    _L1_xattn_in = {k: v for k, v in _L1_xattn_all.items() if k in ('Wq', 'Wk', 'Wv', 'Wo', 'bo')}
    del _L1_xattn_all

    def _L1_ffn_setup():
        import jax, jax.numpy as jnp
        import numpy as np
        B, S, D = (1, 512, 256)
        E, F = (16, 256)
        NG, TKG, K = (4, 2, 4)
        NSH = 2
        SCALE = 2.5
        STD = 0.02
        EPG = E // NG

        def _route(x_flat, router_w, bias):
            logits = x_flat.astype(jnp.float32) @ router_w.T
            scores = jax.nn.sigmoid(logits)
            s = scores + bias[None, :]
            sg = s.reshape(-1, NG, EPG)
            group_score = jax.lax.top_k(sg, 2)[0].sum(-1)
            gidx = jax.lax.top_k(group_score, TKG)[1]
            gmask = jnp.sum(jax.nn.one_hot(gidx, NG, dtype=jnp.float32), axis=1) > 0
            emask = jnp.repeat(gmask, EPG, axis=1)
            masked = jnp.where(emask, s, -1.0)
            topk_idx = jax.lax.top_k(masked, K)[1]
            tw = jnp.take_along_axis(scores, topk_idx, axis=1)
            tw = tw / (tw.sum(-1, keepdims=True) + 1e-20)
            tw = tw * SCALE
            return (topk_idx, tw)
        key = jax.random.key(seed)
        ks = jax.random.split(key, 8)
        return {'hidden_states': jax.random.normal(ks[0], (B, S, D), jnp.float32), 'router_w': jax.random.normal(ks[1], (E, D), jnp.float32) * STD, 'bias': jnp.zeros((E,), jnp.float32), 'gate_w': jax.random.normal(ks[2], (E, D, F), jnp.float32) * STD, 'up_w': jax.random.normal(ks[3], (E, D, F), jnp.float32) * STD, 'down_w': jax.random.normal(ks[4], (E, F, D), jnp.float32) * STD, 'sh_gate_w': jax.random.normal(ks[5], (D, NSH * F), jnp.float32) * STD, 'sh_up_w': jax.random.normal(ks[6], (D, NSH * F), jnp.float32) * STD, 'sh_down_w': jax.random.normal(ks[7], (NSH * F, D), jnp.float32) * STD}
    _L1_ffn_all = _L1_ffn_setup()
    _L1_ffn_in = {k: v for k, v in _L1_ffn_all.items() if k in ('router_w', 'bias', 'gate_w', 'up_w', 'down_w', 'sh_gate_w', 'sh_up_w', 'sh_down_w')}
    del _L1_ffn_all
    return {'x': x, 'ctx_1024': ctx_1024, 'L0_attn_Wqkv': _L0_attn_in['Wqkv'], 'L0_attn_bqkv': _L0_attn_in['bqkv'], 'L0_attn_gq': _L0_attn_in['gq'], 'L0_attn_gk': _L0_attn_in['gk'], 'L0_attn_Wout': _L0_attn_in['Wout'], 'L0_attn_bout': _L0_attn_in['bout'], 'L0_attn_gout': _L0_attn_in['gout'], 'L0_xattn_Wq': _L0_xattn_in['Wq'], 'L0_xattn_Wk': _L0_xattn_in['Wk'], 'L0_xattn_Wv': _L0_xattn_in['Wv'], 'L0_xattn_Wproj': _L0_xattn_in['Wproj'], 'L0_ffn_attention_mask': _L0_ffn_in['attention_mask'], 'L0_ffn_position_ids': _L0_ffn_in['position_ids'], 'L0_ffn_router_w': _L0_ffn_in['router_w'], 'L0_ffn_router_b': _L0_ffn_in['router_b'], 'L0_ffn_wq': _L0_ffn_in['wq'], 'L0_ffn_wk': _L0_ffn_in['wk'], 'L0_ffn_wv': _L0_ffn_in['wv'], 'L0_ffn_wo': _L0_ffn_in['wo'], 'L0_ffn_w1': _L0_ffn_in['w1'], 'L0_ffn_w2': _L0_ffn_in['w2'], 'L0_ffn_ln1': _L0_ffn_in['ln1'], 'L0_ffn_ln2': _L0_ffn_in['ln2'], 'L1_attn_w_qkv': _L1_attn_in['w_qkv'], 'L1_attn_b_qkv': _L1_attn_in['b_qkv'], 'L1_attn_w_proj': _L1_attn_in['w_proj'], 'L1_attn_b_proj': _L1_attn_in['b_proj'], 'L1_xattn_Wq': _L1_xattn_in['Wq'], 'L1_xattn_Wk': _L1_xattn_in['Wk'], 'L1_xattn_Wv': _L1_xattn_in['Wv'], 'L1_xattn_Wo': _L1_xattn_in['Wo'], 'L1_xattn_bo': _L1_xattn_in['bo'], 'L1_ffn_router_w': _L1_ffn_in['router_w'], 'L1_ffn_bias': _L1_ffn_in['bias'], 'L1_ffn_gate_w': _L1_ffn_in['gate_w'], 'L1_ffn_up_w': _L1_ffn_in['up_w'], 'L1_ffn_down_w': _L1_ffn_in['down_w'], 'L1_ffn_sh_gate_w': _L1_ffn_in['sh_gate_w'], 'L1_ffn_sh_up_w': _L1_ffn_in['sh_up_w'], 'L1_ffn_sh_down_w': _L1_ffn_in['sh_down_w']}

def reference(x, ctx_1024, L0_attn_Wqkv, L0_attn_bqkv, L0_attn_gq, L0_attn_gk, L0_attn_Wout, L0_attn_bout, L0_attn_gout, L0_xattn_Wq, L0_xattn_Wk, L0_xattn_Wv, L0_xattn_Wproj, L0_ffn_attention_mask, L0_ffn_position_ids, L0_ffn_router_w, L0_ffn_router_b, L0_ffn_wq, L0_ffn_wk, L0_ffn_wv, L0_ffn_wo, L0_ffn_w1, L0_ffn_w2, L0_ffn_ln1, L0_ffn_ln2, L1_attn_w_qkv, L1_attn_b_qkv, L1_attn_w_proj, L1_attn_b_proj, L1_xattn_Wq, L1_xattn_Wk, L1_xattn_Wv, L1_xattn_Wo, L1_xattn_bo, L1_ffn_router_w, L1_ffn_bias, L1_ffn_gate_w, L1_ffn_up_w, L1_ffn_down_w, L1_ffn_sh_gate_w, L1_ffn_sh_up_w, L1_ffn_sh_down_w):
    import jax
    import jax.numpy as jnp

    def _L0_attn_ref(x, Wqkv, bqkv, gq, gk, Wout, bout, gout):
        import jax, jax.numpy as jnp
        import numpy as np
        DIM = 256
        NUM_HEAD = 16
        DIM_HEAD = DIM // NUM_HEAD
        RMS_EPS = 1.1920929e-07
        EPS_LIN = 1e-06
        THETA = 10000.0

        def rmsnorm(x, g, eps=RMS_EPS):
            return x * jax.lax.rsqrt(jnp.mean(x * x, axis=-1, keepdims=True) + eps) * g

        def rope_cos_sin(seq_len, dim_head, dtype=jnp.float32):
            inv_freq = 1.0 / THETA ** (jnp.arange(0, dim_head, 2, dtype=dtype) / dim_head)
            t = jnp.arange(seq_len, dtype=dtype)
            freqs = jnp.outer(t, inv_freq)
            return (jnp.cos(freqs), jnp.sin(freqs))

        def apply_rope(t, cos, sin):
            tr = t[..., 0::2]
            ti = t[..., 1::2]
            out_r = tr * cos - ti * sin
            out_i = tr * sin + ti * cos
            return jnp.stack([out_r, out_i], axis=-1).reshape(t.shape)
        B, L, D = x.shape
        qkv = x @ Wqkv.T + bqkv
        q, k, v = jnp.split(qkv, 3, axis=-1)
        q = rmsnorm(q, gq)
        k = rmsnorm(k, gk)
        split = lambda t: t.reshape(B, L, NUM_HEAD, DIM_HEAD).transpose(0, 2, 1, 3)
        q, k, v = (split(q), split(k), split(v))
        cos, sin = rope_cos_sin(L, DIM_HEAD)
        cos = cos[None, None]
        sin = sin[None, None]
        q = apply_rope(q, cos, sin)
        k = apply_rope(k, cos, sin)
        qf = jax.nn.relu(q)
        kf = jax.nn.relu(k)
        vpad = jnp.concatenate([v, jnp.ones_like(v[..., :1])], axis=-1)
        vk = jnp.einsum('bhlp,bhld->bhpd', vpad, kf)
        res = jnp.einsum('bhpd,bhld->bhlp', vk, qf)
        attn = res[..., :-1] / (res[..., -1:] + EPS_LIN)
        attn = attn.transpose(0, 2, 1, 3).reshape(B, L, D)
        out = rmsnorm(attn @ Wout.T + bout, gout)
        return out

    def _L0_xattn_ref(q, k, v, Wq, Wk, Wv, Wproj):
        import jax, jax.numpy as jnp
        import numpy as np
        D_MODEL = 256
        NUM_HEADS = 16
        HEAD_SIZE = D_MODEL // NUM_HEADS
        L = q.shape[1]
        qh = jnp.einsum('bld,ed->ble', q, Wq)
        kh = jnp.einsum('bld,ed->ble', k, Wk)
        vh = jnp.einsum('bld,ed->ble', v, Wv)
        att = jnp.einsum('bqd,bkd->bqk', qh, kh) * HEAD_SIZE ** (-0.5)
        causal = jnp.tril(jnp.ones((L, L), dtype=bool))
        att = jnp.where(causal, att, -jnp.inf)
        att = jax.nn.softmax(att, axis=-1)
        y = jnp.einsum('bqk,bkd->bqd', att, vh)
        y = jnp.einsum('bld,ed->ble', y, Wproj)
        return y

    def _L0_ffn_ref(x, attention_mask, position_ids, router_w, router_b, wq, wk, wv, wo, w1, w2, ln1, ln2):
        import jax, jax.numpy as jnp
        import numpy as np
        B, S, D, H, F = (4, 1024, 256, 16, 1024)
        CAP = 0.125
        ROPE_BASE = 10000.0

        def rmsnorm(x, g):
            return x * jax.lax.rsqrt(jnp.mean(x * x, -1, keepdims=True) + 1e-06) * g

        def rope(t, pos):
            hd = t.shape[-1]
            inv = 1.0 / ROPE_BASE ** (jnp.arange(0, hd, 2, dtype=jnp.float32) / hd)
            f = pos[:, None, :, None].astype(jnp.float32) * inv
            emb = jnp.concatenate([f, f], axis=-1)
            cos, sin = (jnp.cos(emb), jnp.sin(emb))
            rot = jnp.concatenate([-t[..., hd // 2:], t[..., :hd // 2]], axis=-1)
            return t * cos + rot * sin
        b, s, d = x.shape
        hd = d // H
        weights = (x @ router_w)[..., 0] + router_b[0]
        k = int(CAP * s)
        topv, topi = jax.lax.top_k(weights, k)
        thr = topv[:, -1]
        sel_mask = (weights > thr[:, None]).astype(x.dtype)
        kc = k - 1
        sel_idx = jnp.sort(topi[:, :kc], axis=1)
        bidx = jnp.arange(b)[:, None]
        x_sel = x[bidx, sel_idx]
        pos_sel = position_ids[bidx, sel_idx]
        w_sel = weights[bidx, sel_idx]
        m = attention_mask[:, 0]
        m_sel = m[bidx[:, :, None], sel_idx[:, :, None], sel_idx[:, None, :]]
        hn = rmsnorm(x_sel, ln1)

        def heads(t):
            return t.reshape(b, kc, H, hd).transpose(0, 2, 1, 3)
        q = rope(heads(hn @ wq), pos_sel)
        kk = rope(heads(hn @ wk), pos_sel)
        v = heads(hn @ wv)
        sc = jnp.einsum('bhqd,bhkd->bhqk', q, kk) / np.sqrt(hd).astype(np.float32)
        sc = sc + m_sel[:, None]
        a = jax.nn.softmax(sc, axis=-1)
        o = jnp.einsum('bhqk,bhkd->bhqd', a, v).transpose(0, 2, 1, 3).reshape(b, kc, d) @ wo
        x1 = x_sel + o
        x2 = x1 + jax.nn.gelu(rmsnorm(x1, ln2) @ w1) @ w2
        proc = x2 * w_sel[..., None]
        out = jnp.zeros_like(x).at[bidx, sel_idx].set(proc)
        return out + x * (1.0 - sel_mask)[..., None]

    def _L1_attn_ref(x, w_qkv, b_qkv, w_proj, b_proj):
        import jax, jax.numpy as jnp
        import numpy as np
        NUM_HEADS = 16
        B, N, C = x.shape
        H = NUM_HEADS
        D = C // H
        scale = D ** (-0.5)
        qkv = x @ w_qkv + b_qkv
        qkv = qkv.reshape(B, N, 3, H, D)
        q, k, v = (jnp.moveaxis(qkv, 2, 0)[i] for i in range(3))
        scores = jnp.einsum('bqhd,bkhd->bhqk', q.astype(jnp.float32), k.astype(jnp.float32)) * scale
        attn = jax.nn.softmax(scores, axis=-1).astype(q.dtype)
        out = jnp.einsum('bhqk,bkhd->bqhd', attn, v).reshape(B, N, C)
        return out @ w_proj + b_proj

    def _L1_xattn_ref(x, context, Wq, Wk, Wv, Wo, bo):
        import jax, jax.numpy as jnp
        import numpy as np
        HIDDEN = 256
        HEADS = 16
        HEAD_DIM = HIDDEN // HEADS
        SCALE = 1.0 / np.sqrt(HEAD_DIM).astype(np.float32)
        b, t, c = x.shape
        kv_t = context.shape[1]
        q = x @ Wq.T
        k = context @ Wk.T
        v = context @ Wv.T
        q = q.reshape(b, t, HEADS, HEAD_DIM).transpose(0, 2, 1, 3)
        k = k.reshape(b, kv_t, HEADS, HEAD_DIM).transpose(0, 2, 1, 3)
        v = v.reshape(b, kv_t, HEADS, HEAD_DIM).transpose(0, 2, 1, 3)
        scores = jnp.einsum('bhqd,bhkd->bhqk', q, k) * SCALE
        causal = jnp.tril(jnp.ones((t, kv_t), dtype=bool))
        scores = jnp.where(causal[None, None, :, :], scores, -jnp.inf)
        probs = jax.nn.softmax(scores, axis=-1)
        y = jnp.einsum('bhqk,bhkd->bhqd', probs, v)
        y = y.transpose(0, 2, 1, 3).reshape(b, t, c)
        return y @ Wo.T + bo

    def _L1_ffn_ref(hidden_states, router_w, bias, gate_w, up_w, down_w, sh_gate_w, sh_up_w, sh_down_w):
        import jax, jax.numpy as jnp
        import numpy as np
        B, S, D = (1, 512, 256)
        E, F = (16, 256)
        NG, TKG, K = (4, 2, 4)
        NSH = 2
        SCALE = 2.5
        STD = 0.02
        EPG = E // NG

        def _route(x_flat, router_w, bias):
            logits = x_flat.astype(jnp.float32) @ router_w.T
            scores = jax.nn.sigmoid(logits)
            s = scores + bias[None, :]
            sg = s.reshape(-1, NG, EPG)
            group_score = jax.lax.top_k(sg, 2)[0].sum(-1)
            gidx = jax.lax.top_k(group_score, TKG)[1]
            gmask = jnp.sum(jax.nn.one_hot(gidx, NG, dtype=jnp.float32), axis=1) > 0
            emask = jnp.repeat(gmask, EPG, axis=1)
            masked = jnp.where(emask, s, -1.0)
            topk_idx = jax.lax.top_k(masked, K)[1]
            tw = jnp.take_along_axis(scores, topk_idx, axis=1)
            tw = tw / (tw.sum(-1, keepdims=True) + 1e-20)
            tw = tw * SCALE
            return (topk_idx, tw)
        x = hidden_states.reshape(-1, D)
        topk_idx, tw = _route(x, router_w, bias)
        combine = (jax.nn.one_hot(topk_idx, E, dtype=tw.dtype) * tw[..., None]).sum(1)
        h = jnp.einsum('td,edf->etf', x, gate_w)
        u = jnp.einsum('td,edf->etf', x, up_w)
        y = jnp.einsum('etf,efd->etd', jax.nn.silu(h) * u, down_w)
        routed = jnp.einsum('etd,te->td', y, combine)
        sh = jax.nn.silu(x @ sh_gate_w) * (x @ sh_up_w) @ sh_down_w
        return (routed + sh).reshape(hidden_states.shape)
    x = _layernorm(x + _L0_attn_ref(x, L0_attn_Wqkv, L0_attn_bqkv, L0_attn_gq, L0_attn_gk, L0_attn_Wout, L0_attn_bout, L0_attn_gout), axis=-1)
    x = _layernorm(x + _L0_xattn_ref(x, ctx_1024, ctx_1024, L0_xattn_Wq, L0_xattn_Wk, L0_xattn_Wv, L0_xattn_Wproj), axis=-1)
    x = _layernorm(x + _L0_ffn_ref(x, L0_ffn_attention_mask, L0_ffn_position_ids, L0_ffn_router_w, L0_ffn_router_b, L0_ffn_wq, L0_ffn_wk, L0_ffn_wv, L0_ffn_wo, L0_ffn_w1, L0_ffn_w2, L0_ffn_ln1, L0_ffn_ln2), axis=-1)
    x = _layernorm(x + _L1_attn_ref(x, L1_attn_w_qkv, L1_attn_b_qkv, L1_attn_w_proj, L1_attn_b_proj), axis=-1)
    x = _layernorm(x + _L1_xattn_ref(x, ctx_1024, L1_xattn_Wq, L1_xattn_Wk, L1_xattn_Wv, L1_xattn_Wo, L1_xattn_bo), axis=-1)
    x = _layernorm(x + _L1_ffn_ref(x, L1_ffn_router_w, L1_ffn_bias, L1_ffn_gate_w, L1_ffn_up_w, L1_ffn_down_w, L1_ffn_sh_gate_w, L1_ffn_sh_up_w, L1_ffn_sh_down_w), axis=-1)
    return x

_drawn_inputs = setup_inputs


def setup_inputs(seed=0):
    import zlib

    import numpy as np

    out = dict(_drawn_inputs(seed))
    spreads = {'L0_attn_gq': (1.0, 0.2),
     'L0_attn_gk': (1.0, 0.2),
     'L0_attn_gout': (1.0, 0.2),
     'L0_ffn_ln1': (1.0, 0.6),
     'L0_ffn_ln2': (1.0, 0.6),
     'L1_attn_b_qkv': (0.0, 0.1),
     'L1_attn_b_proj': (0.0, 0.1),
     'L1_xattn_bo': (0.0, 0.1),
     'L1_ffn_bias': (0.0, 0.452)}
    factors = {'L0_ffn_router_w': 4.91,
     'L0_ffn_wq': 8.0,
     'L0_ffn_wk': 8.0,
     'L0_ffn_wv': 7.169,
     'L0_ffn_wo': 7.496,
     'L0_ffn_w1': 5.405,
     'L0_ffn_w2': 5.338,
     'L1_xattn_Wq': 8.0,
     'L1_xattn_Wk': 8.0,
     'L1_ffn_router_w': 3.736,
     'L1_ffn_gate_w': 2.754,
     'L1_ffn_up_w': 2.686,
     'L1_ffn_down_w': 2.706,
     'L1_ffn_sh_gate_w': 2.688,
     'L1_ffn_sh_up_w': 2.699,
     'L1_ffn_sh_down_w': 2.667}
    for name, (base, spread) in spreads.items():
        noise = np.random.default_rng([zlib.crc32(name.encode()), seed]).standard_normal(out[name].shape)
        drawn = base * np.exp(spread * noise) if base else spread * noise
        out[name] = jnp.asarray(drawn.astype(out[name].dtype))
    for name, factor in factors.items():
        out[name] = (out[name] * factor).astype(out[name].dtype)
    return out
```

```python
from contextlib import ExitStack

import numpy as np

import concourse.bass as bass
from concourse import mybir
from concourse.alu_op_type import AluOpType as ALU

F32 = mybir.dt.float32
BF16 = mybir.dt.bfloat16
I32 = mybir.dt.int32
ACT = mybir.ActivationFunctionType
AX = mybir.AxisListType

P = 128
B = 16
D = 256
KC = D // P
H = 16
HD = D // H
HH = H // KC
QH = 4
NQ = H // QH
SCALE = HD ** -0.5
VW = P + 2
NW = P + HH
HV = HD + 1

SEL = int(0.125 * P) - 1
TSEQ = 8
TILES = B // TSEQ
S = SEL * TSEQ
F0 = 1024
FC = F0 // P
XW = D + 2
E = 16
EF = 256
NE = E + 2
GT = 512
G = B * P // GT
TG = GT // P
GROUPS, TOPG, TOPK = 4, 2, 4
EPG = E // GROUPS
MOE_SCALE = 2.5

RMS_EPS = 1.1920929e-07
LIN_EPS = 1e-06
FFN_EPS = 1e-06
LN_EPS = 1e-05
NEG = -1e30
FAR = -3e38
BIG = 3e38
MAGIC = 1.5 * 2.0 ** 23
PI = float(np.pi)


def layout(*fields):
    at, where = 0, {}
    for name, width in fields:
        where[name] = slice(at, at + width)
        at += width
    return where, at


CONST, N_CONST = layout(("ident", P), ("causal", P), ("before", P), ("blocks", P), ("heads", HH),
                        ("cos", D), ("sin", D), ("slots", P), ("seqslot", B), ("apart", S),
                        ("invfreq", 8), ("key", E), ("half", 2), ("ln_eps", 1), ("rms_eps", 2))
ROWS, N_ROWS = layout(("bqkv", 3 * D), ("gq", D), ("gk", D), ("bout", D), ("gout", D), ("ln1", D),
                      ("ln2", D), ("bv", D), ("bproj", D), ("bo", D), ("router_b", 1), ("ebias", E))
COLS, N_COLS = layout(("bqk", 2 * KC), ("router_w", KC))


def constants():
    c = np.zeros((P, N_CONST), np.float32)
    p = np.arange(P)[:, None]
    j = np.arange(P)[None, :]
    c[:, CONST["ident"]] = p == j
    c[:, CONST["causal"]] = np.where(j <= p, 0.0, NEG)
    c[:, CONST["before"]] = j < p
    c[:, CONST["blocks"]] = p // HD == j // HD
    c[:, CONST["heads"]] = p // HD == np.arange(HH)[None, :]
    inv = (1.0 / np.float32(10000.0) ** (np.arange(0, HD, 2, dtype=np.float32) / HD)).astype(np.float32)
    angle = np.arange(P, dtype=np.float32)[:, None] * inv[None, :]
    c[:, CONST["cos"]] = np.tile(np.repeat(np.cos(angle), 2, axis=1), (1, H))
    sine = np.stack([-np.sin(angle), np.sin(angle)], axis=-1).reshape(P, HD)
    c[:, CONST["sin"]] = np.tile(sine, (1, H))
    c[:, CONST["slots"]] = j
    c[:, CONST["seqslot"]] = (np.arange(B) % TSEQ)[None, :] * SEL
    c[:S, CONST["apart"]] = np.where(p[:S] // SEL == j[:, :S] // SEL, 0.0, FAR)
    c[:, CONST["invfreq"]] = inv
    c[:, CONST["key"]] = E - np.arange(E)
    c[:, CONST["half"]] = -0.5
    c[:, CONST["ln_eps"]] = LN_EPS
    c[:, CONST["rms_eps"]] = RMS_EPS
    return c


class Turn:

    def __init__(self, b, p, half):
        self.b, self.p, self.half = b, p, half
        self.peeled = isinstance(b, int)


def turn(b):
    return Turn(b, b % 2, b // 2)


class Step:

    def __init__(self, sem, n, round=0, turns=B):
        self.sem, self.n, self.round, self.turns = sem, n, round, turns

    def again(self, round):
        return Step(self.sem, self.n, round, self.turns)

    def at(self, t, k, back=0):
        return self.n * (t.b + self.turns * self.round - back) + k

    def end(self):
        return self.n * self.turns * (self.round + 1)


def wait(eng, step, t, k, back=0):
    if t.peeled and t.b + step.turns * step.round < back:
        return
    eng.wait_ge(step.sem, step.at(t, k, back))


def wait_end(eng, step):
    eng.wait_ge(step.sem, step.end())


def pipelined(eng, stages, start=0, stop=B, peel=0):
    deepest = max(lag for _, lag in stages)
    first = start + max(deepest + deepest % 2 + 2, peel)

    def iteration(i):
        for stage, lag in stages:
            if start <= i - lag < stop:
                stage(turn(i - lag))

    for i in range(start, first):
        iteration(i)
    with eng.Fori(first // 2, stop // 2) as j:
        for u in (0, 1):
            for stage, lag in stages:
                b = u - lag
                stage(Turn(2 * j + b, b % 2, j + b // 2))
    for i in range(stop, stop + deepest):
        iteration(i)


def build(nc, a):
    out = a["out"]
    with ExitStack() as ctx:
        def sb(name, shape, dt=F32):
            return ctx.enter_context(nc.sbuf_tensor(name, shape, dt))

        def sem(name):
            return ctx.enter_context(nc.semaphore(name))

        def step(name, n, turns=B):
            return Step(sem(name), n, 0, turns)

        bank = [ctx.enter_context(nc.psum_tensor(f"bank{i}", [P, 512], F32)) for i in range(8)]

        X = sb("X", [P, B, XW])
        const = sb("const", [P, N_CONST])
        rows = sb("rows", [P, N_ROWS])
        cols = sb("cols", [P, N_COLS])
        ident_bf = sb("ident_bf", [P, P], BF16)
        causal_bf = sb("causal_bf", [P, P], BF16)
        xs = [sb(f"xs{i}", [P, D]) for i in range(2)]
        xT = [sb(f"xT{i}", [P, KC, P]) for i in range(2)]
        inT = [sb(f"inT{i}", [P, KC, P]) for i in range(2)]
        y = [sb(f"y{i}", [P, D]) for i in range(2)]
        bn = [sb(f"bn{i}", [P, 6]) for i in range(2)]
        mv = [sb(f"mv{i}", [P, 2]) for i in range(2)]
        lr = [sb(f"lr{i}", [P, 2]) for i in range(2)]
        keep1 = sb("keep1", [P, B])

        def c(name, n=P):
            return const[0:n, CONST[name]]

        def row(name, n=P):
            return rows[0:n, ROWS[name]]

        ident = c("ident")

        ARENA = 39 * 1024
        arena = sb("arena", [P, ARENA])

        class Carve:
            def __init__(self, at):
                self.at = at

            def __call__(self, *shape):
                n = int(np.prod(shape))
                self.at += self.at % 2
                view = arena[:, self.at:self.at + n]
                self.at += n
                assert self.at <= ARENA, self.at
                if len(shape) == 2:
                    view = view.rearrange("p (a b) -> p a b", b=shape[1])
                if len(shape) == 3:
                    view = view.rearrange("p (a b c) -> p a b c", b=shape[1], c=shape[2])
                return view

        A = Carve(0)
        a_w = A(KC, 3 * D)
        a_wout = A(KC, D)
        a_cos = A(2 * D)
        a_sin = A(2 * D)
        a_qk = [A(2 * D) for _ in range(2)]
        a_v = [A(KC, VW) for _ in range(2)]
        a_ms = [A(2) for _ in range(2)]
        a_sqs = [A(3, D) for _ in range(2)]
        a_r = [A(2) for _ in range(2)]
        a_u = [A(2 * D) for _ in range(2)]
        a_sw = [A(2 * D) for _ in range(2)]
        a_f = [A(2 * D) for _ in range(2)]
        a_kv = [A(KC, NW) for _ in range(2)]
        a_fT = [A(KC, P) for _ in range(2)]
        a_den = [A(KC, HH) for _ in range(2)]
        a_rden = [A(KC, HH) for _ in range(2)]
        a_at = [A(D) for _ in range(2)]
        a_atT = [A(KC, P) for _ in range(2)]
        a_o = [A(D) for _ in range(2)]
        a_oms = [A(1) for _ in range(2)]
        a_or = [A(2) for _ in range(2)]
        b_wq = A(KC, D)
        b_wk = A(KC, D)
        b_wv = A(KC, D)
        b_wp = A(KC, D)
        b_A = A(KC, D)
        b_B = A(KC, D)
        b_qT = [A(KC, P) for _ in range(2)]
        b_v = [A(D) for _ in range(2)]
        b_s = [A(P) for _ in range(2)]
        b_nmax = [A(1) for _ in range(2)]
        b_p = [A(P) for _ in range(2)]
        b_sum = [A(1) for _ in range(2)]
        b_rsum = [A(1) for _ in range(2)]
        b_pT = [A(P) for _ in range(2)]
        c_wqkv = A(KC, 3 * D)
        c_wo = A(KC, D)
        c_w1 = A(KC, F0)
        c_w2 = A(FC, D)
        c_mask = A(4, P)
        c_posi = A(4)
        c_rw = A(KC, P)
        c_ET = A(B, P)
        c_proc = A(TILES, D)
        weights_end = A.at
        A = Carve(0)
        c_wr = [A(P) for _ in range(2)]
        c_small = [A(4) for _ in range(2)]
        c_counts = A(B, 4)
        c_slot, c_over = A(B), A(B)
        c_cmp = [A(4, P) for _ in range(2)]
        c_E = [A(P) for _ in range(2)]
        c_U = [A(P) for _ in range(2)]
        c_ets = [A(P) for _ in range(2)]
        c_sel = [A(XW) for _ in range(TILES)]
        c_sqs = [A(2, D) for _ in range(TILES)]
        c_msk = [A(S) for _ in range(TILES)]
        c_st = [A(16) for _ in range(TILES)]
        c_hn = [A(D) for _ in range(TILES)]
        c_hT = A(KC, TILES * S)
        c_ang = [A(8, 8) for _ in range(TILES)]
        c_arg = [A(2, 8) for _ in range(TILES)]
        c_cs = [A(3, 8) for _ in range(TILES)]
        c_x = [A(2 * D) for _ in range(TILES)]
        c_z = [A(2 * D) for _ in range(TILES)]
        c_v = [A(H, HV) for _ in range(TILES)]
        c_qT = [A(KC, S) for _ in range(TILES)]
        c_rs = [A(H) for _ in range(TILES)]
        c_at = [A(D) for _ in range(TILES)]
        c_oT = [A(KC, S) for _ in range(TILES)]
        c_x1 = [A(D) for _ in range(TILES)]
        A = Carve(weights_end)
        c_kexp = A(H, S)
        c_S = [A(H, S) for _ in range(TILES)]
        c_mx = [A(H) for _ in range(TILES)]
        c_pT = [A(H, S) for _ in range(TILES)]
        c_gT = A(FC, TILES * S)
        A = Carve(0)
        d_w = [A(KC, 4 * D) for _ in range(2)]
        d_bq = A(KC)
        d_qT = [A(KC, P) for _ in range(2)]
        d_kT = [A(KC, P) for _ in range(2)]
        d_kexp = [A(H, P) for _ in range(2)]
        d_v = [A(H, HV) for _ in range(2)]
        d_S = [A(H, P) for _ in range(2)]
        d_mx = [A(H) for _ in range(2)]
        d_pT = [A(H, P) for _ in range(2)]
        d_rs = [A(H) for _ in range(2)]
        d_at = [A(D) for _ in range(2)]
        d_atT = [A(KC, P) for _ in range(2)]
        d_xb = [A(D) for _ in range(2)]
        f_rw = A(KC, E)
        f_XT = A(KC, B * P)
        A = Carve(0)
        f_lg = A(B, E)
        f_sc = A(B, E)
        f_s = A(B, E)
        f_pair = A(B * GROUPS, 6)
        f_gs = A(B, GROUPS)
        f_c1 = A(B * GROUPS, GROUPS)
        f_c2 = A(B * GROUPS, GROUPS)
        f_gm = A(B, GROUPS)
        f_v = A(B, E)
        f_eq = A(B, E)
        f_m = A(B)
        f_sel = A(B, E)
        f_comb = A(B, NE)
        f_ws = [A(3 * KC, EF) for _ in range(2)]
        f_h = [A(GT) for _ in range(2)]
        f_a = [A(KC, GT) for _ in range(2)]
        f_out = [A(D) for _ in range(2)]

        l_const = sem("l_const")
        held = sem("held")
        l_aw = sem("l_aw")
        l_rows = sem("l_rows")
        l_x = sem("l_x")
        l_bw = sem("l_bw")
        l_cw = sem("l_cw")
        l_dw = [sem("l_dw0"), sem("l_dw1")]
        l_inT = [sem("l_inT0"), sem("l_inT1")]
        l_ew = [sem("l_ew0"), sem("l_ew1")]
        s_out = [sem("s_out0"), sem("s_out1")]
        a_tab = sem("a_tab")

        copied = step("copied", 1)
        turned = step("turned", 1)
        xt_done = step("xt_done", 1)
        stats = step("stats", 2)
        rstd = step("rstd", 2)
        normed = step("normed", 1)
        a_qkp = step("a_qkp", 1)
        a_vp = step("a_vp", 1)
        a_qkb = step("a_qkb", 1)
        a_vb = step("a_vb", 1)
        a_sq = step("a_sq", 2)
        a_rms = step("a_rms", 2)
        a_swap = step("a_swap", 2)
        a_turn = step("a_turn", 1)
        a_rope = step("a_rope", 1)
        a_relu = step("a_relu", 2)
        a_kvp = step("a_kvp", 1)
        a_fTp = step("a_fTp", 1)
        a_kvm = step("a_kvm", 2)
        a_fTc = step("a_fTc", 1)
        a_nd = step("a_nd", 1)
        a_div = step("a_div", 3)
        a_atp = step("a_atp", 1)
        a_atc = step("a_atc", 1)
        a_op = step("a_op", 1)
        a_ob = step("a_ob", 1)
        a_osq = step("a_osq", 1)
        a_orms = step("a_orms", 2)
        a_y = step("a_y", 2)
        b_fold = step("b_fold", 2, 1)
        b_folded = step("b_folded", 2, 1)
        b_qp = step("b_qp", 1)
        b_vp = step("b_vp", 1)
        b_qc = step("b_qc", 1)
        b_vc = step("b_vc", 1)
        b_sp = step("b_sp", 1)
        b_max = step("b_max", 1)
        b_exp = step("b_exp", 1)
        b_pTp = step("b_pTp", 1)
        b_pTc = step("b_pTc", 2)
        b_yp = step("b_yp", 1)
        b_y = step("b_y", 1)
        c_prep = sem("c_prep")
        c_wp = step("c_wp", 1)
        c_wc = step("c_wc", 1)
        c_cnt = step("c_cnt", 4)
        c_kept = step("c_kept", 1)
        c_place = sem("c_place")
        c_hot = step("c_hot", 1)
        c_Up = step("c_Up", 1)
        c_Uc = step("c_Uc", 1)
        c_ETp = step("c_ETp", 1)
        c_ETc = step("c_ETc", 1)
        c_gp = step("c_gp", 1)
        c_mp = step("c_mp", 1)
        c_pe = sem("c_pe")
        c_dve = sem("c_dve")
        c_act = sem("c_act")
        c_pool = sem("c_pool")
        c_link = sem("c_link")

        def stage_at(k, g):
            return TILES * k + g + 1

        dve_at = act_at = stage_at

        def keys_at(g):
            return TILES * 5 + 2 * (g + 1)

        c_fp = step("c_fp", 4, 1)
        c_gelu = step("c_gelu", 4, 1)
        c_etsc = step("c_etsc", 1)
        c_sp = step("c_sp", 1)
        c_y = step("c_y", 1)
        d_prep = sem("d_prep")
        d_qkp = step("d_qkp", 1)
        d_vp = step("d_vp", 1)
        d_qkc = step("d_qkc", 4)
        d_vc = step("d_vc", 1)
        d_kx = step("d_kx", 2)
        d_xbc = step("d_xbc", 1)
        d_sp = step("d_sp", NQ)
        d_max = step("d_max", 2 * NQ)
        d_exp = step("d_exp", NQ)
        d_pTp = step("d_pTp", NQ)
        d_pTc = step("d_pTc", NQ)
        d_pv = step("d_pv", 1)
        d_div = step("d_div", 2)
        d_atp = step("d_atp", 1)
        d_atc = step("d_atc", 1)
        d_op = step("d_op", 1)
        d_y = step("d_y", 1)
        f_xtc = step("f_xtc", 1)
        f_lp = step("f_lp", 1)
        f_lc = step("f_lc", 1)
        f_sig = sem("f_sig")
        f_route = sem("f_route")
        MT = NE * G
        f_hp = step("f_hp", 4, MT)
        f_silu = step("f_silu", 2, MT)
        f_mul = step("f_mul", 2, MT)
        f_dp = step("f_dp", 2, MT)
        f_acc = step("f_acc", TG, MT)

        A_, B_, C_, D_, E_, F_ = range(6)
        XT = {B_: 0, C_: 1, D_: 2, E_: 3, F_: 4}

        block = ctx.enter_context(nc.Block())

        def hold(eng):
            eng.sem_inc(held, 1)

        @block.sync
        def _(sp):
            def load_x(t):
                wait(sp, a_vp, t, 1, back=2)
                sp.dma_start(inT[t.p][:], a["xT"][t.b]).then_inc(l_inT[t.p], 16)

            def load_ctx_b(t):
                if not t.peeled or t.b >= 2:
                    wait(sp, b_sp, t, 1, back=2)
                    wait(sp, b_vp, t, 1, back=2)
                else:
                    wait_end(sp, a_vp)
                sp.dma_start(inT[t.p][:], a["ctxT"][t.b]).then_inc(l_inT[t.p], 16)

            def load_ctx_e(t):
                vp = d_vp.again(1)
                if not t.peeled or t.b >= 2:
                    wait(sp, vp, t, 1, back=2)
                else:
                    wait_end(sp, b_sp)
                sp.dma_start(inT[t.p][:], a["ctxT"][t.b]).then_inc(l_inT[t.p], 16)

            load_x(turn(0))
            sp.dma_start(const[:], a["const"]).then_inc(l_const, 16)
            load_x(turn(1))
            sp.dma_start(X[:, :, 0:D], a["x"].rearrange("b p d -> p b d")).then_inc(l_x, 16)
            sp.dma_start(b_wq, a["b_wq"]).then_inc(l_bw, 16)
            sp.dma_start(b_wk, a["b_wk"]).then_inc(l_bw, 16)
            sp.dma_start(b_wv, a["b_wv"]).then_inc(l_bw, 16)
            sp.dma_start(b_wp, a["b_wp"]).then_inc(l_bw, 16)
            sp.dma_start(c_wqkv, a["c_wqkv"]).then_inc(l_cw, 16)
            sp.dma_start(c_wo, a["c_wo"]).then_inc(l_cw, 16)
            sp.dma_start(c_w1, a["c_w1"]).then_inc(l_cw, 16)
            sp.dma_start(c_w2, a["c_w2"]).then_inc(l_cw, 16)
            sp.dma_start(c_mask, a["mask"]).then_inc(l_cw, 16)
            sp.dma_start(c_posi.bitcast(I32), a["pos"]).then_inc(l_cw, 16)
            load_x(turn(2))
            load_x(turn(3))
            with sp.Fori(2, B // 2) as j:
                for u in (0, 1):
                    load_x(Turn(2 * j + u, u, j))
            load_ctx_b(turn(0))
            load_ctx_b(turn(1))
            with sp.Fori(1, B // 2) as j:
                for u in (0, 1):
                    load_ctx_b(Turn(2 * j + u, u, j))
            wait_end(sp, c_sp)
            sp.dma_start(d_w[0], a["d_w"]).then_inc(l_dw[0], 16)
            sp.dma_start(d_w[1], a["e_w"]).then_inc(l_dw[1], 16)
            sp.dma_start(f_rw, a["f_rw"]).then_inc(l_dw[1], 16)
            load_ctx_e(turn(0))
            load_ctx_e(turn(1))
            with sp.Fori(1, B // 2) as j:
                for u in (0, 1):
                    load_ctx_e(Turn(2 * j + u, u, j))
            sp.wait_ge(normed.sem, normed.again(E_).end())
            sp.dma_start(f_ws[0], a["f_w"][0]).then_inc(l_ew[0], 16)
            sp.dma_start(f_ws[1], a["f_w"][1]).then_inc(l_ew[1], 16)
            with sp.Fori(1, NE // 2) as j:
                for u in (0, 1):
                    sp.wait_ge(f_dp.sem, f_dp.n * G * (2 * j + u - 1))
                    sp.dma_start(f_ws[u], a["f_w"][2 * j + u]).then_inc(l_ew[u], 16)
            for b in range(B):
                sp.wait_ge(normed.sem, normed.again(F_).at(turn(b), 1))
                sp.dma_start(out[b], f_out[b % 2]).then_inc(s_out[b % 2], 16)
            for q in s_out:
                sp.wait_ge(q, 16 * (B // 2))

        @block.gpsimd
        def _(pool):
            def copy_x(round, before):
                step_ = copied.again(XT[round])
                def stage(t):
                    wait(pool, normed.again(before), t, 1)
                    wait(pool, turned.again(XT[round]), t, 1, back=2)
                    pool.tensor_copy(xs[t.p][:], X[:, t.b, 0:D]).then_inc(step_.sem, 1)
                return stage

            def ln_power(round):
                st, rs, nd = stats.again(round), rstd.again(round), normed.again(round)
                def stage(t):
                    wait(pool, st, t, 2)
                    wait(pool, nd, t, 1, back=2)
                    pool.tensor_tensor(lr[t.p][:, 0:1], mv[t.p][:, 1:2], c("ln_eps"), ALU.add).then_inc(rs.sem, 1)
                    wait(pool, rs, t, 1)
                    pool.tensor_tensor(lr[t.p][:, 1:2], lr[t.p][:, 0:1], c("half")[:, 0:1], ALU.pow).then_inc(rs.sem, 1)
                return stage

            pool.wait_ge(l_const, 16)

            def a_swap_(t):
                wait(pool, a_qkb, t, 1)
                wait(pool, a_rope, t, 1, back=2)
                q = a_qk[t.p].rearrange("p (n two) -> p n two", two=2)
                s_ = a_sin.rearrange("p (n two) -> p n two", two=2)
                o = a_sw[t.p].rearrange("p (n two) -> p n two", two=2)
                if t.peeled and t.b == 0:
                    pool.wait_ge(a_tab, 6)
                pool.tensor_tensor(o[:, :, 0], q[:, :, 1], s_[:, :, 0], ALU.mult).then_inc(a_swap.sem, 1)
                pool.tensor_tensor(o[:, :, 1], q[:, :, 0], s_[:, :, 1], ALU.mult).then_inc(a_swap.sem, 1)

            def a_rms_(t):
                wait(pool, a_sq, t, 2)
                wait(pool, a_relu, t, 2, back=2)
                pool.tensor_tensor(a_ms[t.p], a_ms[t.p], c("rms_eps"), ALU.add).then_inc(a_rms.sem, 1)
                wait(pool, a_rms, t, 1)
                pool.tensor_tensor(a_r[t.p], a_ms[t.p], c("half"), ALU.pow).then_inc(a_rms.sem, 1)

            def a_orms_(t):
                wait(pool, a_osq, t, 1)
                wait(pool, a_y, t, 1, back=2)
                pool.tensor_tensor(a_or[t.p][:, 0:1], a_oms[t.p], c("rms_eps")[:, 0:1], ALU.add).then_inc(a_orms.sem, 1)
                wait(pool, a_orms, t, 1)
                pool.tensor_tensor(a_or[t.p][:, 1:2], a_or[t.p][:, 0:1], c("half")[:, 0:1], ALU.pow).then_inc(a_orms.sem, 1)

            pipelined(pool, [(ln_power(A_), 6), (a_orms_, 5), (a_swap_, 1), (a_rms_, 1)])

            pipelined(pool, [(ln_power(B_), 4), (copy_x(B_, A_), 0)])

            def c_kept_(t):
                wait(pool, c_cnt, t, 4)
                pool.tensor_copy(c_counts[:, t.b, :], c_small[t.p]).then_inc(c_kept.sem, 1)

            pipelined(pool, [(copy_x(C_, B_), 0), (c_kept_, 2)])
            for k in (0, 2):
                for g in range(TILES):
                    pool.wait_ge(c_act, act_at(0 if k == 0 else 7, g))
                    pool.tensor_scalar(c_st[g][0:S, 1 + k:2 + k], c_st[g][0:S, k:k + 1], FFN_EPS, None,
                                       ALU.add).then_inc(c_pool, 1)
                    pool.wait_ge(c_pool, 2 * (k // 2 * TILES + g) + 1)
                    pool.tensor_tensor(c_st[g][0:S, 4 + k:5 + k], c_st[g][0:S, 1 + k:2 + k], c("half", S)[:, 0:1],
                                       ALU.pow).then_inc(c_pool, 1)

            def c_ets_(t):
                wait(pool, c_ETc, t, 1)
                wait(pool, c_sp, t, 1, back=2)
                pool.tensor_copy(c_ets[t.p][0:S], c_ET[0:S, t.b, :]).then_inc(c_etsc.sem, 1)

            pipelined(pool, [(c_ets_, 0), (ln_power(C_), 1)])

            for n, round in enumerate((D_, E_)):
                def d_kx_(t, n=n):
                    kx = d_kx.again(n)
                    wait(pool, d_sp.again(n), t, NQ, back=2)
                    for k in range(KC):
                        wait(pool, d_qkc.again(n), t, k + 1)
                        pool.tensor_tensor(d_kexp[t.p][:, k * HH:(k + 1) * HH, :],
                                           d_kT[t.p][:, k:k + 1, :].to_broadcast([P, HH, P]),
                                           c("heads").unsqueeze(2).to_broadcast([P, HH, P]),
                                           ALU.mult).then_inc(kx.sem, 1)

                def d_xb_(t, n=n, round=round):
                    wait(pool, normed.again(round - 1), t, 1)
                    wait(pool, d_y.again(n), t, 1, back=2)
                    hold(pool)
                    pool.tensor_tensor(d_xb[t.p], X[:, t.b, 0:D], row("bproj" if n == 0 else "bo"),
                                       ALU.add).then_inc(d_xbc.sem, 1)

                pipelined(pool, [(ln_power(round), 4), (copy_x(round, round - 1), 0), (d_xb_, 3), (d_kx_, 1)])

            def f_xt_(t):
                wait(pool, xt_done.again(XT[F_]), t, 1)
                pool.tensor_copy(f_XT.rearrange("p k (b t) -> p k b t", b=B)[:, :, t.b, :], xT[t.p][:])\
                    .then_inc(f_xtc.sem, 1)

            pipelined(pool, [(copy_x(F_, E_), 0), (f_xt_, 1)])
            pipelined(pool, [(ln_power(F_), 0)])

        @block.tensor
        def _(pe):
            def turn_x(round, free=None):
                tu = turned.again(XT[round])
                def stage(t):
                    wait(pe, copied.again(XT[round]), t, 1)
                    wait(pe, xt_done.again(XT[round]), t, 1, back=1)
                    if free is not None and t.peeled:
                        free(t)
                    for k in range(KC):
                        m = pe.transpose(bank[0][:, k * P:(k + 1) * P], xs[t.p][:, k * P:(k + 1) * P], ident)
                    m.then_inc(tu.sem, 1)
                return stage

            def product(o, lhs, rhs):
                n = len(lhs)
                for k in range(n):
                    m = pe.matmul(o, lhs[k], rhs[k], start=k == 0, stop=k == n - 1)
                return m

            def transposes(o, src, n, width):
                for k in range(n):
                    m = pe.transpose(o[:, k * width:(k + 1) * width], src(k), ident[0:width, 0:width])
                return m

            pe.wait_ge(l_const, 16)
            pe.wait_ge(l_aw, 32)

            def a_qkp_(t):
                pe.wait_ge(l_inT[t.p], 16 * (t.half + 1))
                wait(pe, a_qkb, t, 1, back=1)
                product(bank[1][:, 0:2 * D], [inT[t.p][:, k, :] for k in range(KC)],
                        [a_w[:, k, 0:2 * D] for k in range(KC)]).then_inc(a_qkp.sem, 1)

            def a_vp_(t):
                wait(pe, a_vb, t, 1, back=1)
                product(bank[2][:, 0:D], [inT[t.p][:, k, :] for k in range(KC)],
                        [a_w[:, k, 2 * D:3 * D] for k in range(KC)]).then_inc(a_vp.sem, 1)

            def a_kv_(t):
                wait(pe, a_relu, t, 2)
                wait(pe, a_kvm, t, 2, back=1)
                wait(pe, a_vb, t, 1)
                for h in range(KC):
                    m = pe.matmul(bank[3][:, h * VW:(h + 1) * VW], a_f[t.p][:, D + h * P:D + (h + 1) * P],
                                  a_v[t.p][:, h, :], start=True, stop=True)
                m.then_inc(a_kvp.sem, 1)
                wait(pe, a_fTc, t, 1, back=1)
                transposes(bank[4], lambda k: a_f[t.p][:, k * P:(k + 1) * P], KC, P).then_inc(a_fTp.sem, 1)

            def a_nd_(t):
                wait(pe, a_kvm, t, 2)
                wait(pe, a_fTc, t, 1)
                wait(pe, a_div, t, 3, back=1)
                for h in range(KC):
                    m = pe.matmul(bank[5][:, h * NW:(h + 1) * NW], a_fT[t.p][:, h, :], a_kv[t.p][:, h, :],
                                  start=True, stop=True)
                m.then_inc(a_nd.sem, 1)

            def a_atp_(t):
                wait(pe, a_div, t, 3)
                wait(pe, a_atc, t, 1, back=1)
                transposes(bank[6], lambda k: a_at[t.p][:, k * P:(k + 1) * P], KC, P).then_inc(a_atp.sem, 1)

            def a_op_(t):
                wait(pe, a_atc, t, 1)
                wait(pe, a_ob, t, 1, back=1)
                product(bank[7][:, 0:D], [a_atT[t.p][:, k, :] for k in range(KC)],
                        [a_wout[:, k, :] for k in range(KC)]).then_inc(a_op.sem, 1)

            pipelined(pe, [(a_nd_, 4), (a_kv_, 3), (a_qkp_, 0), (a_atp_, 4), (a_vp_, 1), (a_op_, 4)])

            pe.wait_ge(l_bw, 64)
            wait_end(pe, a_vb)
            for n, (o, wl, wr) in enumerate(((bank[1], b_wq, b_wk), (bank[2], b_wv, b_wp))):
                for k in range(KC):
                    m = product(o[:, k * D:(k + 1) * D], [wl[:, e, k * P:(k + 1) * P] for e in range(KC)],
                                [wr[:, e, :] for e in range(KC)])
                m.then_inc(b_fold.sem, 1)

            def b_q_(t):
                wait(pe, xt_done.again(XT[B_]), t, 1)
                wait(pe, b_qc, t, 1, back=1)
                if t.peeled and t.b == 0:
                    wait_end(pe, b_folded)
                for k in range(KC):
                    m = product(bank[1][:, k * P:(k + 1) * P], [b_A[:, j, k * P:(k + 1) * P] for j in range(KC)],
                                [xT[t.p][:, j, :] for j in range(KC)])
                m.then_inc(b_qp.sem, 1)

            def b_v_(t):
                pe.wait_ge(l_inT[t.p], 16 * (B // 2 + t.half + 1))
                wait(pe, b_vc, t, 1, back=1)
                product(bank[2][:, 0:D], [inT[t.p][:, k, :] for k in range(KC)],
                        [b_B[:, k, :] for k in range(KC)]).then_inc(b_vp.sem, 1)

            def b_s_(t):
                pe.wait_ge(l_inT[t.p], 16 * (B // 2 + t.half + 1))
                wait(pe, b_qc, t, 1)
                wait(pe, b_max, t, 1, back=1)
                if t.peeled and t.b == 0:
                    wait_end(pe, a_kvm)
                product(bank[3][:, 0:P], [b_qT[t.p][:, k, :] for k in range(KC)],
                        [inT[t.p][:, k, :] for k in range(KC)]).then_inc(b_sp.sem, 1)

            def b_pT_(t):
                wait(pe, b_exp, t, 1)
                wait(pe, b_pTc, t, 2, back=1)
                if t.peeled and t.b == 0:
                    wait_end(pe, a_fTc)
                pe.transpose(bank[4][:, 0:P], b_p[t.p], ident).then_inc(b_pTp.sem, 1)

            def b_y_(t):
                wait(pe, b_pTc, t, 2)
                wait(pe, b_vc, t, 1)
                wait(pe, b_y, t, 1, back=1)
                if t.peeled and t.b == 0:
                    wait_end(pe, a_div)
                pe.matmul(bank[5][:, 0:D], b_pT[t.p], b_v[t.p], start=True, stop=True).then_inc(b_yp.sem, 1)

            pipelined(pe, [(b_pT_, 3), (b_s_, 2), (turn_x(B_), 0), (b_q_, 1), (b_v_, 2), (b_y_, 3)])

            def c_w_(t):
                wait(pe, xt_done.again(XT[C_]), t, 1)
                wait(pe, c_wc, t, 1, back=1)
                if t.peeled and t.b == 0:
                    pe.wait_ge(c_prep, 4)
                    wait_end(pe, b_qc)
                product(bank[1][:, 0:P], [c_rw[:, k, :] for k in range(KC)],
                        [xT[t.p][:, k, :] for k in range(KC)]).then_inc(c_wp.sem, 1)

            pipelined(pe, [(turn_x(C_), 0), (c_w_, 1)])

            def c_gather_(g):
                def stage(t):
                    first, last = t.peeled and t.b == TSEQ * g, t.peeled and t.b == TSEQ * (g + 1) - 1
                    if first:
                        wait_end(pe, b_y)
                        wait_end(pe, a_ob)
                    m = 3 if not t.peeled else min(t.b, 3)
                    wait(pe, c_hot, t, 1)
                    wait(pe, c_Uc, t, 1, back=1)
                    pe.matmul(bank[3][:, 0:S], c_mask[:, m, :], c_E[t.p][:, 0:S], start=True, stop=True)\
                      .then_inc(c_Up.sem, 1)
                    wait(pe, c_ETc, t, 1, back=1)
                    pe.transpose(bank[5][0:S, 0:P], c_E[t.p][:, 0:S], ident).then_inc(c_ETp.sem, 1)
                    pe.matmul(bank[2 + 4 * g][0:S, 0:XW], c_E[t.p][:, 0:S], X[:, t.b, :],
                              start=first, stop=last).then_inc(c_gp.sem, 1)
                return stage

            def c_masks_(g):
                def stage(t):
                    first, last = t.peeled and t.b == TSEQ * g, t.peeled and t.b == TSEQ * (g + 1) - 1
                    wait(pe, c_Uc, t, 1)
                    pe.matmul(bank[4 + 3 * g][0:S, 0:S], c_U[t.p][:, 0:S], c_E[t.p][:, 0:S],
                              start=first, stop=last).then_inc(c_mp.sem, 1)
                return stage

            for g in range(TILES):
                pipelined(pe, [(c_masks_(g), 2), (c_gather_(g), 1)], TSEQ * g, TSEQ * (g + 1), peel=4)

            pe.wait_ge(l_cw, 96)
            tiles = [(g, turn(g)) for g in range(TILES)]
            for g, t in tiles:
                pe.wait_ge(c_dve, dve_at(1, g))
                if g == 0:
                    wait_end(pe, xt_done.again(XT[C_]))
                    wait_end(pe, c_wc)
                for k in range(KC):
                    m = pe.transpose(bank[g][:, k * S:(k + 1) * S], c_hn[g][0:S, k * P:(k + 1) * P], ident[0:S, 0:S])
                m.then_inc(c_pe, 1)
            for g, t in tiles:
                pe.wait_ge(c_act, act_at(1, g))
                if g == 0:
                    pe.wait_ge(c_dve, dve_at(0, 1))
                    wait_end(pe, c_Uc)
                    wait_end(pe, c_ETc)
                lhs = [c_hT[:, k, g * S:(g + 1) * S] for k in range(KC)]
                product(bank[2 + g][0:S, 0:2 * D], lhs, [c_wqkv[:, k, 0:2 * D] for k in range(KC)])\
                    .then_inc(c_pe, 1)
            for g, t in tiles:
                lhs = [c_hT[:, k, g * S:(g + 1) * S] for k in range(KC)]
                product(bank[4 + g][0:S, 0:D], lhs, [c_wqkv[:, k, 2 * D:3 * D] for k in range(KC)])\
                    .then_inc(c_pe, 1)
            for g, t in tiles:
                pe.wait_ge(c_dve, dve_at(4, g))
                for k in range(2 * KC):
                    m = pe.transpose(bank[6 + g][:, k * S:(k + 1) * S], c_z[g][0:S, k * P:(k + 1) * P], ident[0:S, 0:S])
                m.then_inc(c_pe, 1)
            for g, t in tiles:
                pe.wait_ge(c_act, act_at(3, g))
                pe.wait_ge(c_dve, keys_at(g))
                if g == 0:
                    pe.wait_ge(c_dve, dve_at(3, 1))
                    pe.wait_ge(c_act, act_at(2, 1))
                else:
                    pe.wait_ge(c_act, act_at(3, 1))
                for r in range(NQ):
                    m = pe.matmul(bank[4 * g + r][0:S, 0:QH * S], c_qT[g][:, r // 2, :],
                                  c_kexp[:, QH * r:QH * (r + 1), :].rearrange("p a b -> p (a b)"),
                                  start=True, stop=True)
                m.then_inc(c_pe, 1)
            for g, t in tiles:
                pe.wait_ge(c_act, act_at(4, g))
                for r in range(NQ):
                    for i in range(QH):
                        m = pe.transpose(bank[4 * g + r][0:S, i * S:(i + 1) * S], c_S[g][0:S, QH * r + i, :],
                                         ident[0:S, 0:S])
                m.then_inc(c_pe, 1)
            for g, t in tiles:
                pe.wait_ge(c_act, act_at(5, g))
                for h in range(H):
                    m = pe.matmul(bank[4 * g][0:S, h * HV:(h + 1) * HV], c_pT[g][0:S, h, :], c_v[g][0:S, h, :],
                                  start=True, stop=True)
                m.then_inc(c_pe, 1)
            for g, t in tiles:
                pe.wait_ge(c_dve, dve_at(10, g))
                for k in range(KC):
                    m = pe.transpose(bank[4 * g + 1][:, k * S:(k + 1) * S], c_at[g][0:S, k * P:(k + 1) * P],
                                     ident[0:S, 0:S])
                m.then_inc(c_pe, 1)
            for g, t in tiles:
                pe.wait_ge(c_act, act_at(6, g))
                product(bank[4 * g + 2][0:S, 0:D], [c_oT[g][:, k, :] for k in range(KC)],
                        [c_wo[:, k, :] for k in range(KC)]).then_inc(c_pe, 1)
            for g, t in tiles:
                pe.wait_ge(c_dve, dve_at(12, g))
                for k in range(KC):
                    m = pe.transpose(bank[4 * g + 3][:, k * S:(k + 1) * S], c_hn[g][0:S, k * P:(k + 1) * P],
                                     ident[0:S, 0:S])
                m.then_inc(c_pe, 1)
            pe.wait_ge(c_act, act_at(8, 1))
            for q in range(FC // 2):
                o = bank[(0, 1, 4, 5)[q]]
                for i in range(2):
                    f = 2 * q + i
                    m = product(o[:, i * TILES * S:(i + 1) * TILES * S],
                                [c_w1[:, k, f * P:(f + 1) * P] for k in range(KC)],
                                [c_hT[:, k, :] for k in range(KC)])
                m.then_inc(c_fp.sem, 1)
            wait_end(pe, c_gelu)
            for g, t in tiles:
                product(bank[4 * g + 2][0:S, 0:D], [c_gT[:, f, g * S:(g + 1) * S] for f in range(FC)],
                        [c_w2[:, f, :] for f in range(FC)]).then_inc(c_pe, 1)

            def c_scatter_(g):
                def stage(t):
                    wait(pe, c_etsc, t, 1)
                    wait(pe, c_y, t, 1, back=2)
                    if t.peeled and t.b == TSEQ * g:
                        pe.wait_ge(c_dve, dve_at(14, 1))
                    pe.matmul(bank[t.p][:, 0:D], c_ets[t.p][0:S], c_proc[0:S, g, :], start=True, stop=True)\
                      .then_inc(c_sp.sem, 1)
                return stage

            for g in range(TILES):
                pipelined(pe, [(c_scatter_(g), 0)], TSEQ * g, TSEQ * (g + 1), peel=2)

            for n, round in enumerate((D_, E_)):
                w = d_w[n]
                wq, wk, wv, wo = (w[:, :, i * D:(i + 1) * D] for i in range(4))
                pe.wait_ge(l_dw[n], 16 if n == 0 else 32)

                def bank0_free(t, n=n):
                    if n == 0 and t.b == 0:
                        wait_end(pe, c_y)

                def d_turn_(t, n=n, round=round):
                    if t.peeled and t.b < 4:
                        if n == 1:
                            wait_end(pe, d_atc.again(0))
                    else:
                        wait(pe, d_atc.again(n), t, 1, back=4)
                    turn_x(round, bank0_free)(t)

                def d_proj_(t, n=n, round=round):
                    wait(pe, xt_done.again(XT[round]), t, 1)
                    wait(pe, d_qkc.again(n), t, 4, back=1)
                    x_ = xT[t.p]
                    src = x_ if n == 0 else inT[t.p]
                    for k in range(KC):
                        product(bank[1][:, k * P:(k + 1) * P], [wq[:, j, k * P:(k + 1) * P] for j in range(KC)],
                                [x_[:, j, :] for j in range(KC)])
                    if n == 1:
                        pe.wait_ge(l_inT[t.p], 16 * (2 * (B // 2) + t.half + 1))
                    for k in range(KC):
                        m = product(bank[1][:, D + k * P:D + (k + 1) * P],
                                    [wk[:, j, k * P:(k + 1) * P] for j in range(KC)],
                                    [src[:, j, :] for j in range(KC)])
                    m.then_inc(d_qkp.sem, 1)

                def d_v_(t, n=n):
                    src = xT[t.p] if n == 0 else inT[t.p]
                    wait(pe, d_vc.again(n), t, 1, back=1)
                    if t.peeled and t.b < 3:
                        if n == 1:
                            wait_end(pe, d_y.again(0))
                    else:
                        wait(pe, d_y.again(n), t, 1, back=3)
                    product(bank[2][:, 0:D], [src[:, j, :] for j in range(KC)],
                            [wv[:, j, :] for j in range(KC)]).then_inc(d_vp.sem, 1)

                def d_scores_(r, n=n):
                    def stage(t):
                        if r % 2 == 0:
                            wait(pe, d_qkc.again(n), t, KC + r // 2 + 1)
                            wait(pe, d_kx.again(n), t, r // 2 + 1)
                        if r < 2:
                            wait(pe, d_max.again(n), t, 2 * (NQ + r - 1), back=1)
                        else:
                            wait(pe, d_max.again(n), t, 2 * (r - 1))
                        o = bank[3 + r % 2]
                        m = pe.matmul(o[:], d_qT[t.p][:, r // 2, :],
                                      d_kexp[t.p][:, QH * r:QH * (r + 1), :].rearrange("p a b -> p (a b)"),
                                      start=True, stop=n == 0)
                        if n == 1:
                            for i in range(QH):
                                m = pe.matmul(o[:, i * P:(i + 1) * P], ident_bf[:], causal_bf[:],
                                              start=False, stop=i == QH - 1)
                        m.then_inc(d_sp.sem, 1)
                    return stage

                def d_pT_(r, n=n):
                    def stage(t):
                        wait(pe, d_exp.again(n), t, r + 1)
                        if r < 2:
                            wait(pe, d_pTc.again(n), t, NQ + r - 1, back=1)
                        else:
                            wait(pe, d_pTc.again(n), t, r - 1)
                        for i in range(QH):
                            m = pe.transpose(bank[5 + r % 2][:, i * P:(i + 1) * P], d_S[t.p][:, QH * r + i, :], ident)
                        m.then_inc(d_pTp.sem, 1)
                    return stage

                def d_pv_(t, n=n):
                    wait(pe, d_pTc.again(n), t, NQ)
                    wait(pe, d_vc.again(n), t, 1)
                    wait(pe, d_div.again(n), t, 2, back=1)
                    for h in range(H):
                        m = pe.matmul(bank[7][:, h * HV:(h + 1) * HV], d_pT[t.p][:, h, :], d_v[t.p][:, h, :],
                                      start=True, stop=True)
                    m.then_inc(d_pv.sem, 1)

                def d_atp_(t, n=n, round=round):
                    wait(pe, d_div.again(n), t, 2)
                    wait(pe, d_atc.again(n), t, 1, back=1)
                    if t.peeled and t.b + 3 >= B:
                        wait_end(pe, xt_done.again(XT[round]))
                    else:
                        wait(pe, xt_done.again(XT[round]), Turn(t.b + 3, 0, 0), 1)
                    transposes(bank[0][:, D:2 * D], lambda k: d_at[t.p][:, k * P:(k + 1) * P], KC, P)\
                        .then_inc(d_atp.sem, 1)

                def d_out_(t, n=n):
                    wait(pe, d_atc.again(n), t, 1)
                    wait(pe, d_y.again(n), t, 1, back=1)
                    if t.peeled and t.b + 2 >= B:
                        wait_end(pe, d_vc.again(n))
                    else:
                        wait(pe, d_vc.again(n), Turn(t.b + 2, 0, 0), 1)
                    product(bank[2][:, D:2 * D], [d_atT[t.p][:, k, :] for k in range(KC)],
                            [wo[:, k, :] for k in range(KC)]).then_inc(d_op.sem, 1)

                pipelined(pe, [(d_scores_(0), 2), (d_scores_(1), 2), (d_pv_, 3), (d_turn_, 0), (d_proj_, 1),
                               (d_scores_(2), 2), (d_pT_(0), 2), (d_atp_, 3), (d_v_, 1), (d_scores_(3), 2),
                               (d_pT_(1), 2), (d_out_, 3), (d_pT_(2), 2), (d_pT_(3), 2)])

            def f_lg_(t):
                wait(pe, xt_done.again(XT[F_]), t, 1)
                wait(pe, f_lc, t, 1, back=1)
                product(bank[1][:, 0:E], [xT[t.p][:, k, :] for k in range(KC)],
                        [f_rw[:, k, :] for k in range(KC)]).then_inc(f_lp.sem, 1)

            def f_turn_(t):
                if t.peeled and t.b == 0:
                    wait_end(pe, d_atc.again(1))
                turn_x(F_)(t)

            pipelined(pe, [(f_turn_, 0), (f_lg_, 1)])
            wait_end(pe, f_xtc)
            wait_end(pe, f_lc)
            wait_end(pe, d_y.again(1))

            def f_up(m, p, g, load):
                if g == 0:
                    pe.wait_ge(l_ew[p], load)
                w = f_ws[p]
                for c_ in range(KC):
                    for i in range(2):
                        o = bank[2 * i + c_]
                        wait(pe, f_silu if i == 0 else f_mul, m, c_ + 1, back=1)
                        for k in range(KC):
                            mm = pe.matmul(o[:], w[:, i * KC + k, c_ * P:(c_ + 1) * P],
                                           f_XT[:, k, g * GT:(g + 1) * GT], start=k == 0, stop=k == KC - 1)
                        mm.then_inc(f_hp.sem, 1)

            def f_down(m, p):
                w = f_ws[p]
                for q in range(2):
                    wait(pe, f_mul, m, 2)
                    wait(pe, f_acc, m, 2 * q + 2, back=2)
                    for i in range(2):
                        s0 = (2 * q + i) * P
                        mm = product(bank[4 + 2 * m.p + q][:, i * D:(i + 1) * D],
                                     [f_a[m.p][:, k, s0:s0 + P] for k in range(KC)],
                                     [w[:, 2 * KC + k, :] for k in range(KC)])
                    mm.then_inc(f_dp.sem, 1)

            def pair(j):
                for i in range(2 * G):
                    g, p = i % G, i // G
                    f_up(Turn(2 * G * j + i, i % 2, 0), p, g, 16 * (j + 1))
                    if i or not isinstance(j, int):
                        f_down(Turn(2 * G * j + i - 1, (i - 1) % 2, 0), (i - 1) // G % 2)

            pair(0)
            with pe.Fori(1, NE // 2) as j:
                pair(j)
            f_down(turn(MT - 1), 1)

        @block.scalar
        def _(act):
            act.dma_start(a_w, a["a_w"]).then_inc(l_aw, 16)
            act.dma_start(rows[:], a["rows"].partition_broadcast(P)).then_inc(l_rows, 16)
            act.dma_start(cols[:], a["cols"]).then_inc(l_rows, 16)
            act.dma_start(a_wout, a["a_wout"]).then_inc(l_aw, 16)

            def copy_xT(round, before, reader):
                xd = xt_done.again(XT[round])
                def stage(t):
                    wait(act, turned.again(XT[round]), t, 1)
                    if t.peeled and t.b < 2:
                        if before is not None:
                            wait_end(act, before)
                    else:
                        wait(act, reader, t, 1, back=2)
                    if round == F_:
                        wait(act, f_xtc, t, 1, back=2)
                    act.copy(xT[t.p][:], bank[0][:, 0:D].rearrange("p (k t) -> p k t", k=KC)).then_inc(xd.sem, 1)
                return stage

            def a_sq_(t):
                wait(act, a_qkb, t, 1)
                wait(act, a_rms, t, 2, back=2)
                for i in range(2):
                    act.activation(a_sqs[t.p][:, i, :], a_qk[t.p][:, i * D:(i + 1) * D], ACT.Square, scale=D ** -0.5,
                                   accum_out=a_ms[t.p][:, i:i + 1]).then_inc(a_sq.sem, 1)

            def a_relu_(t):
                wait(act, a_rope, t, 1)
                wait(act, a_rms, t, 2)
                wait(act, a_kvp, t, 1, back=2)
                wait(act, a_fTp, t, 1, back=2)
                for i in range(2):
                    act.activation(a_f[t.p][:, i * D:(i + 1) * D], a_u[t.p][:, i * D:(i + 1) * D], ACT.Relu,
                                   scale=a_r[t.p][:, i:i + 1]).then_inc(a_relu.sem, 1)

            def a_fTc_(t):
                wait(act, a_fTp, t, 1)
                wait(act, a_nd, t, 1, back=2)
                act.copy(a_fT[t.p], bank[4][:, 0:D].rearrange("p (k t) -> p k t", k=KC)).then_inc(a_fTc.sem, 1)

            def a_atc_(t):
                wait(act, a_atp, t, 1)
                wait(act, a_op, t, 1, back=2)
                act.copy(a_atT[t.p], bank[6][:, 0:D].rearrange("p (k t) -> p k t", k=KC)).then_inc(a_atc.sem, 1)

            def a_osq_(t):
                wait(act, a_ob, t, 1)
                wait(act, a_orms, t, 1, back=2)
                act.activation(a_sqs[t.p][:, 2, :], a_o[t.p], ACT.Square, scale=D ** -0.5, accum_out=a_oms[t.p]).then_inc(a_osq.sem, 1)

            pipelined(act, [(a_osq_, 5), (a_fTc_, 3), (a_sq_, 1), (a_relu_, 2), (a_atc_, 4)])

            act.wait_ge(b_fold.sem, 1)
            act.mul(b_A, bank[1][:].rearrange("p (k n) -> p k n", k=KC), SCALE).then_inc(b_folded.sem, 1)
            act.wait_ge(b_fold.sem, 2)
            act.copy(b_B, bank[2][:].rearrange("p (k n) -> p k n", k=KC)).then_inc(b_folded.sem, 1)

            def b_qc_(t):
                wait(act, b_qp, t, 1)
                wait(act, b_sp, t, 1, back=2)
                act.copy(b_qT[t.p], bank[1][:, 0:D].rearrange("p (k t) -> p k t", k=KC)).then_inc(b_qc.sem, 1)

            def b_exp_(t):
                wait(act, b_max, t, 1)
                wait(act, b_pTp, t, 1, back=2)
                wait(act, b_pTc, t, 1, back=2)
                act.activation(b_p[t.p], b_s[t.p], ACT.Exp, bias=b_nmax[t.p], scale=-1.0,
                               accum_out=b_sum[t.p]).then_inc(b_exp.sem, 1)

            pipelined(act, [(copy_xT(B_, None, b_qp), 0), (b_qc_, 1), (b_exp_, 2)])

            def c_U_(t):
                wait(act, c_Up, t, 1)
                wait(act, c_mp, t, 1, back=2)
                act.copy(c_U[t.p][:, 0:S], bank[3][:, 0:S]).then_inc(c_Uc.sem, 1)
                wait(act, c_ETp, t, 1)
                act.copy(c_ET[0:S, t.b, :], bank[5][0:S, 0:P]).then_inc(c_ETc.sem, 1)

            def c_wc_(t):
                wait(act, c_wp, t, 1)
                wait(act, c_cnt, t, 4, back=2)
                act.activation(c_wr[t.p], bank[1][:, 0:P], ACT.Identity, bias=row("router_b")).then_inc(c_wc.sem, 1)

            pipelined(act, [(copy_xT(C_, b_qp, c_wp), 0), (c_wc_, 1)])
            pipelined(act, [(c_U_, 0)])

            tiles = range(TILES)
            for g in tiles:
                act.wait_ge(c_dve, dve_at(0, g))
                act.activation(c_sqs[g][0:S, 0, :], c_sel[g][0:S, 0:D], ACT.Square, scale=D ** -0.5, accum_out=c_st[g][0:S, 0:1])\
                   .then_inc(c_act, 1)
            for g in tiles:
                act.wait_ge(c_pe, TILES * 0 + g + 1)
                act.copy(c_hT[:, :, g * S:(g + 1) * S], bank[g][:, 0:KC * S].rearrange("p (k t) -> p k t", k=KC))\
                   .then_inc(c_act, 1)
            for g in tiles:
                act.wait_ge(c_dve, dve_at(2, g))
                act.activation(c_cs[g][0:S, 0:2, :], c_arg[g][0:S], ACT.Sin)
                act.wait_ge(c_pe, TILES * 2 + g + 1)
                act.copy(c_v[g][0:S, :, 0:HD], bank[4 + g][0:S, 0:D].rearrange("p (h d) -> p h d", h=H))\
                   .then_inc(c_act, 1)
            for g in tiles:
                act.wait_ge(c_pe, TILES * 3 + g + 1)
                act.mul(c_qT[g], bank[6 + g][:, 0:KC * S].rearrange("p (k t) -> p k t", k=KC), SCALE)\
                   .then_inc(c_act, 1)
            for g in tiles:
                act.wait_ge(c_dve, dve_at(9, g))
                act.activation(c_S[g][0:S], c_S[g][0:S], ACT.Exp).then_inc(c_act, 1)
            for g in tiles:
                act.wait_ge(c_pe, TILES * 5 + g + 1)
                for r in range(NQ):
                    m = act.copy(c_pT[g][0:S, QH * r:QH * (r + 1), :],
                                 bank[4 * g + r][0:S, 0:QH * S].rearrange("p (a b) -> p a b", a=QH))
                m.then_inc(c_act, 1)
            for g in tiles:
                act.wait_ge(c_pe, TILES * 7 + g + 1)
                act.copy(c_oT[g], bank[4 * g + 1][:, 0:KC * S].rearrange("p (k t) -> p k t", k=KC))\
                   .then_inc(c_act, 1)
            for g in tiles:
                act.wait_ge(c_dve, dve_at(11, g))
                act.activation(c_sqs[g][0:S, 1, :], c_x1[g][0:S], ACT.Square, scale=D ** -0.5, accum_out=c_st[g][0:S, 2:3])\
                   .then_inc(c_act, 1)
            for g in tiles:
                act.wait_ge(c_pe, TILES * 9 + g + 1)
                act.copy(c_hT[:, :, g * S:(g + 1) * S],
                         bank[4 * g + 3][:, 0:KC * S].rearrange("p (k t) -> p k t", k=KC)).then_inc(c_act, 1)
            for q in range(FC // 2):
                act.wait_ge(c_fp.sem, q + 1)
                act.activation(c_gT[:, 2 * q:2 * q + 2, :],
                               bank[(0, 1, 4, 5)[q]][:, 0:2 * TILES * S].rearrange("p (a b) -> p a b", a=2),
                               ACT.Gelu_apprx_tanh).then_inc(c_gelu.sem, 1)

            act.wait_ge(d_prep, 3)
            for n, round in enumerate((D_, E_)):
                def d_qkc_(t, n=n):
                    qk = d_qkc.again(n)
                    wait(act, d_qkp.again(n), t, 1)
                    wait(act, d_sp.again(n), t, NQ, back=2)
                    wait(act, d_kx.again(n), t, 2, back=2)
                    for k in range(KC):
                        act.activation(d_kT[t.p][:, k, :], bank[1][:, D + k * P:D + (k + 1) * P], ACT.Identity,
                                       bias=cols[:, KC + k:KC + k + 1] if n == 0 else 0.0).then_inc(qk.sem, 1)
                    for k in range(KC):
                        act.activation(d_qT[t.p][:, k, :], bank[1][:, k * P:(k + 1) * P], ACT.Identity, scale=SCALE,
                                       bias=d_bq[:, k:k + 1] if n == 0 else 0.0).then_inc(qk.sem, 1)

                def d_exp_(r, n=n):
                    def stage(t):
                        wait(act, d_max.again(n), t, 2 * r + 2)
                        v = d_S[t.p][:, QH * r:QH * (r + 1), :]
                        act.activation(v, v, ACT.Exp).then_inc(d_exp.sem, 1)
                    return stage

                def d_pTc_(r, n=n):
                    def stage(t):
                        wait(act, d_pTp.again(n), t, r + 1)
                        wait(act, d_pv.again(n), t, 1, back=2)
                        act.copy(d_pT[t.p][:, QH * r:QH * (r + 1), :],
                                 bank[5 + r % 2][:].rearrange("p (a b) -> p a b", a=QH)).then_inc(d_pTc.sem, 1)
                    return stage

                def d_atc_(t, n=n):
                    wait(act, d_atp.again(n), t, 1)
                    wait(act, d_op.again(n), t, 1, back=2)
                    act.copy(d_atT[t.p], bank[0][:, D:2 * D].rearrange("p (k t) -> p k t", k=KC))\
                       .then_inc(d_atc.sem, 1)

                reader = d_vp.again(n) if n == 0 else d_qkp.again(n)
                before = c_wp if n == 0 else d_vp.again(0)
                pipelined(act, [(d_exp_(0), 2), (d_exp_(1), 2), (copy_xT(round, before, reader), 0), (d_qkc_, 1),
                                (d_pTc_(0), 2), (d_atc_, 3), (d_exp_(2), 2), (d_pTc_(1), 2), (d_exp_(3), 2),
                                (d_pTc_(2), 2), (d_pTc_(3), 2)])

            pipelined(act, [(copy_xT(F_, d_qkp.again(1), f_lp), 0)])
            wait_end(act, f_lc)
            act.activation(f_sc, f_lg, ACT.Sigmoid).then_inc(f_sig, 1)

            def f_silu_(m):
                for c_ in range(KC):
                    wait(act, f_hp, m, 2 * c_ + 1)
                    wait(act, f_mul, m, c_ + 1, back=1)
                    act.activation(f_h[c_], bank[c_][:], ACT.Silu).then_inc(f_silu.sem, 1)

            for m in range(G):
                f_silu_(turn(m))
            with act.Fori(1, NE) as e:
                for g in range(G):
                    f_silu_(Turn(G * e + g, g % 2, 0))

        @block.vector
        def _(dve):
            def ln_stats(round):
                st = stats.again(round)
                def stage(t):
                    wait(dve, rstd.again(round), t, 1, back=2)
                    dve.bn_stats(bn[t.p][:], y[t.p][:]).then_inc(st.sem, 1)
                    wait(dve, st, t, 1)
                    hold(dve)
                    dve.bn_aggr(mv[t.p][:], bn[t.p][:]).then_inc(st.sem, 1)
                return stage

            def ln_final(round, to=None):
                nd = normed.again(round)
                def stage(t):
                    wait(dve, rstd.again(round), t, 2)
                    o = X[:, t.b, 0:D] if to is None else to(t)
                    dve.tensor_scalar(o, y[t.p][:], mv[t.p][:, 0:1], lr[t.p][:, 1:2], ALU.subtract, ALU.mult)\
                       .then_inc(nd.sem, 1)
                return stage

            for i in range(2):
                dve.memset(a_v[i][:, :, P:VW], 1.0)
            dve.wait_ge(l_const, 16)
            dve.tensor_copy(ident_bf[:], ident)
            dve.tensor_copy(causal_bf[:], c("causal"))
            dve.wait_ge(l_rows, 32)
            for i, gain in enumerate(("gq", "gk")):
                sl = slice(i * D, (i + 1) * D)
                dve.tensor_tensor(a_cos[:, sl], c("cos"), row(gain), ALU.mult).then_inc(a_tab, 1)
                pairs = lambda v: v.rearrange("p (n two) -> p n two", two=2)
                for z in range(2):
                    dve.tensor_tensor(pairs(a_sin[:, sl])[:, :, z], pairs(c("sin"))[:, :, z],
                                      pairs(row(gain))[:, :, 1 - z], ALU.mult).then_inc(a_tab, 1)
            dve.wait_ge(a_tab, 6)

            def a_qkb_(t):
                wait(dve, a_qkp, t, 1)
                wait(dve, a_swap, t, 2, back=2)
                wait(dve, a_sq, t, 2, back=2)
                wait(dve, a_turn, t, 1, back=2)
                dve.tensor_tensor(a_qk[t.p], bank[1][:], row("bqkv")[:, 0:2 * D], ALU.add).then_inc(a_qkb.sem, 1)

            def a_vb_(t):
                wait(dve, a_vp, t, 1)
                wait(dve, a_kvp, t, 1, back=2)
                dve.tensor_tensor(a_v[t.p][:, :, 0:P], bank[2][:, 0:D].rearrange("p (k n) -> p k n", k=KC),
                                  row("bqkv")[:, 2 * D:3 * D].rearrange("p (k n) -> p k n", k=KC), ALU.add)\
                   .then_inc(a_vb.sem, 1)

            def a_turn_(t):
                wait(dve, a_qkb, t, 1)
                wait(dve, a_relu, t, 2, back=2)
                dve.tensor_tensor(a_u[t.p], a_qk[t.p], a_cos, ALU.mult).then_inc(a_turn.sem, 1)

            def a_rope_(t):
                wait(dve, a_turn, t, 1)
                wait(dve, a_swap, t, 2)
                dve.tensor_tensor(a_u[t.p], a_u[t.p], a_sw[t.p], ALU.add).then_inc(a_rope.sem, 1)

            def a_kvm_(t):
                wait(dve, a_kvp, t, 1)
                wait(dve, a_nd, t, 1, back=2)
                kv = bank[3][:, 0:KC * VW].rearrange("p (k n) -> p k n", k=KC)
                dve.tensor_tensor(a_kv[t.p][:, :, 0:P], kv[:, :, 0:P],
                                  c("blocks").unsqueeze(1).to_broadcast([P, KC, P]), ALU.mult).then_inc(a_kvm.sem, 1)
                dve.tensor_tensor(a_kv[t.p][:, :, P:NW], kv[:, :, P:P + 1].to_broadcast([P, KC, HH]),
                                  c("heads").unsqueeze(1).to_broadcast([P, KC, HH]), ALU.mult).then_inc(a_kvm.sem, 1)

            def a_div_(t):
                wait(dve, a_nd, t, 1)
                wait(dve, a_atp, t, 1, back=2)
                nd = bank[5][:, 0:KC * NW].rearrange("p (k n) -> p k n", k=KC)
                dve.tensor_scalar(a_den[t.p], nd[:, :, P:NW], LIN_EPS, None, ALU.add).then_inc(a_div.sem, 1)
                wait(dve, a_div, t, 1)
                dve.reciprocal(a_rden[t.p], a_den[t.p]).then_inc(a_div.sem, 1)
                wait(dve, a_div, t, 2)
                dve.tensor_tensor(a_at[t.p].rearrange("p (k h d) -> p k h d", k=KC, h=HH),
                                  nd[:, :, 0:P].rearrange("p k (h d) -> p k h d", h=HH),
                                  a_rden[t.p].unsqueeze(3).to_broadcast([P, KC, HH, HD]), ALU.mult)\
                   .then_inc(a_div.sem, 1)

            def a_ob_(t):
                wait(dve, a_op, t, 1)
                wait(dve, a_osq, t, 1, back=2)
                wait(dve, a_y, t, 1, back=2)
                dve.tensor_tensor(a_o[t.p], bank[7][:, 0:D], row("bout"), ALU.add).then_inc(a_ob.sem, 1)

            def a_y_(t):
                if t.peeled and t.b == 0:
                    dve.wait_ge(l_x, 16)
                wait(dve, a_orms, t, 2)
                wait(dve, normed, t, 1, back=2)
                dve.scalar_tensor_tensor(out=y[t.p][:], in0=a_o[t.p], scalar=a_or[t.p][:, 1:2], in1=row("gout"),
                                         op0=ALU.mult, op1=ALU.mult).then_inc(a_y.sem, 1)
                wait(dve, a_y, t, 1)
                dve.tensor_tensor(y[t.p][:], y[t.p][:], X[:, t.b, 0:D], ALU.add).then_inc(a_y.sem, 1)
                wait(dve, a_y, t, 2)
                ln_stats(A_)(t)

            pipelined(dve, [(a_ob_, 5), (a_div_, 4), (a_kvm_, 3), (ln_final(A_), 6), (a_rope_, 2), (a_turn_, 1),
                            (a_qkb_, 0), (a_vb_, 1), (a_y_, 5)])

            def b_vc_(t):
                wait(dve, b_vp, t, 1)
                wait(dve, b_yp, t, 1, back=2)
                dve.tensor_copy(b_v[t.p], bank[2][:, 0:D]).then_inc(b_vc.sem, 1)

            def b_max_(t):
                wait(dve, b_sp, t, 1)
                wait(dve, b_exp, t, 1, back=2)
                hold(dve)
                dve.tensor_tensor_reduce(b_s[t.p], bank[3][:, 0:P], c("causal"), -1.0, BIG, ALU.add, ALU.min,
                                         b_nmax[t.p]).then_inc(b_max.sem, 1)

            def b_pTc_(t):
                wait(dve, b_exp, t, 1)
                wait(dve, b_y, t, 1, back=2)
                dve.reciprocal(b_rsum[t.p], b_sum[t.p]).then_inc(b_pTc.sem, 1)
                wait(dve, b_pTp, t, 1)
                wait(dve, b_yp, t, 1, back=2)
                dve.tensor_copy(b_pT[t.p], bank[4][:, 0:P]).then_inc(b_pTc.sem, 1)

            def b_y_(t):
                wait(dve, b_yp, t, 1)
                wait(dve, b_pTc, t, 1)
                wait(dve, normed.again(B_), t, 1, back=2)
                dve.scalar_tensor_tensor(out=y[t.p][:], in0=bank[5][:, 0:D], scalar=b_rsum[t.p],
                                         in1=X[:, t.b, 0:D], op0=ALU.mult, op1=ALU.add).then_inc(b_y.sem, 1)
                wait(dve, b_y, t, 1)
                ln_stats(B_)(t)

            pipelined(dve, [(b_y_, 4), (b_pTc_, 3), (b_max_, 2), (ln_final(B_), 4), (b_vc_, 2)])

            dve.wait_ge(l_cw, 96)
            dve.tensor_copy(c_rw, cols[:, COLS["router_w"]].unsqueeze(2).to_broadcast([P, KC, P])).then_inc(c_prep, 1)
            dve.tensor_scalar(c_mask, c_mask, NEG, None, ALU.max).then_inc(c_prep, 1)
            dve.tensor_copy(X[:, 0:3, D + 1:D + 2], c_posi.bitcast(I32)[:, 0:3].unsqueeze(2)).then_inc(c_prep, 1)
            dve.tensor_copy(X[:, 3:B, D + 1:D + 2],
                            c_posi.bitcast(I32)[:, 3:4].unsqueeze(2).to_broadcast([P, B - 3, 1])).then_inc(c_prep, 1)

            def c_cnt_(t):
                w = c_wr[t.p]
                col, gt, ge, tie = (c_small[t.p][:, i:i + 1] for i in range(4))
                wait(dve, c_wc, t, 1)
                wait(dve, c_kept, t, 1, back=2)
                dve.tensor_tensor_reduce(c_cmp[t.p][:, 0, :], w, ident, 1.0, 0.0, ALU.mult, ALU.add, col)\
                   .then_inc(c_cnt.sem, 1)
                wait(dve, c_cnt, t, 1)
                dve.tensor_scalar(c_cmp[t.p][:, 1, :], w, col, 0.0, ALU.is_gt, ALU.add,
                                  accum_out=gt).then_inc(c_cnt.sem, 1)
                dve.tensor_scalar(c_cmp[t.p][:, 2, :], w, col, 0.0, ALU.is_ge, ALU.add,
                                  accum_out=ge).then_inc(c_cnt.sem, 1)
                dve.scalar_tensor_tensor(out=c_cmp[t.p][:, 3, :], in0=w, scalar=col, in1=c("before"),
                                         op0=ALU.is_equal, op1=ALU.mult, accum_out=tie)\
                   .then_inc(c_cnt.sem, 1)

            pipelined(dve, [(c_cnt_, 0)])

            n_place = [0]

            def place(m):
                n_place[0] += 1
                m.then_inc(c_place, 1)
                dve.wait_ge(c_place, n_place[0])

            wait_end(dve, c_kept)
            c_col, c_gt, c_ge, c_tie = (c_counts[:, :, i] for i in range(4))
            place(dve.tensor_tensor(c_slot, c_gt, c_tie, ALU.add))
            place(dve.tensor_scalar(c_over, c_slot, SEL - 0.5, 1000.0, ALU.is_gt, ALU.mult))
            place(dve.tensor_tensor(c_slot, c_slot, c_over, ALU.add))
            place(dve.tensor_tensor(c_slot, c_slot, c("seqslot"), ALU.add))
            place(dve.tensor_scalar(keep1[:], c_ge, SEL + 0.5, 1.0, ALU.is_gt, ALU.add))
            place(dve.tensor_copy(X[:, :, D:D + 1], c_counts[:, :, 0:1]))

            def c_hot_(t):
                wait(dve, c_gp, t, 1, back=2)
                wait(dve, c_mp, t, 1, back=2)
                dve.tensor_scalar(c_E[t.p], c("slots"), c_slot[:, bass.ds(t.b, 1)], None, ALU.is_equal)\
                   .then_inc(c_hot.sem, 1)

            pipelined(dve, [(c_hot_, 0)])

            tiles = range(TILES)
            link = [0]

            def chain(m):
                link[0] += 1
                m.then_inc(c_link, 1)
                dve.wait_ge(c_link, link[0])

            def done(m):
                m.then_inc(c_dve, 1)

            for g in tiles:
                dve.memset(c_v[g][0:S, :, HD:HV], 1.0)
            for g in tiles:
                wait(dve, c_gp, turn(TSEQ * (g + 1) - 1), 1)
                chain(dve.tensor_copy(c_sel[g][0:S], bank[2 + 4 * g][0:S, 0:XW]))
                wait(dve, c_mp, turn(TSEQ * (g + 1) - 1), 1)
                done(dve.tensor_tensor(c_msk[g][0:S], bank[4 + 3 * g][0:S, 0:S], c("apart", S), ALU.add))
            for g in tiles:
                dve.wait_ge(c_pool, 2 * g + 2)
                done(dve.scalar_tensor_tensor(out=c_hn[g][0:S], in0=c_sel[g][0:S, 0:D], scalar=c_st[g][0:S, 4:5],
                                              in1=row("ln1", S), op0=ALU.mult, op1=ALU.mult))
            two_pi = [6.28125, 1.93500518798828125e-3, 3.0199159819e-7]
            for g in tiles:
                f, nf, r, r2, ov = (c_ang[g][0:S, i, :] for i in range(5))
                chain(dve.tensor_scalar(f, c("invfreq", S), c_sel[g][0:S, D + 1:D + 2], None, ALU.mult))
                chain(dve.tensor_scalar(nf, f, 1.0 / (2 * PI), MAGIC, ALU.mult, ALU.add))
                chain(dve.tensor_scalar(nf, nf, MAGIC, None, ALU.subtract))
                for part in two_pi:
                    chain(dve.scalar_tensor_tensor(out=f, in0=nf, scalar=-part, in1=f, op0=ALU.mult, op1=ALU.add))
                chain(dve.tensor_scalar(c_arg[g][0:S, 1, :], f, -PI, PI, ALU.max, ALU.min))
                chain(dve.tensor_scalar(r, f, PI / 2, None, ALU.add))
                chain(dve.tensor_scalar(ov, r, PI, -2 * PI, ALU.is_gt, ALU.mult))
                chain(dve.tensor_tensor(r, r, ov, ALU.add))
                done(dve.tensor_scalar(c_arg[g][0:S, 0, :], r, -PI, PI, ALU.max, ALU.min))
            for g in tiles:
                dve.wait_ge(c_pe, TILES * 1 + g + 1)
                done(dve.tensor_copy(c_x[g][0:S], bank[2 + g][0:S, 0:2 * D]))
            for g in tiles:
                dve.wait_ge(c_act, act_at(2, g))
                dve.wait_ge(c_dve, dve_at(3, g))
                x_ = c_x[g][0:S].rearrange("p (h z d) -> p h z d", z=2, d=8)
                z_ = c_z[g][0:S].rearrange("p (h z d) -> p h z d", z=2, d=8)
                cs = c_cs[g][0:S]
                bc = lambda v: v.unsqueeze(1).to_broadcast([S, 2 * H, 8])
                chain(dve.tensor_scalar(cs[:, 2, :], cs[:, 1, :], -1.0, None, ALU.mult))
                dve.tensor_tensor(z_[:, :, 0, :], x_[:, :, 1, :], bc(cs[:, 2, :]), ALU.mult)
                chain(dve.tensor_tensor(z_[:, :, 1, :], x_[:, :, 0, :], bc(cs[:, 1, :]), ALU.mult))
                dve.tensor_tensor(x_[:, :, 0, :], x_[:, :, 0, :], bc(cs[:, 0, :]), ALU.mult)
                chain(dve.tensor_tensor(x_[:, :, 1, :], x_[:, :, 1, :], bc(cs[:, 0, :]), ALU.mult))
                done(dve.tensor_tensor(c_z[g][0:S], c_z[g][0:S], c_x[g][0:S], ALU.add))
            for g in tiles:
                dve.wait_ge(c_act, act_at(3, g))
                if g:
                    dve.wait_ge(c_pe, TILES * 4 + g)
                for k in range(KC):
                    kT = bank[6 + g][:, (KC + k) * S:(KC + k + 1) * S]
                    done(dve.tensor_tensor(c_kexp[:, k * HH:(k + 1) * HH, :],
                                           kT.unsqueeze(1).to_broadcast([P, HH, S]),
                                           c("heads").unsqueeze(2).to_broadcast([P, HH, S]), ALU.mult))
            for g in tiles:
                dve.wait_ge(c_pe, TILES * 4 + g + 1)
                for r in range(NQ):
                    m = dve.tensor_tensor(c_S[g][0:S, QH * r:QH * (r + 1), :],
                                          bank[4 * g + r][0:S, 0:QH * S].rearrange("p (a b) -> p a b", a=QH),
                                          c_msk[g][0:S].unsqueeze(1).to_broadcast([S, QH, S]), ALU.add)
                done(m)
            for g in tiles:
                dve.wait_ge(c_dve, dve_at(7, g))
                done(dve.tensor_reduce(c_mx[g][0:S], c_S[g][0:S], AX.X, ALU.max))
            for g in tiles:
                dve.wait_ge(c_dve, dve_at(8, g))
                done(dve.tensor_tensor(c_S[g][0:S], c_S[g][0:S], c_mx[g][0:S].unsqueeze(2).to_broadcast([S, H, S]),
                                       ALU.subtract))
            for g in tiles:
                dve.wait_ge(c_pe, TILES * 6 + g + 1)
                o = bank[4 * g][0:S, 0:H * HV].rearrange("p (h d) -> p h d", h=H)
                chain(dve.reciprocal(c_rs[g][0:S], o[:, :, HD]))
                done(dve.tensor_tensor(c_at[g][0:S].rearrange("p (h d) -> p h d", h=H), o[:, :, 0:HD],
                                       c_rs[g][0:S].unsqueeze(2).to_broadcast([S, H, HD]), ALU.mult))
            for g in tiles:
                dve.wait_ge(c_pe, TILES * 8 + g + 1)
                done(dve.tensor_tensor(c_x1[g][0:S], bank[4 * g + 2][0:S, 0:D], c_sel[g][0:S, 0:D], ALU.add))
            for g in tiles:
                dve.wait_ge(c_pool, 2 * (TILES + g) + 2)
                done(dve.scalar_tensor_tensor(out=c_hn[g][0:S], in0=c_x1[g][0:S], scalar=c_st[g][0:S, 6:7],
                                              in1=row("ln2", S), op0=ALU.mult, op1=ALU.mult))
            for g in tiles:
                dve.wait_ge(c_pe, TILES * 10 + g + 1)
                done(dve.tensor_tensor(c_x1[g][0:S], bank[4 * g + 2][0:S, 0:D], c_x1[g][0:S], ALU.add))
            for g in tiles:
                dve.wait_ge(c_dve, dve_at(13, g))
                done(dve.tensor_scalar(c_proc[0:S, g, :], c_x1[g][0:S], c_sel[g][0:S, D:D + 1], None, ALU.mult))

            def c_y_(t):
                wait(dve, c_sp, t, 1)
                wait(dve, normed.again(C_), t, 1, back=2)
                dve.scalar_tensor_tensor(out=y[t.p][:], in0=X[:, t.b, 0:D],
                                         scalar=keep1[:, bass.ds(t.b, 1)],
                                         in1=bank[t.p][:, 0:D], op0=ALU.mult, op1=ALU.add).then_inc(c_y.sem, 1)
                wait(dve, c_y, t, 1)
                ln_stats(C_)(t)

            pipelined(dve, [(c_y_, 0), (ln_final(C_), 1)])

            dve.tensor_scalar(d_bq, cols[:, 0:KC], SCALE, None, ALU.mult).then_inc(d_prep, 1)
            for i in range(2):
                dve.memset(d_v[i][:, :, HD:HV], 1.0).then_inc(d_prep, 1)
            for n, round in enumerate((D_, E_)):
                def d_vc_(t, n=n):
                    wait(dve, d_vp.again(n), t, 1)
                    wait(dve, d_pv.again(n), t, 1, back=2)
                    o = d_v[t.p][:, :, 0:HD]
                    v = bank[2][:, 0:D].rearrange("p (h d) -> p h d", h=H)
                    if n == 0:
                        dve.tensor_tensor(o, v, row("bv").rearrange("p (h d) -> p h d", h=H), ALU.add)\
                           .then_inc(d_vc.sem, 1)
                    else:
                        dve.tensor_copy(o, v).then_inc(d_vc.sem, 1)

                def d_max_(r, n=n):
                    dm = d_max.again(n)
                    def stage(t):
                        wait(dve, d_sp.again(n), t, r + 1)
                        s_ = bank[3 + r % 2][:].rearrange("p (a b) -> p a b", a=QH)
                        mx = d_mx[t.p][:, QH * r:QH * (r + 1)]
                        dve.tensor_reduce(mx, s_, AX.X, ALU.max).then_inc(dm.sem, 1)
                        wait(dve, dm, t, 2 * r + 1)
                        wait(dve, d_pTp.again(n), t, NQ, back=2)
                        dve.tensor_tensor(d_S[t.p][:, QH * r:QH * (r + 1), :], s_,
                                          mx.unsqueeze(2).to_broadcast([P, QH, P]), ALU.subtract).then_inc(dm.sem, 1)
                    return stage

                def d_div_(t, n=n):
                    wait(dve, d_pv.again(n), t, 1)
                    wait(dve, d_atp.again(n), t, 1, back=2)
                    o = bank[7][:, 0:H * HV].rearrange("p (h d) -> p h d", h=H)
                    dve.reciprocal(d_rs[t.p], o[:, :, HD]).then_inc(d_div.sem, 1)
                    wait(dve, d_div.again(n), t, 1)
                    dve.tensor_tensor(d_at[t.p].rearrange("p (h d) -> p h d", h=H), o[:, :, 0:HD],
                                      d_rs[t.p].unsqueeze(2).to_broadcast([P, H, HD]), ALU.mult)\
                       .then_inc(d_div.sem, 1)

                def d_y_(t, n=n, round=round):
                    wait(dve, d_op.again(n), t, 1)
                    wait(dve, d_xbc.again(n), t, 1)
                    wait(dve, normed.again(round), t, 1, back=2)
                    dve.tensor_tensor(y[t.p][:], bank[2][:, D:2 * D], d_xb[t.p], ALU.add).then_inc(d_y.sem, 1)
                    wait(dve, d_y.again(n), t, 1)
                    ln_stats(round)(t)

                pipelined(dve, [(d_y_, 4), (d_max_(0), 2), (d_max_(1), 2), (d_div_, 3), (ln_final(round), 4),
                                (d_max_(2), 2), (d_vc_, 1), (d_max_(3), 2)])

            def f_lc_(t):
                wait(dve, f_lp, t, 1)
                dve.tensor_copy(f_lg[:, t.b, :], bank[1][:, 0:E]).then_inc(f_lc.sem, 1)

            pipelined(dve, [(f_lc_, 0)])
            n_route = [0]

            def route(m):
                n_route[0] += 1
                m.then_inc(f_route, 1)
                dve.wait_ge(f_route, n_route[0])

            dve.wait_ge(f_sig, 1)
            grp = lambda v: v.rearrange("p b (g e) -> p (b g) e", e=EPG)
            route(dve.tensor_tensor(f_s, f_sc, row("ebias").unsqueeze(1).to_broadcast([P, B, E]), ALU.add))
            s4 = grp(f_s)
            at = 0
            for d in range(1, EPG):
                m = dve.tensor_tensor(f_pair[:, :, at:at + EPG - d], s4[:, :, 0:EPG - d], s4[:, :, d:EPG], ALU.add)
                at += EPG - d
            route(m)
            gs = f_gs.rearrange("p b g -> p (b g)")
            route(dve.tensor_reduce(gs, f_pair, AX.X, ALU.max))
            def group_pair(first):
                return (f_gs.unsqueeze(2).to_broadcast([P, B, GROUPS, GROUPS]) if first else
                        f_gs.unsqueeze(3).to_broadcast([P, B, GROUPS, GROUPS]))
            c4 = lambda v: v.rearrange("p (b g) e -> p b g e", g=GROUPS)
            dve.tensor_tensor(c4(f_c1), group_pair(True), group_pair(False), ALU.is_gt)
            route(dve.tensor_tensor(c4(f_c2), group_pair(True), group_pair(False), ALU.is_equal))
            for g in range(GROUPS):
                m = dve.memset(c4(f_c2)[:, :, g, g:GROUPS], 0.0)
            route(m)
            route(dve.tensor_tensor(f_c1, f_c1, f_c2, ALU.add))
            gm = f_gm.rearrange("p b g -> p (b g)")
            route(dve.tensor_reduce(gm, f_c1, AX.X, ALU.add))
            route(dve.tensor_scalar(gm, gm, TOPG - 0.5, None, ALU.is_lt))
            route(dve.tensor_tensor(grp(f_v), grp(f_s), gm.unsqueeze(2).to_broadcast([P, B * GROUPS, EPG]), ALU.mult))
            route(dve.tensor_scalar(gm, gm, 1.0, None, ALU.subtract))
            route(dve.tensor_tensor(grp(f_v), grp(f_v), gm.unsqueeze(2).to_broadcast([P, B * GROUPS, EPG]), ALU.add))
            route(dve.memset(f_sel, 0.0))
            key = c("key").unsqueeze(1).to_broadcast([P, B, E])
            for _ in range(TOPK):
                route(dve.tensor_reduce(f_m, f_v, AX.X, ALU.max))
                route(dve.tensor_tensor(f_eq, f_v, f_m.unsqueeze(2).to_broadcast([P, B, E]), ALU.is_equal))
                route(dve.tensor_tensor(f_eq, f_eq, key, ALU.mult))
                route(dve.tensor_reduce(f_m, f_eq, AX.X, ALU.max))
                route(dve.tensor_tensor(f_eq, key, f_m.unsqueeze(2).to_broadcast([P, B, E]), ALU.is_equal))
                route(dve.tensor_tensor(f_sel, f_sel, f_eq, ALU.add))
                flat = lambda v: v.rearrange("p b e -> p (b e)")
                route(dve.scalar_tensor_tensor(out=flat(f_v), in0=flat(f_eq), scalar=-BIG, in1=flat(f_v),
                                               op0=ALU.mult, op1=ALU.add))
            route(dve.tensor_tensor(f_sel, f_sel, f_sc, ALU.mult))
            route(dve.tensor_reduce(f_m, f_sel, AX.X, ALU.add))
            route(dve.tensor_scalar(f_m, f_m, 1e-20, None, ALU.add))
            route(dve.reciprocal(f_m, f_m))
            route(dve.tensor_scalar(f_m, f_m, MOE_SCALE, None, ALU.mult))
            route(dve.memset(f_comb[:, :, E:NE], 1.0))
            route(dve.tensor_tensor(f_comb[:, :, 0:E], f_sel, f_m.unsqueeze(2).to_broadcast([P, B, E]), ALU.mult))

            def f_mul_(m):
                for c_ in range(KC):
                    wait(dve, f_hp, m, 2 * c_ + 2)
                    wait(dve, f_silu, m, c_ + 1)
                    wait(dve, f_dp, m, 2, back=2)
                    dve.tensor_tensor(f_a[m.p][:, c_, :], f_h[c_], bank[2 + c_][:], ALU.mult).then_inc(f_mul.sem, 1)

            def f_acc_(m, g, e):
                for i in range(TG):
                    b = TG * g + i
                    if i % 2 == 0:
                        wait(dve, f_dp, m, i // 2 + 1)
                    wait(dve, f_acc, m, i + 1, back=G)
                    dve.scalar_tensor_tensor(out=X[:, b, 0:D],
                                             in0=bank[4 + 2 * m.p + i // 2][:, (i % 2) * D:(i % 2 + 1) * D],
                                             scalar=f_comb[:, b, bass.ds(e, 1)],
                                             in1=X[:, b, 0:D], op0=ALU.mult, op1=ALU.add).then_inc(f_acc.sem, 1)

            for m in range(2 * G):
                f_mul_(turn(m))
                if m:
                    f_acc_(turn(m - 1), (m - 1) % G, (m - 1) // G)
            with dve.Fori(2, NE) as e:
                for g in range(G):
                    f_mul_(Turn(G * e + g, g % 2, 0))
                    f_acc_(Turn(G * e + g - 1, (g - 1) % 2, 0), (g - 1) % G, e if g else e - 1)
            f_acc_(turn(MT - 1), G - 1, NE - 1)

            def f_stats_(t):
                st = stats.again(F_)
                wait(dve, rstd.again(F_), t, 1, back=2)
                if t.peeled and t.b == 0:
                    wait_end(dve, f_acc)
                dve.bn_stats(bn[t.p][:], X[:, t.b, 0:D]).then_inc(st.sem, 1)
                wait(dve, st, t, 1)
                hold(dve)
                dve.bn_aggr(mv[t.p][:], bn[t.p][:]).then_inc(st.sem, 1)

            def f_final_(t):
                wait(dve, rstd.again(F_), t, 2)
                if not t.peeled or t.b >= 2:
                    dve.wait_ge(s_out[t.p], 16 * t.half)
                dve.tensor_scalar(f_out[t.p], X[:, t.b, 0:D], mv[t.p][:, 0:1], lr[t.p][:, 1:2], ALU.subtract,
                                  ALU.mult).then_inc(normed.sem, 1)

            pipelined(dve, [(f_stats_, 0), (f_final_, 1)])


def packed(m):
    return m.reshape(-1, P, m.shape[1]).transpose(1, 0, 2)


def kernel(x, ctx_1024, L0_attn_Wqkv, L0_attn_bqkv, L0_attn_gq, L0_attn_gk, L0_attn_Wout, L0_attn_bout, L0_attn_gout,
           L0_xattn_Wq, L0_xattn_Wk, L0_xattn_Wv, L0_xattn_Wproj, L0_ffn_attention_mask, L0_ffn_position_ids,
           L0_ffn_router_w, L0_ffn_router_b, L0_ffn_wq, L0_ffn_wk, L0_ffn_wv, L0_ffn_wo, L0_ffn_w1, L0_ffn_w2,
           L0_ffn_ln1, L0_ffn_ln2, L1_attn_w_qkv, L1_attn_b_qkv, L1_attn_w_proj, L1_attn_b_proj, L1_xattn_Wq,
           L1_xattn_Wk, L1_xattn_Wv, L1_xattn_Wo, L1_xattn_bo, L1_ffn_router_w, L1_ffn_bias, L1_ffn_gate_w,
           L1_ffn_up_w, L1_ffn_down_w, L1_ffn_sh_gate_w, L1_ffn_sh_up_w, L1_ffn_sh_down_w):
    import concourse.bacc as bacc
    from concourse.bass_utils import run_bass_kernel_spmd

    n = np.asarray
    turned = lambda v: n(v).reshape(B, P, KC, P).transpose(0, 3, 2, 1)
    bqkv = n(L1_attn_b_qkv)
    shared = [n(L1_ffn_sh_gate_w), n(L1_ffn_sh_up_w), n(L1_ffn_sh_down_w)]
    experts = []
    for e in range(NE):
        if e < E:
            w = [n(L1_ffn_gate_w)[e], n(L1_ffn_up_w)[e], n(L1_ffn_down_w)[e]]
        else:
            part = slice((e - E) * EF, (e - E + 1) * EF)
            w = [shared[0][:, part], shared[1][:, part], shared[2][part]]
        experts.append(np.concatenate([packed(v) for v in w], axis=1))
    arrays = {
        "x": n(x),
        "xT": turned(x),
        "ctxT": turned(ctx_1024),
        "const": constants(),
        "rows": np.concatenate([n(v).reshape(-1) for v in (
            L0_attn_bqkv, L0_attn_gq, L0_attn_gk, L0_attn_bout, L0_attn_gout, L0_ffn_ln1, L0_ffn_ln2,
            bqkv[2 * D:], L1_attn_b_proj, L1_xattn_bo, L0_ffn_router_b, L1_ffn_bias)]),
        "cols": np.concatenate([bqkv[:2 * D].reshape(2 * KC, P).T, n(L0_ffn_router_w).reshape(KC, P).T], axis=1),
        "a_w": packed(n(L0_attn_Wqkv).T),
        "a_wout": packed(n(L0_attn_Wout).T),
        "b_wq": packed(n(L0_xattn_Wq)),
        "b_wk": packed(n(L0_xattn_Wk)),
        "b_wv": packed(n(L0_xattn_Wv)),
        "b_wp": packed(n(L0_xattn_Wproj).T),
        "c_wqkv": np.concatenate([packed(n(v)) for v in (L0_ffn_wq, L0_ffn_wk, L0_ffn_wv)], axis=2),
        "c_wo": packed(n(L0_ffn_wo)),
        "c_w1": packed(n(L0_ffn_w1)),
        "c_w2": packed(n(L0_ffn_w2)),
        "mask": n(L0_ffn_attention_mask)[:, 0, :P, :P].transpose(1, 0, 2),
        "pos": n(L0_ffn_position_ids)[:, :P].T,
        "d_w": np.concatenate([packed(n(L1_attn_w_qkv)), packed(n(L1_attn_w_proj))], axis=2),
        "e_w": np.concatenate([packed(n(v).T) for v in (L1_xattn_Wq, L1_xattn_Wk, L1_xattn_Wv, L1_xattn_Wo)], axis=2),
        "f_rw": packed(n(L1_ffn_router_w).T),
        "f_w": np.stack(experts),
    }
    nc = bacc.Bacc("TRN2", target_bir_lowering=False, num_devices=1)
    given, handles = {}, {}
    for name, v in arrays.items():
        v = np.ascontiguousarray(v)
        given[f"in_{name}"] = v
        handles[name] = nc.dram_tensor(f"in_{name}", v.shape, mybir.dt.from_np(v.dtype), kind="ExternalInput").ap()
    handles["out"] = nc.dram_tensor("out_x", (B, P, D), F32, kind="ExternalOutput").ap()
    build(nc, handles)
    done = run_bass_kernel_spmd(nc, [given], core_ids=[0])
    return done.results[0]["out_x"]
```

```python
from contextlib import ExitStack

import numpy as np

import concourse.bass as bass
from concourse import mybir
from concourse.alu_op_type import AluOpType as ALU

F32 = mybir.dt.float32
F32R = mybir.dt.float32r
BF16 = mybir.dt.bfloat16
I32 = mybir.dt.int32
ACT = mybir.ActivationFunctionType
AX = mybir.AxisListType

P = 128
B = 16
D = 256
KC = D // P
H = 16
HD = D // H
HH = H // KC
QH = 4
NQ = H // QH
SCALE = HD ** -0.5
VW = P + 2
NW = P + HH
HV = HD + 1

SEL = int(0.125 * P) - 1
TSEQ = 8
TILES = B // TSEQ
S = SEL * TSEQ
F0 = 1024
FC = F0 // P
XW = D + 2
E = 16
EF = 256
SH = 2
NE = SH + E
GT = 512
G = B * P // GT
TG = GT // P
GROUPS, TOPG, TOPK = 4, 2, 4
EPG = E // GROUPS
MOE_SCALE = 2.5

RMS_EPS = 1.1920929e-07
LIN_EPS = 1e-06
FFN_EPS = 1e-06
LN_EPS = 1e-05
NEG = -1e30
FAR = -3e38
BIG = 3e38
MAGIC = 1.5 * 2.0 ** 23
PI = float(np.pi)


def layout(*fields):
    at, where = 0, {}
    for name, width in fields:
        where[name] = slice(at, at + width)
        at += width
    return where, at


CONST, N_CONST = layout(("ident", P), ("causal", P), ("before", P), ("blocks", P), ("heads", HH),
                        ("cos", D), ("sin", D), ("slots", P), ("seqslot", B), ("apart", S),
                        ("invfreq", 8), ("key", E), ("half", 2), ("ln_eps", 1), ("rms_eps", 2))
ROWS, N_ROWS = layout(("bqkv", 3 * D), ("gq", D), ("gk", D), ("bout", D), ("gout", D), ("ln1", D),
                      ("ln2", D), ("bv", D), ("bproj", D), ("bo", D), ("router_b", 1), ("ebias", E))
COLS, N_COLS = layout(("bqk", 2 * KC), ("router_w", KC))


def constants():
    c = np.zeros((P, N_CONST), np.float32)
    p = np.arange(P)[:, None]
    j = np.arange(P)[None, :]
    c[:, CONST["ident"]] = p == j
    c[:, CONST["causal"]] = np.where(j <= p, 0.0, NEG)
    c[:, CONST["before"]] = j < p
    c[:, CONST["blocks"]] = p // HD == j // HD
    c[:, CONST["heads"]] = p // HD == np.arange(HH)[None, :]
    inv = (1.0 / np.float32(10000.0) ** (np.arange(0, HD, 2, dtype=np.float32) / HD)).astype(np.float32)
    angle = np.arange(P, dtype=np.float32)[:, None] * inv[None, :]
    c[:, CONST["cos"]] = np.tile(np.repeat(np.cos(angle), 2, axis=1), (1, H))
    sine = np.stack([-np.sin(angle), np.sin(angle)], axis=-1).reshape(P, HD)
    c[:, CONST["sin"]] = np.tile(sine, (1, H))
    c[:, CONST["slots"]] = j
    c[:, CONST["seqslot"]] = (np.arange(B) % TSEQ)[None, :] * SEL
    c[:S, CONST["apart"]] = np.where(p[:S] // SEL == j[:, :S] // SEL, 0.0, FAR)
    c[:, CONST["invfreq"]] = inv
    c[:, CONST["key"]] = E - np.arange(E)
    c[:, CONST["half"]] = -0.5
    c[:, CONST["ln_eps"]] = LN_EPS
    c[:, CONST["rms_eps"]] = RMS_EPS
    return c


class Turn:

    def __init__(self, b, p, half):
        self.b, self.p, self.half = b, p, half
        self.peeled = isinstance(b, int)


def turn(b):
    return Turn(b, b % 2, b // 2)


class Step:

    def __init__(self, sem, n, round=0, turns=B):
        self.sem, self.n, self.round, self.turns = sem, n, round, turns

    def again(self, round):
        return Step(self.sem, self.n, round, self.turns)

    def at(self, t, k, back=0):
        return self.n * (t.b + self.turns * self.round - back) + k

    def end(self):
        return self.n * self.turns * (self.round + 1)


def wait(eng, step, t, k, back=0):
    if t.peeled and t.b + step.turns * step.round < back:
        return
    eng.wait_ge(step.sem, step.at(t, k, back))


def wait_end(eng, step):
    eng.wait_ge(step.sem, step.end())


def pipelined(eng, stages, start=0, stop=B, peel=0):
    deepest = max(lag for _, lag in stages)
    first = start + max(deepest + deepest % 2 + 2, peel)

    def iteration(i):
        for stage, lag in stages:
            if start <= i - lag < stop:
                stage(turn(i - lag))

    for i in range(start, first):
        iteration(i)
    with eng.Fori(first // 2, stop // 2) as j:
        for u in (0, 1):
            for stage, lag in stages:
                b = u - lag
                stage(Turn(2 * j + b, b % 2, j + b // 2))
    for i in range(stop, stop + deepest):
        iteration(i)


def chained(eng, rounds):
    deepest = max(lag for _, lag in rounds[0])
    first = deepest + deepest % 2 + 2

    def iteration(i):
        for k, (_, lag) in enumerate(rounds[0]):
            b = i - lag
            if 0 <= b < B * len(rounds):
                rounds[b // B][k][0](turn(b % B))

    for n, stages in enumerate(rounds):
        for i in range(first):
            iteration(B * n + i)
        with eng.Fori(first // 2, B // 2) as j:
            for u in (0, 1):
                for stage, lag in stages:
                    b = u - lag
                    stage(Turn(2 * j + b, b % 2, j + b // 2))
    for i in range(deepest):
        iteration(B * len(rounds) + i)


def build(nc, a):
    out = a["out"]
    with ExitStack() as ctx:
        def sb(name, shape, dt=F32):
            return ctx.enter_context(nc.sbuf_tensor(name, shape, dt))

        def sem(name):
            return ctx.enter_context(nc.semaphore(name))

        def step(name, n, turns=B):
            return Step(sem(name), n, 0, turns)

        bank = [ctx.enter_context(nc.psum_tensor(f"bank{i}", [P, 512], F32)) for i in range(8)]

        X = sb("X", [P, B, XW])
        const = sb("const", [P, N_CONST])
        rows = sb("rows", [P, N_ROWS])
        cols = sb("cols", [P, N_COLS])
        ident_bf = sb("ident_bf", [P, P], BF16)
        causal_bf = sb("causal_bf", [P, P], BF16)
        xs = [sb(f"xs{i}", [P, D]) for i in range(2)]
        xT = [sb(f"xT{i}", [P, KC, P]) for i in range(2)]
        inT = [sb(f"inT{i}", [P, KC, P]) for i in range(2)]
        y = [sb(f"y{i}", [P, D]) for i in range(2)]
        bn = [sb(f"bn{i}", [P, 6]) for i in range(2)]
        mv = [sb(f"mv{i}", [P, 2]) for i in range(2)]
        lr = [sb(f"lr{i}", [P, 2]) for i in range(2)]
        keep1 = sb("keep1", [P, B])

        def c(name, n=P):
            return const[0:n, CONST[name]]

        def row(name, n=P):
            return rows[0:n, ROWS[name]]

        ident = c("ident")

        ARENA, PLAIN = 39 * 1024, 21 * 1024
        with nc.sbuf_tensor("arena", [P, ARENA], F32) as arena:
            pass
        sb("arena_plain", [P, PLAIN])
        with ExitStack() as attention:
            def parts(name, *shape):
                return [attention.enter_context(nc.sbuf_tensor(f"{name}{i}", [P, *shape], F32R)) for i in range(2)]

            d_xh, d_xl = parts("d_xh", H, P), parts("d_xl", H, P)
            d_qh, d_ql = parts("d_qh", KC, P), parts("d_ql", KC, P)
            d_kh = parts("d_kh", KC, P)
        f_xh = sb("f_xh", [P, KC, B * P], F32R)
        f_xl = sb("f_xl", [P, KC, B * P], F32R)
        f_wh = [sb(f"f_wh{i}", [P, 3 * KC, EF], F32R) for i in range(2)]
        f_wl = [sb(f"f_wl{i}", [P, 3 * KC, EF], F32R) for i in range(2)]
        f_ah = [sb(f"f_ah{i}", [P, KC, GT], F32R) for i in range(2)]
        f_al = [sb(f"f_al{i}", [P, KC, GT], F32R) for i in range(2)]

        class Carve:
            def __init__(self, at):
                self.at = at

            def __call__(self, *shape):
                n = int(np.prod(shape))
                self.at += self.at % 2
                view = arena[:, self.at:self.at + n]
                self.at += n
                assert self.at <= ARENA, self.at
                if len(shape) == 2:
                    view = view.rearrange("p (a b) -> p a b", b=shape[1])
                if len(shape) == 3:
                    view = view.rearrange("p (a b c) -> p a b c", b=shape[1], c=shape[2])
                return view

        A = Carve(0)
        a_w = A(KC, 3 * D)
        a_wout = A(KC, D)
        a_cos = A(2 * D)
        a_sin = A(2 * D)
        a_qk = [A(2 * D) for _ in range(2)]
        a_v = [A(KC, VW) for _ in range(2)]
        a_ms = [A(2) for _ in range(2)]
        a_sqs = [A(3, D) for _ in range(2)]
        a_r = [A(2) for _ in range(2)]
        a_u = [A(2 * D) for _ in range(2)]
        a_sw = [A(2 * D) for _ in range(2)]
        a_f = [A(2 * D) for _ in range(2)]
        a_kv = [A(KC, NW) for _ in range(2)]
        a_fT = [A(KC, P) for _ in range(2)]
        a_den = [A(KC, HH) for _ in range(2)]
        a_rden = [A(KC, HH) for _ in range(2)]
        a_at = [A(D) for _ in range(2)]
        a_atT = [A(KC, P) for _ in range(2)]
        a_o = [A(D) for _ in range(2)]
        a_oms = [A(1) for _ in range(2)]
        a_or = [A(2) for _ in range(2)]
        b_wq = A(KC, D)
        b_wk = A(KC, D)
        b_wv = A(KC, D)
        b_wp = A(KC, D)
        b_A = A(KC, D)
        b_B = A(KC, D)
        b_qT = [A(KC, P) for _ in range(2)]
        b_v = [A(D) for _ in range(2)]
        b_s = [A(P) for _ in range(2)]
        b_nmax = [A(1) for _ in range(2)]
        b_p = [A(P) for _ in range(2)]
        b_sum = [A(1) for _ in range(2)]
        b_rsum = [A(1) for _ in range(2)]
        b_pT = [A(P) for _ in range(2)]
        c_wqkv = A(KC, 3 * D)
        c_wo = A(KC, D)
        c_w1 = A(KC, F0)
        c_w2 = A(FC, D)
        c_mask = A(4, P)
        c_posi = A(4)
        c_rw = A(KC, P)
        c_ET = A(B, P)
        c_proc = A(TILES, D)
        weights_end = A.at
        A = Carve(0)
        c_wr = [A(P) for _ in range(2)]
        c_small = [A(4) for _ in range(2)]
        c_counts = A(B, 4)
        c_slot, c_over = A(B), A(B)
        c_cmp = [A(4, P) for _ in range(2)]
        c_E = [A(P) for _ in range(2)]
        c_U = [A(P) for _ in range(2)]
        c_ets = [A(P) for _ in range(2)]
        c_sel = [A(XW) for _ in range(TILES)]
        c_sqs = [A(2, D) for _ in range(TILES)]
        c_msk = [A(S) for _ in range(TILES)]
        c_st = [A(16) for _ in range(TILES)]
        c_hn = [A(D) for _ in range(TILES)]
        c_hT = A(KC, TILES * S)
        c_ang = [A(8, 8) for _ in range(TILES)]
        c_arg = [A(2, 8) for _ in range(TILES)]
        c_cs = [A(3, 8) for _ in range(TILES)]
        c_x = [A(2 * D) for _ in range(TILES)]
        c_z = [A(2 * D) for _ in range(TILES)]
        c_v = [A(H, HV) for _ in range(TILES)]
        c_qT = [A(KC, S) for _ in range(TILES)]
        c_rs = [A(H) for _ in range(TILES)]
        c_at = [A(D) for _ in range(TILES)]
        c_oT = [A(KC, S) for _ in range(TILES)]
        c_x1 = [A(D) for _ in range(TILES)]
        A = Carve(weights_end)
        c_kexp = A(H, S)
        c_S = [A(H, S) for _ in range(TILES)]
        c_mx = [A(H) for _ in range(TILES)]
        c_pT = [A(H, S) for _ in range(TILES)]
        c_gT = A(FC, TILES * S)
        d_w0 = A(KC, 4 * D)
        A = Carve(0)
        d_w = [d_w0, A(KC, 4 * D)]
        d_bq = A(KC)
        d_qT = [A(KC, P) for _ in range(2)]
        d_kT = [A(KC, P) for _ in range(2)]
        d_kl = [A(KC, P) for _ in range(2)]
        d_v = [A(H, HV) for _ in range(2)]
        d_S = [A(H, P) for _ in range(2)]
        d_mx = [A(H) for _ in range(2)]
        d_pT = [A(H, P) for _ in range(2)]
        d_rs = [A(H) for _ in range(2)]
        d_at = [A(D) for _ in range(2)]
        d_atT = [A(KC, P) for _ in range(2)]
        d_xb = [A(D) for _ in range(2)]
        f_rw = A(KC, E)
        f_ws0 = A(3 * KC, EF)
        assert A.at <= PLAIN
        A = Carve(0)
        f_lg = A(B, E)
        f_sc = A(B, E)
        f_s = A(B, E)
        f_pair = A(B * GROUPS, 6)
        f_gs = A(B, GROUPS)
        f_c1 = A(B * GROUPS, GROUPS)
        f_c2 = A(B * GROUPS, GROUPS)
        f_gm = A(B, GROUPS)
        f_v = A(B, E)
        f_eq = A(B, E)
        f_m = A(B)
        f_sel = A(B, E)
        f_comb = A(B, NE)
        f_ws = [f_ws0, A(3 * KC, EF)]
        f_h = [A(GT) for _ in range(2)]
        f_a = [A(KC, GT) for _ in range(2)]
        f_out = [A(D) for _ in range(2)]
        assert A.at <= PLAIN

        l_const = sem("l_const")
        held = sem("held")
        l_aw = sem("l_aw")
        l_awo = sem("l_awo")
        l_rows = sem("l_rows")
        l_rest = sem("l_rest")
        l_x = sem("l_x")
        l_bw = sem("l_bw")
        l_cw = sem("l_cw")
        l_dw = [sem("l_dw0"), sem("l_dw1")]
        l_inT = [sem("l_inT0"), sem("l_inT1")]
        l_ew = [sem("l_ew0"), sem("l_ew1")]
        s_out = [sem("s_out0"), sem("s_out1")]
        a_tab = sem("a_tab")

        copied = step("copied", 1)
        turned = step("turned", 1)
        xt_done = step("xt_done", 1)
        stats = step("stats", 2)
        rstd = step("rstd", 2)
        normed = step("normed", 1)
        a_qkp = step("a_qkp", 1)
        a_vp = step("a_vp", 1)
        a_qkb = step("a_qkb", 1)
        a_vb = step("a_vb", 1)
        a_sq = step("a_sq", 2)
        a_rms = step("a_rms", 2)
        a_swap = step("a_swap", 2)
        a_turn = step("a_turn", 1)
        a_rope = step("a_rope", 1)
        a_relu = step("a_relu", 2)
        a_kvp = step("a_kvp", 1)
        a_fTp = step("a_fTp", 1)
        a_kvm = step("a_kvm", 2)
        a_fTc = step("a_fTc", 1)
        a_nd = step("a_nd", 1)
        a_div = step("a_div", 3)
        a_atp = step("a_atp", 1)
        a_atc = step("a_atc", 1)
        a_op = step("a_op", 1)
        a_ob = step("a_ob", 1)
        a_osq = step("a_osq", 1)
        a_orms = step("a_orms", 2)
        a_y = step("a_y", 2)
        b_fold = step("b_fold", 2, 1)
        b_folded = step("b_folded", 2, 1)
        b_qp = step("b_qp", 1)
        b_vp = step("b_vp", 1)
        b_qc = step("b_qc", 1)
        b_vc = step("b_vc", 1)
        b_sp = step("b_sp", 1)
        b_max = step("b_max", 1)
        b_exp = step("b_exp", 1)
        b_pTp = step("b_pTp", 1)
        b_pTc = step("b_pTc", 2)
        b_yp = step("b_yp", 1)
        b_y = step("b_y", 1)
        c_prep = sem("c_prep")
        c_wp = step("c_wp", 1)
        c_wc = step("c_wc", 1)
        c_cnt = step("c_cnt", 4)
        c_kept = step("c_kept", 1)
        c_place = sem("c_place")
        c_hot = step("c_hot", 1)
        c_Up = step("c_Up", 1)
        c_Uc = step("c_Uc", 1)
        c_ETp = step("c_ETp", 1)
        c_ETc = step("c_ETc", 1)
        c_gp = step("c_gp", 1)
        c_mp = step("c_mp", 1)
        c_pe = sem("c_pe")
        c_dve = sem("c_dve")
        c_act = sem("c_act")
        c_pool = sem("c_pool")
        c_link = sem("c_link")

        def stage_at(k, g):
            return TILES * k + g + 1

        def tile_major(first, last):
            def at(k, g):
                if first <= k <= last:
                    return TILES * first + (last - first + 1) * g + (k - first) + 1
                return stage_at(k, g)
            return at

        dve_at, act_at, pe_at = tile_major(7, 9), tile_major(4, 5), tile_major(5, 6)

        def keys_at(g):
            return TILES * 5 + 2 * (g + 1)

        c_fp = step("c_fp", 4, 1)
        c_gelu = step("c_gelu", 4, 1)
        c_etsc = step("c_etsc", 1)
        c_sp = step("c_sp", 1)
        c_y = step("c_y", 1)
        d_prep = sem("d_prep")
        d_qkp = step("d_qkp", 1)
        d_vp = step("d_vp", 1)
        d_qkc = step("d_qkc", 4)
        d_vc = step("d_vc", 1)
        d_hi = step("d_hi", 2)
        d_lo = step("d_lo", 2)
        d_kx = step("d_kx", 2 * KC)
        d_xbc = step("d_xbc", 1)
        d_sp = step("d_sp", NQ)
        d_max = step("d_max", 2 * NQ)
        d_exp = step("d_exp", NQ)
        d_pTp = step("d_pTp", NQ)
        d_pTc = step("d_pTc", NQ)
        d_pv = step("d_pv", NQ)
        d_div = step("d_div", 2)
        d_atp = step("d_atp", 1)
        d_atc = step("d_atc", 1)
        d_op = step("d_op", 1)
        d_y = step("d_y", 1)
        f_xhc = step("f_xhc", 1)
        f_xlc = step("f_xlc", 1)
        f_lp = step("f_lp", 1)
        f_lc = step("f_lc", 1)
        f_sig = sem("f_sig")
        f_route = sem("f_route")
        MT = NE * G
        f_hp = step("f_hp", 4, MT)
        f_silu = step("f_silu", 2, MT)
        f_mul = step("f_mul", 2, MT)
        f_whc = step("f_whc", 1, NE)
        f_wlc = step("f_wlc", 1, NE)
        f_ahc = step("f_ahc", 2, MT)
        f_alc = step("f_alc", 2, MT)
        f_dp = step("f_dp", 2, MT)
        f_acc = step("f_acc", TG, MT)

        A_, B_, C_, D_, E_, F_ = range(6)
        XT = {B_: 0, C_: 1, D_: 2, E_: 3, F_: 4}

        block = ctx.enter_context(nc.Block())

        def hold(eng):
            eng.sem_inc(held, 1)

        @block.sync
        def _(sp):
            def load_x(t):
                wait(sp, a_vp, t, 1, back=2)
                sp.dma_start(inT[t.p][:], a["xT"][t.b]).then_inc(l_inT[t.p], 16)

            def load_ctx_b(t):
                if not t.peeled or t.b >= 2:
                    wait(sp, b_sp, t, 1, back=2)
                    wait(sp, b_vp, t, 1, back=2)
                else:
                    wait_end(sp, a_vp)
                sp.dma_start(inT[t.p][:], a["ctxT"][t.b]).then_inc(l_inT[t.p], 16)

            def load_ctx_e(t):
                vp = d_vp.again(1)
                if not t.peeled or t.b >= 2:
                    wait(sp, vp, t, 1, back=2)
                else:
                    wait_end(sp, b_sp)
                sp.dma_start(inT[t.p][:], a["ctxT"][t.b]).then_inc(l_inT[t.p], 16)

            load_x(turn(0))
            sp.dma_start(const[:], a["const"]).then_inc(l_const, 16)
            load_x(turn(1))
            load_x(turn(2))
            sp.dma_start(X[:, :, 0:D], a["x"].rearrange("b p d -> p b d")).then_inc(l_x, 16)
            load_x(turn(3))
            sp.dma_start(b_wq, a["b_wq"]).then_inc(l_bw, 16)
            sp.dma_start(b_wk, a["b_wk"]).then_inc(l_bw, 16)
            sp.dma_start(b_wv, a["b_wv"]).then_inc(l_bw, 16)
            sp.dma_start(b_wp, a["b_wp"]).then_inc(l_bw, 16)
            load_x(turn(4))
            sp.dma_start(c_wqkv, a["c_wqkv"]).then_inc(l_cw, 16)
            sp.dma_start(c_wo, a["c_wo"]).then_inc(l_cw, 16)
            load_x(turn(5))
            sp.dma_start(c_w1, a["c_w1"]).then_inc(l_cw, 16)
            load_x(turn(6))
            sp.dma_start(c_w2, a["c_w2"]).then_inc(l_cw, 16)
            load_x(turn(7))
            sp.dma_start(c_mask, a["mask"]).then_inc(l_cw, 16)
            sp.dma_start(c_posi.bitcast(I32), a["pos"]).then_inc(l_cw, 16)
            sp.dma_start(d_w[0], a["d_w"]).then_inc(l_dw[0], 16)
            with sp.Fori(4, B // 2) as j:
                for u in (0, 1):
                    load_x(Turn(2 * j + u, u, j))
            load_ctx_b(turn(0))
            load_ctx_b(turn(1))
            with sp.Fori(1, B // 2) as j:
                for u in (0, 1):
                    load_ctx_b(Turn(2 * j + u, u, j))
            wait_end(sp, c_sp)
            sp.dma_start(d_w[1], a["e_w"]).then_inc(l_dw[1], 16)
            sp.dma_start(f_rw, a["f_rw"]).then_inc(l_dw[1], 16)
            load_ctx_e(turn(0))
            load_ctx_e(turn(1))
            with sp.Fori(1, B // 2) as j:
                for u in (0, 1):
                    load_ctx_e(Turn(2 * j + u, u, j))
            sp.dma_start(f_ws[0], a["f_w"][0]).then_inc(l_ew[0], 16)
            sp.wait_ge(normed.sem, normed.again(E_).end())
            sp.dma_start(f_ws[1], a["f_w"][1]).then_inc(l_ew[1], 16)
            with sp.Fori(1, NE // 2) as j:
                for u in (0, 1):
                    sp.wait_ge(f_wlc.sem, 2 * j + u - 1)
                    sp.dma_start(f_ws[u], a["f_w"][2 * j + u]).then_inc(l_ew[u], 16)
            for b in range(B):
                sp.wait_ge(normed.sem, normed.again(F_).at(turn(b), 1))
                sp.dma_start(out[b], f_out[b % 2]).then_inc(s_out[b % 2], 16)
            for q in s_out:
                sp.wait_ge(q, 16 * (B // 2))

        @block.gpsimd
        def _(pool):
            def copy_x(round, before):
                step_ = copied.again(XT[round])
                def stage(t):
                    wait(pool, normed.again(before), t, 1)
                    wait(pool, turned.again(XT[round]), t, 1, back=2)
                    pool.tensor_copy(xs[t.p][:], X[:, t.b, 0:D]).then_inc(step_.sem, 1)
                return stage

            def ln_power(round):
                st, rs, nd = stats.again(round), rstd.again(round), normed.again(round)
                def stage(t):
                    wait(pool, st, t, 2)
                    wait(pool, nd, t, 1, back=2)
                    pool.tensor_tensor(lr[t.p][:, 0:1], mv[t.p][:, 1:2], c("ln_eps"), ALU.add).then_inc(rs.sem, 1)
                    wait(pool, rs, t, 1)
                    pool.tensor_tensor(lr[t.p][:, 1:2], lr[t.p][:, 0:1], c("half")[:, 0:1], ALU.pow).then_inc(rs.sem, 1)
                return stage

            pool.wait_ge(l_const, 16)

            def a_swap_(t):
                wait(pool, a_qkb, t, 1)
                wait(pool, a_rope, t, 1, back=2)
                q = a_qk[t.p].rearrange("p (n two) -> p n two", two=2)
                s_ = a_sin.rearrange("p (n two) -> p n two", two=2)
                o = a_sw[t.p].rearrange("p (n two) -> p n two", two=2)
                if t.peeled and t.b == 0:
                    pool.wait_ge(a_tab, 6)
                pool.tensor_tensor(o[:, :, 0], q[:, :, 1], s_[:, :, 0], ALU.mult).then_inc(a_swap.sem, 1)
                pool.tensor_tensor(o[:, :, 1], q[:, :, 0], s_[:, :, 1], ALU.mult).then_inc(a_swap.sem, 1)

            def a_turn_(t):
                wait(pool, a_qkb, t, 1)
                wait(pool, a_relu, t, 2, back=2)
                pool.tensor_tensor(a_u[t.p], a_qk[t.p], a_cos, ALU.mult).then_inc(a_turn.sem, 1)

            def a_rms_(t):
                wait(pool, a_sq, t, 2)
                wait(pool, a_relu, t, 2, back=2)
                pool.tensor_tensor(a_ms[t.p], a_ms[t.p], c("rms_eps"), ALU.add).then_inc(a_rms.sem, 1)
                wait(pool, a_rms, t, 1)
                pool.tensor_tensor(a_r[t.p], a_ms[t.p], c("half"), ALU.pow).then_inc(a_rms.sem, 1)

            def a_orms_(t):
                wait(pool, a_osq, t, 1)
                wait(pool, a_y, t, 1, back=2)
                pool.tensor_tensor(a_or[t.p][:, 0:1], a_oms[t.p], c("rms_eps")[:, 0:1], ALU.add).then_inc(a_orms.sem, 1)
                wait(pool, a_orms, t, 1)
                pool.tensor_tensor(a_or[t.p][:, 1:2], a_or[t.p][:, 0:1], c("half")[:, 0:1], ALU.pow).then_inc(a_orms.sem, 1)

            pipelined(pool, [(ln_power(A_), 6), (a_orms_, 5), (a_swap_, 1), (a_turn_, 1), (a_rms_, 1)])

            pipelined(pool, [(copy_x(B_, A_), 0), (ln_power(B_), 5)])

            def c_kept_(t):
                wait(pool, c_cnt, t, 4)
                pool.tensor_copy(c_counts[:, t.b, :], c_small[t.p]).then_inc(c_kept.sem, 1)

            pipelined(pool, [(copy_x(C_, B_), 0), (c_kept_, 4)])
            for k in (0, 2):
                for g in range(TILES):
                    pool.wait_ge(c_act, act_at(0 if k == 0 else 7, g))
                    pool.tensor_scalar(c_st[g][0:S, 1 + k:2 + k], c_st[g][0:S, k:k + 1], FFN_EPS, None,
                                       ALU.add).then_inc(c_pool, 1)
                    pool.wait_ge(c_pool, 2 * (k // 2 * TILES + g) + 1)
                    pool.tensor_tensor(c_st[g][0:S, 4 + k:5 + k], c_st[g][0:S, 1 + k:2 + k], c("half", S)[:, 0:1],
                                       ALU.pow).then_inc(c_pool, 1)

            def c_ets_(t):
                wait(pool, c_ETc, t, 1)
                wait(pool, c_sp, t, 1, back=2)
                pool.tensor_copy(c_ets[t.p][0:S], c_ET[0:S, t.b, :]).then_inc(c_etsc.sem, 1)

            pipelined(pool, [(c_ets_, 0), (ln_power(C_), 3)])

            rounds = []
            for n, round in enumerate((D_, E_)):
                def d_kx_(t, n=n):
                    kx = d_kx.again(n)
                    wait(pool, d_sp.again(n), t, NQ, back=2)
                    for k in range(KC):
                        for i, (keys, o) in enumerate(((d_kh, d_xh), (d_kl, d_xl))):
                            wait(pool, d_hi.again(n) if i == 0 else d_lo.again(n), t, 1)
                            pool.tensor_tensor(o[t.p][:, k * HH:(k + 1) * HH, :],
                                               keys[t.p][:, k:k + 1, :].to_broadcast([P, HH, P]),
                                               c("heads").unsqueeze(2).to_broadcast([P, HH, P]),
                                               ALU.mult).then_inc(kx.sem, 1)

                def d_xb_(t, n=n, round=round):
                    wait(pool, normed.again(round - 1), t, 1)
                    wait(pool, d_y.again(n), t, 1, back=2)
                    hold(pool)
                    pool.tensor_tensor(d_xb[t.p], X[:, t.b, 0:D], row("bproj" if n == 0 else "bo"),
                                       ALU.add).then_inc(d_xbc.sem, 1)

                rounds.append([(ln_power(round), 4), (d_xb_, 3), (d_kx_, 1)])
            chained(pool, rounds)

            def f_wl_(e, p):
                pool.wait_ge(f_whc.sem, e + 1)
                for i in range(3):
                    part = slice(i * KC, (i + 1) * KC)
                    m = pool.tensor_tensor(f_wl[p][:, part, :], f_ws[p][:, part, :], f_wh[p][:, part, :], ALU.subtract)
                m.then_inc(f_wlc.sem, 1)

            def f_al_(m):
                for c_ in range(KC):
                    wait(pool, f_ahc, m, c_ + 1)
                    wait(pool, f_dp, m, 2, back=2)
                    pool.tensor_tensor(f_al[m.p][:, c_, :], f_a[m.p][:, c_, :], f_ah[m.p][:, c_, :], ALU.subtract)\
                        .then_inc(f_alc.sem, 1)

            def f_low(j, last=False):
                for i in range(2 * G):
                    f_al_(Turn(2 * G * j + i, i % 2, 0))
                    if last and i > G:
                        f_power(i - G - 1)
                    if i == 1:
                        f_wl_(2 * j + 1, 1)
                    if i == G + 1 and not last:
                        f_wl_(2 * j + 2, 0)

            def f_power(g):
                for b in range(TG * g, TG * (g + 1)):
                    ln_power(F_)(turn(b))

            f_wl_(0, 0)
            pipelined(pool, [(copy_x(F_, E_), 0)])
            f_low(0)
            with pool.Fori(1, NE // 2 - 1) as j:
                f_low(j)
            f_low(NE // 2 - 1, True)
            f_power(G - 1)

        @block.tensor
        def _(pe):
            def turn_x(round, free=None):
                tu = turned.again(XT[round])
                def stage(t):
                    wait(pe, copied.again(XT[round]), t, 1)
                    wait(pe, xt_done.again(XT[round]), t, 1, back=1)
                    if free is not None and t.peeled:
                        free(t)
                    for k in range(KC):
                        m = pe.transpose(bank[0][:, k * P:(k + 1) * P], xs[t.p][:, k * P:(k + 1) * P], ident)
                    m.then_inc(tu.sem, 1)
                return stage

            def product(o, lhs, rhs):
                n = len(lhs)
                for k in range(n):
                    m = pe.matmul(o, lhs[k], rhs[k], start=k == 0, stop=k == n - 1)
                return m

            def split_product(o, lhs, rhs, last=True):
                n = len(lhs)
                for k in range(n):
                    for i, (x_, y_) in enumerate(((0, 0), (0, 1), (1, 0))):
                        mm = pe.matmul(o, lhs[k][x_], rhs[k][y_], start=k + i == 0, stop=last and k == n - 1 and i == 2)
                return mm

            def transposes(o, src, n, width):
                for k in range(n):
                    m = pe.transpose(o[:, k * width:(k + 1) * width], src(k), ident[0:width, 0:width])
                return m

            pe.wait_ge(l_aw, 16)

            def a_qkp_(t):
                pe.wait_ge(l_inT[t.p], 16 * (t.half + 1))
                wait(pe, a_qkb, t, 1, back=1)
                product(bank[1][:, 0:2 * D], [inT[t.p][:, k, :] for k in range(KC)],
                        [a_w[:, k, 0:2 * D] for k in range(KC)]).then_inc(a_qkp.sem, 1)

            def a_vp_(t):
                wait(pe, a_vb, t, 1, back=1)
                product(bank[2][:, 0:D], [inT[t.p][:, k, :] for k in range(KC)],
                        [a_w[:, k, 2 * D:3 * D] for k in range(KC)]).then_inc(a_vp.sem, 1)

            def a_kv_(t):
                if t.peeled and t.b == 0:
                    pe.wait_ge(l_const, 16)
                wait(pe, a_relu, t, 2)
                wait(pe, a_kvm, t, 2, back=1)
                wait(pe, a_vb, t, 1)
                for h in range(KC):
                    m = pe.matmul(bank[3][:, h * VW:(h + 1) * VW], a_f[t.p][:, D + h * P:D + (h + 1) * P],
                                  a_v[t.p][:, h, :], start=True, stop=True)
                m.then_inc(a_kvp.sem, 1)
                wait(pe, a_fTc, t, 1, back=1)
                transposes(bank[4], lambda k: a_f[t.p][:, k * P:(k + 1) * P], KC, P).then_inc(a_fTp.sem, 1)

            def a_nd_(t):
                wait(pe, a_kvm, t, 2)
                wait(pe, a_fTc, t, 1)
                wait(pe, a_div, t, 3, back=1)
                for h in range(KC):
                    m = pe.matmul(bank[5][:, h * NW:(h + 1) * NW], a_fT[t.p][:, h, :], a_kv[t.p][:, h, :],
                                  start=True, stop=True)
                m.then_inc(a_nd.sem, 1)

            def a_atp_(t):
                wait(pe, a_div, t, 3)
                wait(pe, a_atc, t, 1, back=1)
                transposes(bank[6], lambda k: a_at[t.p][:, k * P:(k + 1) * P], KC, P).then_inc(a_atp.sem, 1)

            def a_op_(t):
                if t.peeled and t.b == 0:
                    pe.wait_ge(l_awo, 16)
                wait(pe, a_atc, t, 1)
                wait(pe, a_ob, t, 1, back=1)
                product(bank[7][:, 0:D], [a_atT[t.p][:, k, :] for k in range(KC)],
                        [a_wout[:, k, :] for k in range(KC)]).then_inc(a_op.sem, 1)

            pipelined(pe, [(a_nd_, 4), (a_kv_, 3), (a_qkp_, 0), (a_atp_, 4), (a_vp_, 1), (a_op_, 4)])

            pe.wait_ge(l_bw, 64)
            wait_end(pe, a_vb)
            for n, (o, wl, wr) in enumerate(((bank[1], b_wq, b_wk), (bank[2], b_wv, b_wp))):
                for k in range(KC):
                    m = product(o[:, k * D:(k + 1) * D], [wl[:, e, k * P:(k + 1) * P] for e in range(KC)],
                                [wr[:, e, :] for e in range(KC)])
                m.then_inc(b_fold.sem, 1)

            def b_q_(t):
                wait(pe, xt_done.again(XT[B_]), t, 1)
                wait(pe, b_qc, t, 1, back=1)
                if t.peeled and t.b == 0:
                    wait_end(pe, b_folded)
                for k in range(KC):
                    m = product(bank[1][:, k * P:(k + 1) * P], [b_A[:, j, k * P:(k + 1) * P] for j in range(KC)],
                                [xT[t.p][:, j, :] for j in range(KC)])
                m.then_inc(b_qp.sem, 1)

            def b_v_(t):
                pe.wait_ge(l_inT[t.p], 16 * (B // 2 + t.half + 1))
                wait(pe, b_vc, t, 1, back=1)
                product(bank[2][:, 0:D], [inT[t.p][:, k, :] for k in range(KC)],
                        [b_B[:, k, :] for k in range(KC)]).then_inc(b_vp.sem, 1)

            def b_s_(t):
                pe.wait_ge(l_inT[t.p], 16 * (B // 2 + t.half + 1))
                wait(pe, b_qc, t, 1)
                wait(pe, b_max, t, 1, back=1)
                if t.peeled and t.b == 0:
                    wait_end(pe, a_kvm)
                product(bank[3][:, 0:P], [b_qT[t.p][:, k, :] for k in range(KC)],
                        [inT[t.p][:, k, :] for k in range(KC)]).then_inc(b_sp.sem, 1)

            def b_pT_(t):
                wait(pe, b_exp, t, 1)
                wait(pe, b_pTc, t, 2, back=1)
                if t.peeled and t.b == 0:
                    wait_end(pe, a_fTc)
                pe.transpose(bank[4][:, 0:P], b_p[t.p], ident).then_inc(b_pTp.sem, 1)

            def b_y_(t):
                wait(pe, b_pTc, t, 2)
                wait(pe, b_vc, t, 1)
                wait(pe, b_y, t, 1, back=1)
                if t.peeled and t.b == 0:
                    wait_end(pe, a_div)
                pe.matmul(bank[5][:, 0:D], b_pT[t.p], b_v[t.p], start=True, stop=True).then_inc(b_yp.sem, 1)

            pipelined(pe, [(b_pT_, 3), (b_s_, 2), (turn_x(B_), 0), (b_q_, 1), (b_v_, 2), (b_y_, 3)])

            def c_w_(t):
                wait(pe, xt_done.again(XT[C_]), t, 1)
                wait(pe, c_wc, t, 1, back=1)
                if t.peeled and t.b == 0:
                    pe.wait_ge(c_prep, 4)
                    wait_end(pe, b_qc)
                product(bank[1][:, 0:P], [c_rw[:, k, :] for k in range(KC)],
                        [xT[t.p][:, k, :] for k in range(KC)]).then_inc(c_wp.sem, 1)

            pipelined(pe, [(turn_x(C_), 0), (c_w_, 1)])

            def c_gather_(g):
                def stage(t):
                    first, last = t.peeled and t.b == TSEQ * g, t.peeled and t.b == TSEQ * (g + 1) - 1
                    if first:
                        wait_end(pe, b_y)
                        wait_end(pe, a_ob)
                    m = 3 if not t.peeled else min(t.b, 3)
                    wait(pe, c_hot, t, 1)
                    wait(pe, c_Uc, t, 1, back=1)
                    pe.matmul(bank[3][:, 0:S], c_mask[:, m, :], c_E[t.p][:, 0:S], start=True, stop=True)\
                      .then_inc(c_Up.sem, 1)
                    wait(pe, c_ETc, t, 1, back=1)
                    pe.transpose(bank[5][0:S, 0:P], c_E[t.p][:, 0:S], ident).then_inc(c_ETp.sem, 1)
                    pe.matmul(bank[2 + 4 * g][0:S, 0:XW], c_E[t.p][:, 0:S], X[:, t.b, :],
                              start=first, stop=last).then_inc(c_gp.sem, 1)
                return stage

            def c_masks_(g):
                def stage(t):
                    first, last = t.peeled and t.b == TSEQ * g, t.peeled and t.b == TSEQ * (g + 1) - 1
                    wait(pe, c_Uc, t, 1)
                    pe.matmul(bank[4 + 3 * g][0:S, 0:S], c_U[t.p][:, 0:S], c_E[t.p][:, 0:S],
                              start=first, stop=last).then_inc(c_mp.sem, 1)
                return stage

            for g in range(TILES):
                pipelined(pe, [(c_masks_(g), 2), (c_gather_(g), 1)], TSEQ * g, TSEQ * (g + 1), peel=4)

            pe.wait_ge(l_cw, 96)
            tiles = [(g, turn(g)) for g in range(TILES)]
            for g, t in tiles:
                pe.wait_ge(c_dve, dve_at(1, g))
                if g == 0:
                    wait_end(pe, xt_done.again(XT[C_]))
                    wait_end(pe, c_wc)
                for k in range(KC):
                    m = pe.transpose(bank[g][:, k * S:(k + 1) * S], c_hn[g][0:S, k * P:(k + 1) * P], ident[0:S, 0:S])
                m.then_inc(c_pe, 1)
            for g, t in tiles:
                pe.wait_ge(c_act, act_at(1, g))
                if g == 0:
                    pe.wait_ge(c_dve, dve_at(0, 1))
                    wait_end(pe, c_Uc)
                    wait_end(pe, c_ETc)
                lhs = [c_hT[:, k, g * S:(g + 1) * S] for k in range(KC)]
                product(bank[2 + g][0:S, 0:2 * D], lhs, [c_wqkv[:, k, 0:2 * D] for k in range(KC)])\
                    .then_inc(c_pe, 1)
            for g, t in tiles:
                lhs = [c_hT[:, k, g * S:(g + 1) * S] for k in range(KC)]
                product(bank[4 + g][0:S, 0:D], lhs, [c_wqkv[:, k, 2 * D:3 * D] for k in range(KC)])\
                    .then_inc(c_pe, 1)
            for g, t in tiles:
                pe.wait_ge(c_dve, dve_at(4, g))
                for k in range(2 * KC):
                    m = pe.transpose(bank[6 + g][:, k * S:(k + 1) * S], c_z[g][0:S, k * P:(k + 1) * P], ident[0:S, 0:S])
                m.then_inc(c_pe, 1)
            for g, t in tiles:
                pe.wait_ge(c_act, act_at(3, g))
                pe.wait_ge(c_dve, keys_at(g))
                if g == 0:
                    pe.wait_ge(c_dve, dve_at(3, 1))
                    pe.wait_ge(c_act, act_at(2, 1))
                else:
                    pe.wait_ge(c_act, act_at(3, 1))
                for r in range(NQ):
                    m = pe.matmul(bank[4 * g + r][0:S, 0:QH * S], c_qT[g][:, r // 2, :],
                                  c_kexp[:, QH * r:QH * (r + 1), :].rearrange("p a b -> p (a b)"),
                                  start=True, stop=True)
                m.then_inc(c_pe, 1)
            for g, t in tiles:
                pe.wait_ge(c_act, act_at(4, g))
                for r in range(NQ):
                    for i in range(QH):
                        m = pe.transpose(bank[4 * g + r][0:S, i * S:(i + 1) * S], c_S[g][0:S, QH * r + i, :],
                                         ident[0:S, 0:S])
                m.then_inc(c_pe, 1)
                pe.wait_ge(c_act, act_at(5, g))
                for h in range(H):
                    m = pe.matmul(bank[4 * g][0:S, h * HV:(h + 1) * HV], c_pT[g][0:S, h, :], c_v[g][0:S, h, :],
                                  start=True, stop=True)
                m.then_inc(c_pe, 1)
            for g, t in tiles:
                pe.wait_ge(c_dve, dve_at(10, g))
                for k in range(KC):
                    m = pe.transpose(bank[4 * g + 1][:, k * S:(k + 1) * S], c_at[g][0:S, k * P:(k + 1) * P],
                                     ident[0:S, 0:S])
                m.then_inc(c_pe, 1)
            for g, t in tiles:
                pe.wait_ge(c_act, act_at(6, g))
                product(bank[4 * g + 2][0:S, 0:D], [c_oT[g][:, k, :] for k in range(KC)],
                        [c_wo[:, k, :] for k in range(KC)]).then_inc(c_pe, 1)
            for g, t in tiles:
                pe.wait_ge(c_dve, dve_at(12, g))
                for k in range(KC):
                    m = pe.transpose(bank[4 * g + 3][:, k * S:(k + 1) * S], c_hn[g][0:S, k * P:(k + 1) * P],
                                     ident[0:S, 0:S])
                m.then_inc(c_pe, 1)
            pe.wait_ge(c_act, act_at(8, 1))
            for q in range(FC // 2):
                o = bank[(0, 1, 4, 5)[q]]
                for i in range(2):
                    f = 2 * q + i
                    m = product(o[:, i * TILES * S:(i + 1) * TILES * S],
                                [c_w1[:, k, f * P:(f + 1) * P] for k in range(KC)],
                                [c_hT[:, k, :] for k in range(KC)])
                m.then_inc(c_fp.sem, 1)
            wait_end(pe, c_gelu)
            for g, t in tiles:
                product(bank[4 * g + 2][0:S, 0:D], [c_gT[:, f, g * S:(g + 1) * S] for f in range(FC)],
                        [c_w2[:, f, :] for f in range(FC)]).then_inc(c_pe, 1)

            def c_scatter_(g):
                def stage(t):
                    wait(pe, c_etsc, t, 1)
                    wait(pe, c_y, t, 1, back=2)
                    if t.peeled and t.b == TSEQ * g:
                        pe.wait_ge(c_dve, dve_at(14, 1))
                    pe.matmul(bank[t.p][:, 0:D], c_ets[t.p][0:S], c_proc[0:S, g, :], start=True, stop=True)\
                      .then_inc(c_sp.sem, 1)
                return stage

            for g in range(TILES):
                pipelined(pe, [(c_scatter_(g), 0)], TSEQ * g, TSEQ * (g + 1), peel=2)

            rounds = []
            for n, round in enumerate((D_, E_)):
                def weight(i, n=n):
                    return d_w[n][:, :, i * D:(i + 1) * D]

                def bank0_free(t, n=n):
                    if n == 0 and t.b == 0:
                        wait_end(pe, c_y)

                def d_turn_(t, n=n, round=round):
                    wait(pe, d_atc.again(n), t, 1, back=4)
                    turn_x(round, bank0_free)(t)

                def d_proj_(t, n=n, round=round, weight=weight):
                    wait(pe, xt_done.again(XT[round]), t, 1)
                    wait(pe, d_qkc.again(n), t, 4, back=1)
                    if t.peeled and t.b == 0:
                        pe.wait_ge(l_dw[n], 16 if n == 0 else 32)
                    x_ = xT[t.p]
                    src = x_ if n == 0 else inT[t.p]
                    wq, wk = weight(0), weight(1)
                    for k in range(KC):
                        product(bank[1][:, k * P:(k + 1) * P], [wq[:, j, k * P:(k + 1) * P] for j in range(KC)],
                                [x_[:, j, :] for j in range(KC)])
                    if n == 1:
                        pe.wait_ge(l_inT[t.p], 16 * (2 * (B // 2) + t.half + 1))
                    for k in range(KC):
                        m = product(bank[1][:, D + k * P:D + (k + 1) * P],
                                    [wk[:, j, k * P:(k + 1) * P] for j in range(KC)],
                                    [src[:, j, :] for j in range(KC)])
                    m.then_inc(d_qkp.sem, 1)

                def d_v_(t, n=n, weight=weight):
                    src = xT[t.p] if n == 0 else inT[t.p]
                    wait(pe, d_vc.again(n), t, 1, back=1)
                    wait(pe, d_y.again(n), t, 1, back=3)
                    product(bank[2][:, 0:D], [src[:, j, :] for j in range(KC)],
                            [weight(2)[:, j, :] for j in range(KC)]).then_inc(d_vp.sem, 1)

                def d_scores_(r, n=n):
                    def stage(t):
                        if r % 2 == 0:
                            wait(pe, d_lo.again(n), t, 2)
                            wait(pe, d_kx.again(n), t, 2 * (r // 2 + 1))
                        if r < 2:
                            wait(pe, d_max.again(n), t, 2 * (NQ + r - 1), back=1)
                        else:
                            wait(pe, d_max.again(n), t, 2 * (r - 1))
                        o = bank[3 + r % 2]
                        m = split_product(o[:], [[v[t.p][:, r // 2, :] for v in (d_qh, d_ql)]],
                                          [[v[t.p][:, QH * r:QH * (r + 1), :].rearrange("p a b -> p (a b)")
                                            for v in (d_xh, d_xl)]], last=n == 0)
                        if n == 1:
                            m = pe.matmul(o[:].rearrange("p (a b) -> p a b", a=QH), ident_bf[:],
                                          causal_bf[:].unsqueeze(1).to_broadcast([P, QH, P]), start=False, stop=True)
                        m.then_inc(d_sp.sem, 1)
                    return stage

                def d_pT_(r, n=n):
                    def stage(t):
                        wait(pe, d_exp.again(n), t, r + 1)
                        if r < 2:
                            wait(pe, d_pTc.again(n), t, NQ + r - 1, back=1)
                        else:
                            wait(pe, d_pTc.again(n), t, r - 1)
                        for i in range(QH):
                            m = pe.transpose(bank[5 + r % 2][:, i * P:(i + 1) * P], d_S[t.p][:, QH * r + i, :], ident)
                        m.then_inc(d_pTp.sem, 1)
                    return stage

                def d_pv_(r, n=n):
                    def stage(t):
                        wait(pe, d_pTc.again(n), t, r + 1)
                        if r == 0:
                            wait(pe, d_vc.again(n), t, 1)
                            wait(pe, d_div.again(n), t, 2, back=1)
                        for h in range(QH * r, QH * (r + 1)):
                            m = pe.matmul(bank[7][:, h * HV:(h + 1) * HV], d_pT[t.p][:, h, :], d_v[t.p][:, h, :],
                                          start=True, stop=True)
                        m.then_inc(d_pv.sem, 1)
                    return stage

                def d_atp_(t, n=n, round=round):
                    wait(pe, d_div.again(n), t, 2)
                    wait(pe, d_atc.again(n), t, 1, back=1)
                    if n == 1 and t.peeled and t.b + 3 >= B:
                        wait_end(pe, xt_done.again(XT[round]))
                    else:
                        wait(pe, xt_done.again(XT[round]), Turn(t.b + 3, 0, 0), 1)
                    transposes(bank[0][:, D:2 * D], lambda k: d_at[t.p][:, k * P:(k + 1) * P], KC, P)\
                        .then_inc(d_atp.sem, 1)

                def d_out_(t, n=n, weight=weight):
                    wait(pe, d_atc.again(n), t, 1)
                    wait(pe, d_y.again(n), t, 1, back=1)
                    if n == 1 and t.peeled and t.b + 2 >= B:
                        wait_end(pe, d_vc.again(n))
                    else:
                        wait(pe, d_vc.again(n), Turn(t.b + 2, 0, 0), 1)
                    product(bank[2][:, D:2 * D], [d_atT[t.p][:, k, :] for k in range(KC)],
                            [weight(3)[:, k, :] for k in range(KC)]).then_inc(d_op.sem, 1)

                rounds.append([(d_turn_, 0), (d_proj_, 1), (d_scores_(0), 2), (d_pv_(0), 3), (d_scores_(1), 2),
                               (d_pv_(1), 3), (d_scores_(2), 2), (d_pv_(2), 3), (d_pv_(3), 3), (d_scores_(3), 2),
                               (d_pT_(0), 2), (d_atp_, 3), (d_v_, 1), (d_pT_(1), 2), (d_pT_(2), 2),
                               (d_out_, 3), (d_pT_(3), 2)])
            chained(pe, rounds)

            def f_lg_(t):
                wait(pe, xt_done.again(XT[F_]), t, 1)
                wait(pe, f_lc, t, 1, back=2)
                product(bank[1 + t.p][:, 0:E], [xT[t.p][:, k, :] for k in range(KC)],
                        [f_rw[:, k, :] for k in range(KC)]).then_inc(f_lp.sem, 1)

            def f_turn_(t):
                if t.peeled and t.b == 0:
                    wait_end(pe, d_atc.again(1))
                    wait_end(pe, d_y.again(1))
                turn_x(F_)(t)

            pipelined(pe, [(f_turn_, 0), (f_lg_, 1)])
            wait_end(pe, f_xlc)
            wait_end(pe, f_lc)
            wait_end(pe, d_y.again(1))

            def f_up(m, p, g, e):
                if g == 0:
                    pe.wait_ge(f_wlc.sem, e + 1)
                for c_ in range(KC):
                    for i in range(2):
                        wait(pe, f_silu if i == 0 else f_mul, m, c_ + 1, back=1)
                        cut = slice(c_ * P, (c_ + 1) * P)
                        split_product(bank[2 * i + c_][:],
                                      [[w[p][:, i * KC + k, cut] for w in (f_wh, f_wl)] for k in range(KC)],
                                      [[x_[:, k, g * GT:(g + 1) * GT] for x_ in (f_xh, f_xl)] for k in range(KC)])\
                            .then_inc(f_hp.sem, 1)

            def f_down(m, p):
                for q in range(2):
                    wait(pe, f_alc, m, 2)
                    wait(pe, f_acc, m, 2 * q + 2, back=2)
                    for i in range(2):
                        s0 = (2 * q + i) * P
                        mm = split_product(bank[4 + 2 * m.p + q][:, i * D:(i + 1) * D],
                                           [[v[m.p][:, k, s0:s0 + P] for v in (f_ah, f_al)] for k in range(KC)],
                                           [[w[p][:, 2 * KC + k, :] for w in (f_wh, f_wl)] for k in range(KC)])
                    mm.then_inc(f_dp.sem, 1)

            def pair(j):
                for i in range(2 * G):
                    g, p = i % G, i // G
                    f_up(Turn(2 * G * j + i, i % 2, 0), p, g, 2 * j + p)
                    if i or not isinstance(j, int):
                        f_down(Turn(2 * G * j + i - 1, (i - 1) % 2, 0), (i - 1) // G % 2)

            pair(0)
            with pe.Fori(1, NE // 2) as j:
                pair(j)
            f_down(turn(MT - 1), 1)

        @block.scalar
        def _(act):
            act.dma_start(a_w, a["a_w"]).then_inc(l_aw, 16)
            first = ROWS["gk"].stop
            act.dma_start(rows[:, 0:first], a["rows"][0:first].partition_broadcast(P)).then_inc(l_rows, 16)
            act.dma_start(a_wout, a["a_wout"]).then_inc(l_awo, 16)
            act.dma_start(rows[:, first:], a["rows"][first:].partition_broadcast(P)).then_inc(l_rest, 16)
            act.dma_start(cols[:], a["cols"]).then_inc(l_rest, 16)

            def copy_xT(round, before, reader):
                xd = xt_done.again(XT[round])
                def stage(t):
                    wait(act, turned.again(XT[round]), t, 1)
                    if t.peeled and t.b < 2:
                        if round == E_:
                            wait(act, before, t, 1, back=2)
                        elif before is not None:
                            wait_end(act, before)
                    else:
                        wait(act, reader, t, 1, back=2)
                    if round == F_:
                        wait(act, f_xlc, t, 1, back=2)
                    act.copy(xT[t.p][:], bank[0][:, 0:D].rearrange("p (k t) -> p k t", k=KC)).then_inc(xd.sem, 1)
                return stage

            def a_sq_(t):
                wait(act, a_qkb, t, 1)
                wait(act, a_rms, t, 2, back=2)
                for i in range(2):
                    act.activation(a_sqs[t.p][:, i, :], a_qk[t.p][:, i * D:(i + 1) * D], ACT.Square, scale=D ** -0.5,
                                   accum_out=a_ms[t.p][:, i:i + 1]).then_inc(a_sq.sem, 1)

            def a_relu_(t):
                wait(act, a_rope, t, 1)
                wait(act, a_rms, t, 2)
                wait(act, a_kvp, t, 1, back=2)
                wait(act, a_fTp, t, 1, back=2)
                for i in range(2):
                    act.activation(a_f[t.p][:, i * D:(i + 1) * D], a_u[t.p][:, i * D:(i + 1) * D], ACT.Relu,
                                   scale=a_r[t.p][:, i:i + 1]).then_inc(a_relu.sem, 1)

            def a_fTc_(t):
                wait(act, a_fTp, t, 1)
                wait(act, a_nd, t, 1, back=2)
                act.copy(a_fT[t.p], bank[4][:, 0:D].rearrange("p (k t) -> p k t", k=KC)).then_inc(a_fTc.sem, 1)

            def a_atc_(t):
                wait(act, a_atp, t, 1)
                wait(act, a_op, t, 1, back=2)
                act.copy(a_atT[t.p], bank[6][:, 0:D].rearrange("p (k t) -> p k t", k=KC)).then_inc(a_atc.sem, 1)

            def a_osq_(t):
                wait(act, a_ob, t, 1)
                wait(act, a_orms, t, 1, back=2)
                act.activation(a_sqs[t.p][:, 2, :], a_o[t.p], ACT.Square, scale=D ** -0.5,
                               accum_out=a_oms[t.p]).then_inc(a_osq.sem, 1)

            pipelined(act, [(a_osq_, 5), (a_fTc_, 3), (a_sq_, 1), (a_relu_, 2), (a_atc_, 4)])

            act.wait_ge(b_fold.sem, 1)
            act.mul(b_A, bank[1][:].rearrange("p (k n) -> p k n", k=KC), SCALE).then_inc(b_folded.sem, 1)
            act.wait_ge(b_fold.sem, 2)
            act.copy(b_B, bank[2][:].rearrange("p (k n) -> p k n", k=KC)).then_inc(b_folded.sem, 1)

            def b_qc_(t):
                wait(act, b_qp, t, 1)
                wait(act, b_sp, t, 1, back=2)
                act.copy(b_qT[t.p], bank[1][:, 0:D].rearrange("p (k t) -> p k t", k=KC)).then_inc(b_qc.sem, 1)

            def b_exp_(t):
                wait(act, b_max, t, 1)
                wait(act, b_pTp, t, 1, back=2)
                wait(act, b_pTc, t, 1, back=2)
                act.activation(b_p[t.p], b_s[t.p], ACT.Exp, bias=b_nmax[t.p], scale=-1.0,
                               accum_out=b_sum[t.p]).then_inc(b_exp.sem, 1)

            pipelined(act, [(copy_xT(B_, None, b_qp), 0), (b_qc_, 1), (b_exp_, 2)])

            def c_U_(t):
                wait(act, c_Up, t, 1)
                wait(act, c_mp, t, 1, back=2)
                act.copy(c_U[t.p][:, 0:S], bank[3][:, 0:S]).then_inc(c_Uc.sem, 1)
                wait(act, c_ETp, t, 1)
                act.copy(c_ET[0:S, t.b, :], bank[5][0:S, 0:P]).then_inc(c_ETc.sem, 1)

            def c_wc_(t):
                wait(act, c_wp, t, 1)
                wait(act, c_cnt, t, 4, back=2)
                act.activation(c_wr[t.p], bank[1][:, 0:P], ACT.Identity, bias=row("router_b")).then_inc(c_wc.sem, 1)

            pipelined(act, [(copy_xT(C_, b_qp, c_wp), 0), (c_wc_, 1)])
            pipelined(act, [(c_U_, 0)])

            tiles = range(TILES)
            for g in tiles:
                act.wait_ge(c_dve, dve_at(0, g))
                act.activation(c_sqs[g][0:S, 0, :], c_sel[g][0:S, 0:D], ACT.Square, scale=D ** -0.5,
                               accum_out=c_st[g][0:S, 0:1]).then_inc(c_act, 1)
            for g in tiles:
                act.wait_ge(c_pe, pe_at(0, g))
                act.copy(c_hT[:, :, g * S:(g + 1) * S], bank[g][:, 0:KC * S].rearrange("p (k t) -> p k t", k=KC))\
                   .then_inc(c_act, 1)
            for g in tiles:
                act.wait_ge(c_dve, dve_at(2, g))
                act.activation(c_cs[g][0:S, 0:2, :], c_arg[g][0:S], ACT.Sin)
                act.wait_ge(c_pe, pe_at(2, g))
                act.copy(c_v[g][0:S, :, 0:HD], bank[4 + g][0:S, 0:D].rearrange("p (h d) -> p h d", h=H))\
                   .then_inc(c_act, 1)
            for g in tiles:
                act.wait_ge(c_pe, pe_at(3, g))
                act.mul(c_qT[g], bank[6 + g][:, 0:KC * S].rearrange("p (k t) -> p k t", k=KC), SCALE)\
                   .then_inc(c_act, 1)
            for g in tiles:
                act.wait_ge(c_dve, dve_at(9, g))
                act.activation(c_S[g][0:S], c_S[g][0:S], ACT.Exp).then_inc(c_act, 1)
                act.wait_ge(c_pe, pe_at(5, g))
                for r in range(NQ):
                    m = act.copy(c_pT[g][0:S, QH * r:QH * (r + 1), :],
                                 bank[4 * g + r][0:S, 0:QH * S].rearrange("p (a b) -> p a b", a=QH))
                m.then_inc(c_act, 1)
            for g in tiles:
                act.wait_ge(c_pe, pe_at(7, g))
                act.copy(c_oT[g], bank[4 * g + 1][:, 0:KC * S].rearrange("p (k t) -> p k t", k=KC))\
                   .then_inc(c_act, 1)
            for g in tiles:
                act.wait_ge(c_dve, dve_at(11, g))
                act.activation(c_sqs[g][0:S, 1, :], c_x1[g][0:S], ACT.Square, scale=D ** -0.5, accum_out=c_st[g][0:S, 2:3])\
                   .then_inc(c_act, 1)
            for g in tiles:
                act.wait_ge(c_pe, pe_at(9, g))
                act.copy(c_hT[:, :, g * S:(g + 1) * S],
                         bank[4 * g + 3][:, 0:KC * S].rearrange("p (k t) -> p k t", k=KC)).then_inc(c_act, 1)
            for q in range(FC // 2):
                act.wait_ge(c_fp.sem, q + 1)
                act.activation(c_gT[:, 2 * q:2 * q + 2, :],
                               bank[(0, 1, 4, 5)[q]][:, 0:2 * TILES * S].rearrange("p (a b) -> p a b", a=2),
                               ACT.Gelu_apprx_tanh).then_inc(c_gelu.sem, 1)

            act.wait_ge(d_prep, 3)
            rounds = []
            for n, round in enumerate((D_, E_)):
                def d_qkc_(t, n=n):
                    qk = d_qkc.again(n)
                    wait(act, d_qkp.again(n), t, 1)
                    wait(act, d_lo.again(n), t, 2, back=2)
                    for k in range(KC):
                        act.activation(d_kT[t.p][:, k, :], bank[1][:, D + k * P:D + (k + 1) * P], ACT.Identity,
                                       bias=cols[:, KC + k:KC + k + 1] if n == 0 else 0.0).then_inc(qk.sem, 1)
                    for k in range(KC):
                        act.activation(d_qT[t.p][:, k, :], bank[1][:, k * P:(k + 1) * P], ACT.Identity, scale=SCALE,
                                       bias=d_bq[:, k:k + 1] if n == 0 else 0.0).then_inc(qk.sem, 1)

                def d_hi_(t, n=n):
                    wait(act, d_qkc.again(n), t, KC)
                    wait(act, d_kx.again(n), t, 2 * KC, back=2)
                    act.copy(d_kh[t.p][:], d_kT[t.p]).then_inc(d_hi.sem, 1)
                    wait(act, d_qkc.again(n), t, 2 * KC)
                    wait(act, d_sp.again(n), t, NQ, back=2)
                    act.copy(d_qh[t.p][:], d_qT[t.p]).then_inc(d_hi.sem, 1)

                def d_exp_(r, n=n):
                    def stage(t):
                        wait(act, d_max.again(n), t, 2 * r + 2)
                        v = d_S[t.p][:, QH * r:QH * (r + 1), :]
                        act.activation(v, v, ACT.Exp).then_inc(d_exp.sem, 1)
                    return stage

                def d_pTc_(r, n=n):
                    def stage(t):
                        wait(act, d_pTp.again(n), t, r + 1)
                        wait(act, d_pv.again(n), t, NQ, back=2)
                        act.copy(d_pT[t.p][:, QH * r:QH * (r + 1), :],
                                 bank[5 + r % 2][:].rearrange("p (a b) -> p a b", a=QH)).then_inc(d_pTc.sem, 1)
                    return stage

                def d_atc_(t, n=n):
                    wait(act, d_atp.again(n), t, 1)
                    wait(act, d_op.again(n), t, 1, back=2)
                    act.copy(d_atT[t.p], bank[0][:, D:2 * D].rearrange("p (k t) -> p k t", k=KC))\
                       .then_inc(d_atc.sem, 1)

                reader = d_vp.again(n) if n == 0 else d_qkp.again(n)
                before = c_wp if n == 0 else d_vp.again(1)
                def d_xs_(t, round=round):
                    wait(act, normed.again(round - 1), t, 1)
                    wait(act, turned.again(XT[round]), t, 1, back=2)
                    act.copy(xs[t.p][:], X[:, t.b, 0:D]).then_inc(copied.sem, 1)

                rounds.append([(copy_xT(round, before, reader), 1), (d_qkc_, 2), (d_hi_, 2), (d_exp_(0), 3),
                               (d_exp_(1), 3), (d_xs_, 0), (d_exp_(2), 3), (d_pTc_(0), 3), (d_atc_, 4),
                               (d_pTc_(1), 3), (d_exp_(3), 3), (d_pTc_(2), 3), (d_pTc_(3), 3)])
            chained(act, rounds)

            def f_wh_(e, p):
                act.wait_ge(l_ew[p], 8 * (e - p) + 16)
                if isinstance(e, int) and e == 0:
                    wait_end(act, d_sp.again(1))
                if not isinstance(e, int) or e >= 2:
                    act.wait_ge(f_dp.sem, f_dp.n * G * (e - 1))
                act.copy(f_wh[p][:], f_ws[p]).then_inc(f_whc.sem, 1)

            f_wh_(0, 0)

            def f_xh_(t):
                wait(act, xt_done.again(XT[F_]), t, 1)
                act.copy(f_xh[:].rearrange("p k (b t) -> p k b t", b=B)[:, :, t.b, :], xT[t.p][:])\
                    .then_inc(f_xhc.sem, 1)

            pipelined(act, [(copy_xT(F_, d_qkp.again(1), f_lp), 0), (f_xh_, 1)])
            wait_end(act, f_lc)
            act.activation(f_sc, f_lg, ACT.Sigmoid).then_inc(f_sig, 1)

            def f_silu_(m):
                for c_ in range(KC):
                    wait(act, f_hp, m, 2 * c_ + 1)
                    wait(act, f_mul, m, c_ + 1, back=1)
                    act.activation(f_h[c_], bank[c_][:], ACT.Silu).then_inc(f_silu.sem, 1)

            def f_ah_(m):
                for c_ in range(KC):
                    wait(act, f_mul, m, c_ + 1)
                    wait(act, f_dp, m, 2, back=2)
                    act.copy(f_ah[m.p][:, c_, :], f_a[m.p][:, c_, :]).then_inc(f_ahc.sem, 1)

            def f_high(j, last=False):
                for i in range(2 * G):
                    m = Turn(2 * G * j + i, i % 2, 0)
                    f_silu_(m)
                    f_ah_(m)
                    if i == 1:
                        f_wh_(2 * j + 1, 1)
                    if i == G + 1 and not last:
                        f_wh_(2 * j + 2, 0)

            f_high(0)
            with act.Fori(1, NE // 2 - 1) as j:
                f_high(j)
            f_high(NE // 2 - 1, True)

        @block.vector
        def _(dve):
            def ln_stats(round):
                def stage(t):
                    ln_bn(round)(t)
                    ln_aggr(round)(t)
                return stage

            def ln_bn(round):
                def stage(t):
                    if round == A_:
                        wait(dve, a_y, t, 2)
                    if round == C_:
                        wait(dve, c_y, t, 1)
                    dve.bn_stats(bn[t.p][:], y[t.p][:]).then_inc(stats.sem, 1)
                return stage

            def ln_aggr(round):
                st = stats.again(round)
                def stage(t):
                    wait(dve, rstd.again(round), t, 1, back=2)
                    wait(dve, st, t, 1)
                    hold(dve)
                    dve.bn_aggr(mv[t.p][:], bn[t.p][:]).then_inc(st.sem, 1)
                return stage

            def ln_final(round, to=None):
                nd = normed.again(round)
                def stage(t):
                    wait(dve, rstd.again(round), t, 2)
                    o = X[:, t.b, 0:D] if to is None else to(t)
                    dve.tensor_scalar(o, y[t.p][:], mv[t.p][:, 0:1], lr[t.p][:, 1:2], ALU.subtract, ALU.mult)\
                       .then_inc(nd.sem, 1)
                return stage

            for i in range(2):
                dve.memset(a_v[i][:, :, P:VW], 1.0)
            dve.wait_ge(l_const, 16)
            dve.tensor_copy(ident_bf[:], ident)
            dve.tensor_copy(causal_bf[:], c("causal"))
            dve.wait_ge(l_rows, 16)
            for i, gain in enumerate(("gq", "gk")):
                sl = slice(i * D, (i + 1) * D)
                dve.tensor_tensor(a_cos[:, sl], c("cos"), row(gain), ALU.mult).then_inc(a_tab, 1)
                pairs = lambda v: v.rearrange("p (n two) -> p n two", two=2)
                for z in range(2):
                    dve.tensor_tensor(pairs(a_sin[:, sl])[:, :, z], pairs(c("sin"))[:, :, z],
                                      pairs(row(gain))[:, :, 1 - z], ALU.mult).then_inc(a_tab, 1)
            dve.wait_ge(a_tab, 6)

            def a_qkb_(t):
                wait(dve, a_qkp, t, 1)
                wait(dve, a_swap, t, 2, back=2)
                wait(dve, a_sq, t, 2, back=2)
                wait(dve, a_turn, t, 1, back=2)
                dve.tensor_tensor(a_qk[t.p], bank[1][:], row("bqkv")[:, 0:2 * D], ALU.add).then_inc(a_qkb.sem, 1)

            def a_vb_(t):
                wait(dve, a_vp, t, 1)
                wait(dve, a_kvp, t, 1, back=2)
                dve.tensor_tensor(a_v[t.p][:, :, 0:P], bank[2][:, 0:D].rearrange("p (k n) -> p k n", k=KC),
                                  row("bqkv")[:, 2 * D:3 * D].rearrange("p (k n) -> p k n", k=KC), ALU.add)\
                   .then_inc(a_vb.sem, 1)

            def a_rope_(t):
                wait(dve, a_turn, t, 1)
                wait(dve, a_swap, t, 2)
                dve.tensor_tensor(a_u[t.p], a_u[t.p], a_sw[t.p], ALU.add).then_inc(a_rope.sem, 1)

            def a_kvm_(t):
                wait(dve, a_kvp, t, 1)
                wait(dve, a_nd, t, 1, back=2)
                kv = bank[3][:, 0:KC * VW].rearrange("p (k n) -> p k n", k=KC)
                dve.tensor_tensor(a_kv[t.p][:, :, 0:P], kv[:, :, 0:P],
                                  c("blocks").unsqueeze(1).to_broadcast([P, KC, P]), ALU.mult).then_inc(a_kvm.sem, 1)
                dve.tensor_tensor(a_kv[t.p][:, :, P:NW], kv[:, :, P:P + 1].to_broadcast([P, KC, HH]),
                                  c("heads").unsqueeze(1).to_broadcast([P, KC, HH]), ALU.mult).then_inc(a_kvm.sem, 1)

            def a_div_(t):
                wait(dve, a_nd, t, 1)
                wait(dve, a_atp, t, 1, back=2)
                nd = bank[5][:, 0:KC * NW].rearrange("p (k n) -> p k n", k=KC)
                dve.tensor_scalar(a_den[t.p], nd[:, :, P:NW], LIN_EPS, None, ALU.add).then_inc(a_div.sem, 1)
                wait(dve, a_div, t, 1)
                dve.reciprocal(a_rden[t.p], a_den[t.p]).then_inc(a_div.sem, 1)
                wait(dve, a_div, t, 2)
                dve.tensor_tensor(a_at[t.p].rearrange("p (k h d) -> p k h d", k=KC, h=HH),
                                  nd[:, :, 0:P].rearrange("p k (h d) -> p k h d", h=HH),
                                  a_rden[t.p].unsqueeze(3).to_broadcast([P, KC, HH, HD]), ALU.mult)\
                   .then_inc(a_div.sem, 1)

            def a_ob_(t):
                if t.peeled and t.b == 0:
                    dve.wait_ge(l_rest, 32)
                wait(dve, a_op, t, 1)
                wait(dve, a_osq, t, 1, back=2)
                wait(dve, a_y, t, 1, back=2)
                dve.tensor_tensor(a_o[t.p], bank[7][:, 0:D], row("bout"), ALU.add).then_inc(a_ob.sem, 1)

            def a_y_(t):
                wait(dve, a_orms, t, 2)
                wait(dve, normed, t, 1, back=2)
                dve.scalar_tensor_tensor(out=y[t.p][:], in0=a_o[t.p], scalar=a_or[t.p][:, 1:2], in1=row("gout"),
                                         op0=ALU.mult, op1=ALU.mult).then_inc(a_y.sem, 1)

            def a_sum_(t):
                if t.peeled and t.b == 0:
                    dve.wait_ge(l_x, 16)
                wait(dve, a_y, t, 1)
                dve.tensor_tensor(y[t.p][:], y[t.p][:], X[:, t.b, 0:D], ALU.add).then_inc(a_y.sem, 1)

            pipelined(dve, [(a_ob_, 5), (ln_aggr(A_), 6), (a_div_, 4), (a_kvm_, 3), (ln_final(A_), 6),
                            (a_rope_, 2), (a_y_, 5), (a_qkb_, 0), (a_sum_, 5), (a_vb_, 1), (ln_bn(A_), 5)])

            def b_vc_(t):
                wait(dve, b_vp, t, 1)
                wait(dve, b_yp, t, 1, back=2)
                dve.tensor_copy(b_v[t.p], bank[2][:, 0:D]).then_inc(b_vc.sem, 1)

            def b_max_(t):
                wait(dve, b_sp, t, 1)
                wait(dve, b_exp, t, 1, back=2)
                hold(dve)
                dve.tensor_tensor_reduce(b_s[t.p], bank[3][:, 0:P], c("causal"), -1.0, BIG, ALU.add, ALU.min,
                                         b_nmax[t.p]).then_inc(b_max.sem, 1)

            def b_pTc_(t):
                wait(dve, b_exp, t, 1)
                wait(dve, b_y, t, 1, back=2)
                dve.reciprocal(b_rsum[t.p], b_sum[t.p]).then_inc(b_pTc.sem, 1)
                wait(dve, b_pTp, t, 1)
                wait(dve, b_yp, t, 1, back=2)
                dve.tensor_copy(b_pT[t.p], bank[4][:, 0:P]).then_inc(b_pTc.sem, 1)

            def b_y_(t):
                wait(dve, b_yp, t, 1)
                wait(dve, b_pTc, t, 1)
                wait(dve, normed.again(B_), t, 1, back=2)
                dve.scalar_tensor_tensor(out=y[t.p][:], in0=bank[5][:, 0:D], scalar=b_rsum[t.p],
                                         in1=X[:, t.b, 0:D], op0=ALU.mult, op1=ALU.add).then_inc(b_y.sem, 1)
                wait(dve, b_y, t, 1)
                ln_stats(B_)(t)

            pipelined(dve, [(b_y_, 4), (b_pTc_, 3), (b_max_, 2), (ln_final(B_), 4), (b_vc_, 2)])

            dve.wait_ge(l_cw, 96)
            dve.tensor_copy(c_rw, cols[:, COLS["router_w"]].unsqueeze(2).to_broadcast([P, KC, P])).then_inc(c_prep, 1)
            dve.tensor_scalar(c_mask, c_mask, NEG, None, ALU.max).then_inc(c_prep, 1)
            dve.tensor_copy(X[:, 0:3, D + 1:D + 2], c_posi.bitcast(I32)[:, 0:3].unsqueeze(2)).then_inc(c_prep, 1)
            dve.tensor_copy(X[:, 3:B, D + 1:D + 2],
                            c_posi.bitcast(I32)[:, 3:4].unsqueeze(2).to_broadcast([P, B - 3, 1])).then_inc(c_prep, 1)

            def c_cnt_(t):
                w = c_wr[t.p]
                col, gt, ge, tie = (c_small[t.p][:, i:i + 1] for i in range(4))
                wait(dve, c_wc, t, 1)
                wait(dve, c_kept, t, 1, back=2)
                dve.tensor_tensor_reduce(c_cmp[t.p][:, 0, :], w, ident, 1.0, 0.0, ALU.mult, ALU.add, col)\
                   .then_inc(c_cnt.sem, 1)
                wait(dve, c_cnt, t, 1)
                dve.tensor_scalar(c_cmp[t.p][:, 1, :], w, col, 0.0, ALU.is_gt, ALU.add,
                                  accum_out=gt).then_inc(c_cnt.sem, 1)
                dve.tensor_scalar(c_cmp[t.p][:, 2, :], w, col, 0.0, ALU.is_ge, ALU.add,
                                  accum_out=ge).then_inc(c_cnt.sem, 1)
                dve.scalar_tensor_tensor(out=c_cmp[t.p][:, 3, :], in0=w, scalar=col, in1=c("before"),
                                         op0=ALU.is_equal, op1=ALU.mult, accum_out=tie)\
                   .then_inc(c_cnt.sem, 1)

            pipelined(dve, [(c_cnt_, 0)])

            n_place = [0]

            def place(m):
                n_place[0] += 1
                m.then_inc(c_place, 1)
                dve.wait_ge(c_place, n_place[0])

            wait_end(dve, c_kept)
            c_col, c_gt, c_ge, c_tie = (c_counts[:, :, i] for i in range(4))
            place(dve.tensor_tensor(c_slot, c_gt, c_tie, ALU.add))
            place(dve.tensor_scalar(c_over, c_slot, SEL - 0.5, 1000.0, ALU.is_gt, ALU.mult))
            place(dve.tensor_tensor(c_slot, c_slot, c_over, ALU.add))
            place(dve.tensor_tensor(c_slot, c_slot, c("seqslot"), ALU.add))
            place(dve.tensor_scalar(keep1[:], c_ge, SEL + 0.5, 1.0, ALU.is_gt, ALU.add))
            place(dve.tensor_copy(X[:, :, D:D + 1], c_counts[:, :, 0:1]))

            def c_hot_(t):
                wait(dve, c_gp, t, 1, back=2)
                wait(dve, c_mp, t, 1, back=2)
                dve.tensor_scalar(c_E[t.p], c("slots"), c_slot[:, bass.ds(t.b, 1)], None, ALU.is_equal)\
                   .then_inc(c_hot.sem, 1)

            pipelined(dve, [(c_hot_, 0)])

            tiles = range(TILES)
            link = [0]

            def chain(m):
                link[0] += 1
                m.then_inc(c_link, 1)
                dve.wait_ge(c_link, link[0])

            def done(m):
                m.then_inc(c_dve, 1)

            for g in tiles:
                dve.memset(c_v[g][0:S, :, HD:HV], 1.0)
            for g in tiles:
                wait(dve, c_gp, turn(TSEQ * (g + 1) - 1), 1)
                chain(dve.tensor_copy(c_sel[g][0:S], bank[2 + 4 * g][0:S, 0:XW]))
                wait(dve, c_mp, turn(TSEQ * (g + 1) - 1), 1)
                done(dve.tensor_tensor(c_msk[g][0:S], bank[4 + 3 * g][0:S, 0:S], c("apart", S), ALU.add))
            for g in tiles:
                dve.wait_ge(c_pool, 2 * g + 2)
                done(dve.scalar_tensor_tensor(out=c_hn[g][0:S], in0=c_sel[g][0:S, 0:D], scalar=c_st[g][0:S, 4:5],
                                              in1=row("ln1", S), op0=ALU.mult, op1=ALU.mult))
            two_pi = [6.28125, 1.93500518798828125e-3, 3.0199159819e-7]
            for g in tiles:
                f, nf, r, r2, ov = (c_ang[g][0:S, i, :] for i in range(5))
                chain(dve.tensor_scalar(f, c("invfreq", S), c_sel[g][0:S, D + 1:D + 2], None, ALU.mult))
                chain(dve.tensor_scalar(nf, f, 1.0 / (2 * PI), MAGIC, ALU.mult, ALU.add))
                chain(dve.tensor_scalar(nf, nf, MAGIC, None, ALU.subtract))
                for part in two_pi:
                    chain(dve.scalar_tensor_tensor(out=f, in0=nf, scalar=-part, in1=f, op0=ALU.mult, op1=ALU.add))
                chain(dve.tensor_scalar(c_arg[g][0:S, 1, :], f, -PI, PI, ALU.max, ALU.min))
                chain(dve.tensor_scalar(r, f, PI / 2, None, ALU.add))
                chain(dve.tensor_scalar(ov, r, PI, -2 * PI, ALU.is_gt, ALU.mult))
                chain(dve.tensor_tensor(r, r, ov, ALU.add))
                done(dve.tensor_scalar(c_arg[g][0:S, 0, :], r, -PI, PI, ALU.max, ALU.min))
            for g in tiles:
                dve.wait_ge(c_pe, pe_at(1, g))
                done(dve.tensor_copy(c_x[g][0:S], bank[2 + g][0:S, 0:2 * D]))
            for g in tiles:
                dve.wait_ge(c_act, act_at(2, g))
                dve.wait_ge(c_dve, dve_at(3, g))
                x_ = c_x[g][0:S].rearrange("p (h z d) -> p h z d", z=2, d=8)
                z_ = c_z[g][0:S].rearrange("p (h z d) -> p h z d", z=2, d=8)
                cs = c_cs[g][0:S]
                bc = lambda v: v.unsqueeze(1).to_broadcast([S, 2 * H, 8])
                chain(dve.tensor_scalar(cs[:, 2, :], cs[:, 1, :], -1.0, None, ALU.mult))
                dve.tensor_tensor(z_[:, :, 0, :], x_[:, :, 1, :], bc(cs[:, 2, :]), ALU.mult)
                chain(dve.tensor_tensor(z_[:, :, 1, :], x_[:, :, 0, :], bc(cs[:, 1, :]), ALU.mult))
                dve.tensor_tensor(x_[:, :, 0, :], x_[:, :, 0, :], bc(cs[:, 0, :]), ALU.mult)
                chain(dve.tensor_tensor(x_[:, :, 1, :], x_[:, :, 1, :], bc(cs[:, 0, :]), ALU.mult))
                done(dve.tensor_tensor(c_z[g][0:S], c_z[g][0:S], c_x[g][0:S], ALU.add))
            for g in tiles:
                dve.wait_ge(c_act, act_at(3, g))
                if g:
                    dve.wait_ge(c_pe, pe_at(4, g - 1))
                for k in range(KC):
                    kT = bank[6 + g][:, (KC + k) * S:(KC + k + 1) * S]
                    done(dve.tensor_tensor(c_kexp[:, k * HH:(k + 1) * HH, :],
                                           kT.unsqueeze(1).to_broadcast([P, HH, S]),
                                           c("heads").unsqueeze(2).to_broadcast([P, HH, S]), ALU.mult))
            for g in tiles:
                dve.wait_ge(c_pe, pe_at(4, g))
                for r in range(NQ):
                    m = dve.tensor_tensor(c_S[g][0:S, QH * r:QH * (r + 1), :],
                                          bank[4 * g + r][0:S, 0:QH * S].rearrange("p (a b) -> p a b", a=QH),
                                          c_msk[g][0:S].unsqueeze(1).to_broadcast([S, QH, S]), ALU.add)
                done(m)
                dve.wait_ge(c_dve, dve_at(7, g))
                done(dve.tensor_reduce(c_mx[g][0:S], c_S[g][0:S], AX.X, ALU.max))
                dve.wait_ge(c_dve, dve_at(8, g))
                done(dve.tensor_tensor(c_S[g][0:S], c_S[g][0:S], c_mx[g][0:S].unsqueeze(2).to_broadcast([S, H, S]),
                                       ALU.subtract))
            for g in tiles:
                dve.wait_ge(c_pe, pe_at(6, g))
                o = bank[4 * g][0:S, 0:H * HV].rearrange("p (h d) -> p h d", h=H)
                chain(dve.reciprocal(c_rs[g][0:S], o[:, :, HD]))
                done(dve.tensor_tensor(c_at[g][0:S].rearrange("p (h d) -> p h d", h=H), o[:, :, 0:HD],
                                       c_rs[g][0:S].unsqueeze(2).to_broadcast([S, H, HD]), ALU.mult))
            for g in tiles:
                dve.wait_ge(c_pe, pe_at(8, g))
                done(dve.tensor_tensor(c_x1[g][0:S], bank[4 * g + 2][0:S, 0:D], c_sel[g][0:S, 0:D], ALU.add))
            for g in tiles:
                dve.wait_ge(c_pool, 2 * (TILES + g) + 2)
                done(dve.scalar_tensor_tensor(out=c_hn[g][0:S], in0=c_x1[g][0:S], scalar=c_st[g][0:S, 6:7],
                                              in1=row("ln2", S), op0=ALU.mult, op1=ALU.mult))
            for g in tiles:
                dve.wait_ge(c_pe, pe_at(10, g))
                done(dve.tensor_tensor(c_x1[g][0:S], bank[4 * g + 2][0:S, 0:D], c_x1[g][0:S], ALU.add))
            for g in tiles:
                dve.wait_ge(c_dve, dve_at(13, g))
                done(dve.tensor_scalar(c_proc[0:S, g, :], c_x1[g][0:S], c_sel[g][0:S, D:D + 1], None, ALU.mult))

            def c_y_(t):
                wait(dve, c_sp, t, 1)
                wait(dve, normed.again(C_), t, 1, back=2)
                dve.scalar_tensor_tensor(out=y[t.p][:], in0=X[:, t.b, 0:D],
                                         scalar=keep1[:, bass.ds(t.b, 1)],
                                         in1=bank[t.p][:, 0:D], op0=ALU.mult, op1=ALU.add).then_inc(c_y.sem, 1)

            pipelined(dve, [(ln_final(C_), 2), (ln_aggr(C_), 1), (c_y_, 0), (ln_bn(C_), 0)])

            dve.tensor_scalar(d_bq, cols[:, 0:KC], SCALE, None, ALU.mult).then_inc(d_prep, 1)
            for i in range(2):
                dve.memset(d_v[i][:, :, HD:HV], 1.0).then_inc(d_prep, 1)
            rounds = []
            for n, round in enumerate((D_, E_)):
                def d_vc_(t, n=n):
                    wait(dve, d_vp.again(n), t, 1)
                    wait(dve, d_pv.again(n), t, NQ, back=2)
                    o = d_v[t.p][:, :, 0:HD]
                    v = bank[2][:, 0:D].rearrange("p (h d) -> p h d", h=H)
                    if n == 0:
                        dve.tensor_tensor(o, v, row("bv").rearrange("p (h d) -> p h d", h=H), ALU.add)\
                           .then_inc(d_vc.sem, 1)
                    else:
                        dve.tensor_copy(o, v).then_inc(d_vc.sem, 1)

                def d_lo_(t, n=n):
                    wait(dve, d_hi.again(n), t, 1)
                    wait(dve, d_kx.again(n), t, 2 * KC, back=2)
                    dve.tensor_tensor(d_kl[t.p], d_kT[t.p], d_kh[t.p][:], ALU.subtract).then_inc(d_lo.sem, 1)
                    wait(dve, d_hi.again(n), t, 2)
                    wait(dve, d_sp.again(n), t, NQ, back=2)
                    dve.tensor_tensor(d_ql[t.p][:], d_qT[t.p], d_qh[t.p][:], ALU.subtract).then_inc(d_lo.sem, 1)

                def d_max_(r, n=n):
                    dm = d_max.again(n)
                    def stage(t):
                        wait(dve, d_sp.again(n), t, r + 1)
                        s_ = bank[3 + r % 2][:].rearrange("p (a b) -> p a b", a=QH)
                        mx = d_mx[t.p][:, QH * r:QH * (r + 1)]
                        dve.tensor_reduce(mx, s_, AX.X, ALU.max).then_inc(dm.sem, 1)
                        wait(dve, dm, t, 2 * r + 1)
                        wait(dve, d_pTp.again(n), t, NQ, back=2)
                        dve.tensor_tensor(d_S[t.p][:, QH * r:QH * (r + 1), :], s_,
                                          mx.unsqueeze(2).to_broadcast([P, QH, P]), ALU.subtract).then_inc(dm.sem, 1)
                    return stage

                def d_div_(t, n=n):
                    wait(dve, d_pv.again(n), t, NQ)
                    wait(dve, d_atp.again(n), t, 1, back=2)
                    o = bank[7][:, 0:H * HV].rearrange("p (h d) -> p h d", h=H)
                    dve.reciprocal(d_rs[t.p], o[:, :, HD]).then_inc(d_div.sem, 1)
                    wait(dve, d_div.again(n), t, 1)
                    dve.tensor_tensor(d_at[t.p].rearrange("p (h d) -> p h d", h=H), o[:, :, 0:HD],
                                      d_rs[t.p].unsqueeze(2).to_broadcast([P, H, HD]), ALU.mult)\
                       .then_inc(d_div.sem, 1)

                def d_y_(t, n=n, round=round):
                    wait(dve, d_op.again(n), t, 1)
                    wait(dve, d_xbc.again(n), t, 1)
                    wait(dve, normed.again(round), t, 1, back=2)
                    dve.tensor_tensor(y[t.p][:], bank[2][:, D:2 * D], d_xb[t.p], ALU.add).then_inc(d_y.sem, 1)
                    wait(dve, d_y.again(n), t, 1)
                    ln_stats(round)(t)

                rounds.append([(d_y_, 4), (d_max_(0), 2), (d_lo_, 1), (d_max_(1), 2), (d_max_(2), 2), (d_div_, 3),
                               (ln_final(round), 4), (d_max_(3), 2), (d_vc_, 1)])
            chained(dve, rounds)

            def f_lc_(t):
                wait(dve, f_lp, t, 1)
                dve.tensor_copy(f_lg[:, t.b, :], bank[1 + t.p][:, 0:E]).then_inc(f_lc.sem, 1)

            def f_xl_(t):
                wait(dve, f_xhc, t, 1)
                part = lambda v: v[:].rearrange("p k (b t) -> p k b t", b=B)[:, :, t.b, :]
                dve.tensor_tensor(part(f_xl), xT[t.p][:], part(f_xh), ALU.subtract).then_inc(f_xlc.sem, 1)

            pipelined(dve, [(f_lc_, 1), (f_xl_, 0)])
            def f_mul_(m):
                for c_ in range(KC):
                    wait(dve, f_hp, m, 2 * c_ + 2)
                    wait(dve, f_silu, m, c_ + 1)
                    wait(dve, f_alc, m, 2, back=2)
                    dve.tensor_tensor(f_a[m.p][:, c_, :], f_h[c_], bank[2 + c_][:], ALU.mult).then_inc(f_mul.sem, 1)

            def f_acc_(m, g, e):
                for i in range(TG):
                    b = TG * g + i
                    if i % 2 == 0:
                        wait(dve, f_dp, m, i // 2 + 1)
                    wait(dve, f_acc, m, i + 1, back=G)
                    dve.scalar_tensor_tensor(out=X[:, b, 0:D],
                                             in0=bank[4 + 2 * m.p + i // 2][:, (i % 2) * D:(i % 2 + 1) * D],
                                             scalar=f_comb[:, b, bass.ds(e, 1)],
                                             in1=X[:, b, 0:D], op0=ALU.mult, op1=ALU.add).then_inc(f_acc.sem, 1)

            n_route = [0]

            def route(m):
                n_route[0] += 1
                m.then_inc(f_route, 1)
                dve.wait_ge(f_route, n_route[0])

            dve.wait_ge(f_sig, 1)
            grp = lambda v: v.rearrange("p b (g e) -> p (b g) e", e=EPG)
            route(dve.memset(f_comb[:, :, 0:SH], 1.0))
            route(dve.tensor_tensor(f_s, f_sc, row("ebias").unsqueeze(1).to_broadcast([P, B, E]), ALU.add))
            s4 = grp(f_s)
            at = 0
            for d in range(1, EPG):
                m = dve.tensor_tensor(f_pair[:, :, at:at + EPG - d], s4[:, :, 0:EPG - d], s4[:, :, d:EPG], ALU.add)
                at += EPG - d
            route(m)
            gs = f_gs.rearrange("p b g -> p (b g)")
            route(dve.tensor_reduce(gs, f_pair, AX.X, ALU.max))
            def group_pair(first):
                return (f_gs.unsqueeze(2).to_broadcast([P, B, GROUPS, GROUPS]) if first else
                        f_gs.unsqueeze(3).to_broadcast([P, B, GROUPS, GROUPS]))
            c4 = lambda v: v.rearrange("p (b g) e -> p b g e", g=GROUPS)
            dve.tensor_tensor(c4(f_c1), group_pair(True), group_pair(False), ALU.is_gt)
            route(dve.tensor_tensor(c4(f_c2), group_pair(True), group_pair(False), ALU.is_equal))
            for g in range(GROUPS):
                m = dve.memset(c4(f_c2)[:, :, g, g:GROUPS], 0.0)
            route(m)
            route(dve.tensor_tensor(f_c1, f_c1, f_c2, ALU.add))
            gm = f_gm.rearrange("p b g -> p (b g)")
            route(dve.tensor_reduce(gm, f_c1, AX.X, ALU.add))
            route(dve.tensor_scalar(gm, gm, TOPG - 0.5, None, ALU.is_lt))
            route(dve.tensor_tensor(grp(f_v), grp(f_s), gm.unsqueeze(2).to_broadcast([P, B * GROUPS, EPG]), ALU.mult))
            route(dve.tensor_scalar(gm, gm, 1.0, None, ALU.subtract))
            route(dve.tensor_tensor(grp(f_v), grp(f_v), gm.unsqueeze(2).to_broadcast([P, B * GROUPS, EPG]), ALU.add))
            route(dve.memset(f_sel, 0.0))
            f_mul_(turn(0))
            key = c("key").unsqueeze(1).to_broadcast([P, B, E])
            for n in range(TOPK):
                route(dve.tensor_reduce(f_m, f_v, AX.X, ALU.max))
                route(dve.tensor_tensor(f_eq, f_v, f_m.unsqueeze(2).to_broadcast([P, B, E]), ALU.is_equal))
                route(dve.tensor_tensor(f_eq, f_eq, key, ALU.mult))
                route(dve.tensor_reduce(f_m, f_eq, AX.X, ALU.max))
                route(dve.tensor_tensor(f_eq, key, f_m.unsqueeze(2).to_broadcast([P, B, E]), ALU.is_equal))
                route(dve.tensor_tensor(f_sel, f_sel, f_eq, ALU.add))
                flat = lambda v: v.rearrange("p b e -> p (b e)")
                route(dve.scalar_tensor_tensor(out=flat(f_v), in0=flat(f_eq), scalar=-BIG, in1=flat(f_v),
                                               op0=ALU.mult, op1=ALU.add))
                if n % 2 == 1:
                    m = (n + 1) // 2
                    f_mul_(turn(m))
                    f_acc_(turn(m - 1), m - 1, 0)
            route(dve.tensor_tensor(f_sel, f_sel, f_sc, ALU.mult))
            route(dve.tensor_reduce(f_m, f_sel, AX.X, ALU.add))
            route(dve.tensor_scalar(f_m, f_m, 1e-20, None, ALU.add))
            route(dve.reciprocal(f_m, f_m))
            route(dve.tensor_scalar(f_m, f_m, MOE_SCALE, None, ALU.mult))
            route(dve.tensor_tensor(f_comb[:, :, SH:NE], f_sel, f_m.unsqueeze(2).to_broadcast([P, B, E]), ALU.mult))

            for m in range(1 + TOPK // 2, 2 * G):
                f_mul_(turn(m))
                f_acc_(turn(m - 1), (m - 1) % G, (m - 1) // G)
            with dve.Fori(2, NE - 1) as e:
                for g in range(G):
                    f_mul_(Turn(G * e + g, g % 2, 0))
                    f_acc_(Turn(G * e + g - 1, (g - 1) % 2, 0), (g - 1) % G, e if g else e - 1)

            def f_stats_(t):
                st = stats.again(F_)
                wait(dve, rstd.again(F_), t, 1, back=2)
                wait(dve, f_acc, turn(MT - G + t.b // TG), t.b % TG + 1)
                dve.bn_stats(bn[t.p][:], X[:, t.b, 0:D]).then_inc(st.sem, 1)
                wait(dve, st, t, 1)
                dve.bn_aggr(mv[t.p][:], bn[t.p][:]).then_inc(st.sem, 1)

            def f_final_(t):
                wait(dve, rstd.again(F_), t, 2)
                if t.b >= 2:
                    dve.wait_ge(s_out[t.p], 16 * t.half)
                dve.tensor_scalar(f_out[t.p], X[:, t.b, 0:D], mv[t.p][:, 0:1], lr[t.p][:, 1:2], ALU.subtract,
                                  ALU.mult).then_inc(normed.sem, 1)

            def f_norm(g):
                for b in range(TG * g, TG * (g + 1)):
                    f_stats_(turn(b))
                    if b > TG * g:
                        f_final_(turn(b - 1))
                f_final_(turn(TG * (g + 1) - 1))

            for g in range(G):
                f_mul_(turn(MT - G + g))
                f_acc_(turn(MT - G + g - 1), (g - 1) % G, NE - 1 if g else NE - 2)
                if g:
                    f_norm(g - 1)
            f_acc_(turn(MT - 1), G - 1, NE - 1)
            f_norm(G - 1)


def packed(m):
    return m.reshape(-1, P, m.shape[1]).transpose(1, 0, 2)


def kernel(x, ctx_1024, L0_attn_Wqkv, L0_attn_bqkv, L0_attn_gq, L0_attn_gk, L0_attn_Wout, L0_attn_bout, L0_attn_gout,
           L0_xattn_Wq, L0_xattn_Wk, L0_xattn_Wv, L0_xattn_Wproj, L0_ffn_attention_mask, L0_ffn_position_ids,
           L0_ffn_router_w, L0_ffn_router_b, L0_ffn_wq, L0_ffn_wk, L0_ffn_wv, L0_ffn_wo, L0_ffn_w1, L0_ffn_w2,
           L0_ffn_ln1, L0_ffn_ln2, L1_attn_w_qkv, L1_attn_b_qkv, L1_attn_w_proj, L1_attn_b_proj, L1_xattn_Wq,
           L1_xattn_Wk, L1_xattn_Wv, L1_xattn_Wo, L1_xattn_bo, L1_ffn_router_w, L1_ffn_bias, L1_ffn_gate_w,
           L1_ffn_up_w, L1_ffn_down_w, L1_ffn_sh_gate_w, L1_ffn_sh_up_w, L1_ffn_sh_down_w):
    import concourse.bacc as bacc
    from concourse.bass_utils import run_bass_kernel_spmd

    n = np.asarray
    turned = lambda v: n(v).reshape(B, P, KC, P).transpose(0, 3, 2, 1)
    bqkv = n(L1_attn_b_qkv)
    shared = [n(L1_ffn_sh_gate_w), n(L1_ffn_sh_up_w), n(L1_ffn_sh_down_w)]
    experts = []
    for e in range(NE):
        if e < SH:
            part = slice(e * EF, (e + 1) * EF)
            w = [shared[0][:, part], shared[1][:, part], shared[2][part]]
        else:
            w = [n(v)[e - SH] for v in (L1_ffn_gate_w, L1_ffn_up_w, L1_ffn_down_w)]
        experts.append(np.concatenate([packed(v) for v in w], axis=1))
    arrays = {
        "x": n(x),
        "xT": turned(x),
        "ctxT": turned(ctx_1024),
        "const": constants(),
        "rows": np.concatenate([n(v).reshape(-1) for v in (
            L0_attn_bqkv, L0_attn_gq, L0_attn_gk, L0_attn_bout, L0_attn_gout, L0_ffn_ln1, L0_ffn_ln2,
            bqkv[2 * D:], L1_attn_b_proj, L1_xattn_bo, L0_ffn_router_b, L1_ffn_bias)]),
        "cols": np.concatenate([bqkv[:2 * D].reshape(2 * KC, P).T, n(L0_ffn_router_w).reshape(KC, P).T], axis=1),
        "a_w": packed(n(L0_attn_Wqkv).T),
        "a_wout": packed(n(L0_attn_Wout).T),
        "b_wq": packed(n(L0_xattn_Wq)),
        "b_wk": packed(n(L0_xattn_Wk)),
        "b_wv": packed(n(L0_xattn_Wv)),
        "b_wp": packed(n(L0_xattn_Wproj).T),
        "c_wqkv": np.concatenate([packed(n(v)) for v in (L0_ffn_wq, L0_ffn_wk, L0_ffn_wv)], axis=2),
        "c_wo": packed(n(L0_ffn_wo)),
        "c_w1": packed(n(L0_ffn_w1)),
        "c_w2": packed(n(L0_ffn_w2)),
        "mask": n(L0_ffn_attention_mask)[:, 0, :P, :P].transpose(1, 0, 2),
        "pos": n(L0_ffn_position_ids)[:, :P].T,
        "d_w": np.concatenate([packed(n(L1_attn_w_qkv)), packed(n(L1_attn_w_proj))], axis=2),
        "e_w": np.concatenate([packed(n(v).T) for v in (L1_xattn_Wq, L1_xattn_Wk, L1_xattn_Wv, L1_xattn_Wo)], axis=2),
        "f_rw": packed(n(L1_ffn_router_w).T),
        "f_w": np.stack(experts),
    }
    nc = bacc.Bacc("TRN2", target_bir_lowering=False, num_devices=1)
    given, handles = {}, {}
    for name, v in arrays.items():
        v = np.ascontiguousarray(v)
        given[f"in_{name}"] = v
        handles[name] = nc.dram_tensor(f"in_{name}", v.shape, mybir.dt.from_np(v.dtype), kind="ExternalInput").ap()
    handles["out"] = nc.dram_tensor("out_x", (B, P, D), F32, kind="ExternalOutput").ap()
    build(nc, handles)
    done = run_bass_kernel_spmd(nc, [given], core_ids=[0])
    return done.results[0]["out_x"]
```
